# Optimizing a Trainium2 kernel written in Bass

```python
import numpy as np
import jax
import jax.numpy as jnp

def _softmax(x, axis=-1):
    return jax.nn.softmax(x, axis=axis)

def _gelu(x):
    return jax.nn.gelu(x, approximate=True)

def _silu(x):
    return jax.nn.silu(x)

def _sigmoid(x):
    return jax.nn.sigmoid(x)

def _layernorm(x, axis=-1, eps=1e-05):
    m = jnp.mean(x, axis=axis, keepdims=True)
    v = jnp.var(x, axis=axis, keepdims=True)
    return (x - m) / jnp.sqrt(v + eps)

def _scatter_add(tgt, idx, src, axis=0):
    return tgt.at[idx].add(src)

def _segment_sum(src, seg, n):
    return jax.ops.segment_sum(src, seg, n)
kernel_name = 'mk_prb_d2_jaxref_r8_a70e6d'

def setup_inputs(seed: int=0):
    np.random.seed(seed)
    _w = jnp.asarray

    def _L0_attn_setup():
        import jax, jax.numpy as jnp
        import numpy as np
        D_MODEL = 128
        N_HEADS = 4
        N_KV_HEADS = 2
        HEAD_DIM = D_MODEL // N_HEADS
        N_REP = N_HEADS // N_KV_HEADS
        EPS_RMS = 1e-06
        EPS_NORM = 1e-12

        def _rmsnorm(x, w):
            var = jnp.mean(jnp.square(x), axis=-1, keepdims=True)
            return x * jax.lax.rsqrt(var + EPS_RMS) * w

        def _l2norm(x):
            n = jnp.sqrt(jnp.sum(jnp.square(x), axis=-1, keepdims=True))
            return x / jnp.maximum(n, EPS_NORM)
        key = jax.random.key(seed)
        ks = jax.random.split(key, 8)
        B, L = (2, 512)
        s = 0.02
        return {'x': jax.random.normal(ks[0], (B, L, D_MODEL), dtype=jnp.float32), 'norm_w': jnp.ones((D_MODEL,), dtype=jnp.float32), 'Wq': jax.random.normal(ks[1], (D_MODEL, N_HEADS * HEAD_DIM), dtype=jnp.float32) * s, 'Wk': jax.random.normal(ks[2], (D_MODEL, N_KV_HEADS * HEAD_DIM), dtype=jnp.float32) * s, 'Wv': jax.random.normal(ks[3], (D_MODEL, N_KV_HEADS * HEAD_DIM), dtype=jnp.float32) * s, 'Wo': jax.random.normal(ks[4], (N_HEADS * HEAD_DIM, D_MODEL), dtype=jnp.float32) * s, 'gate': jnp.asarray(0.1, dtype=jnp.float32), 'log_temperature': jnp.asarray(np.log(10.0), dtype=jnp.float32)}
    _L0_attn_in = _L0_attn_setup()

    def _L0_ffn_setup():
        import jax, jax.numpy as jnp
        import numpy as np
        B, S, D, E, H = (2, 128, 128, 16, 256)
        TOP_K = 2
        TEMP = 1.0
        key = jax.random.key(seed)
        ks = jax.random.split(key, 4)
        sc_d = 1.0 / np.sqrt(D)
        sc_h = 1.0 / np.sqrt(H)
        return {'x': jax.random.normal(ks[0], (B, S, D), dtype=jnp.float32), 'Wr': jax.random.normal(ks[1], (D, E), dtype=jnp.float32) * sc_d, 'br': jnp.zeros((E,), dtype=jnp.float32), 'W1': jax.random.normal(ks[2], (E, D, H), dtype=jnp.float32) * sc_d, 'b1': jnp.zeros((E, H), dtype=jnp.float32), 'W2': jax.random.normal(ks[3], (E, H, D), dtype=jnp.float32) * sc_h, 'b2': jnp.zeros((E, D), dtype=jnp.float32)}
    _L0_ffn_in = _L0_ffn_setup()

    def _L1_attn_setup():
        import jax, jax.numpy as jnp
        import numpy as np
        D_MODEL = 128
        N_HEADS = 16
        KV_HEADS = 4
        D_HEAD = D_MODEL // N_HEADS

        def _rope_factor(n, d_head, dtype):
            i = jnp.arange(d_head)
            theta = jnp.power(jnp.asarray(10000.0, dtype), (-2.0 * (i // 2) / d_head).astype(dtype))
            pos = jnp.arange(n, dtype=dtype)
            ang = pos[:, None] * theta[None, :]
            sign = jnp.where(jnp.arange(n) % 2 == 1, -1.0, 1.0).astype(dtype)
            return jnp.cos(ang) + sign[:, None] * jnp.sin(ang)

        def _rms_norm(x, g):
            eps = jnp.finfo(x.dtype).eps
            inv = jax.lax.rsqrt(jnp.mean(x * x, axis=-1, keepdims=True) + eps)
            return x * inv * g
        key = jax.random.key(seed)
        ks = jax.random.split(key, 5)
        s_in = 1.0 / np.sqrt(D_MODEL)
        x = jax.random.normal(ks[0], (2, 256, D_MODEL), dtype=jnp.float32)
        w_q = jax.random.normal(ks[1], (D_MODEL, D_MODEL), dtype=jnp.float32) * s_in
        w_k = jax.random.normal(ks[2], (D_MODEL, D_HEAD * KV_HEADS), dtype=jnp.float32) * s_in
        w_v = jax.random.normal(ks[3], (D_MODEL, D_HEAD * KV_HEADS), dtype=jnp.float32) * s_in
        w_o = jax.random.normal(ks[4], (D_MODEL, D_MODEL), dtype=jnp.float32) * s_in
        g = jnp.ones((D_MODEL,), dtype=jnp.float32)
        return {'x': x, 'w_q': w_q, 'w_k': w_k, 'w_v': w_v, 'w_o': w_o, 'g': g}
    _L1_attn_in = _L1_attn_setup()

    def _L1_ffn_setup():
        import jax, jax.numpy as jnp
        import numpy as np
        S, B, H, I, E = (64, 2, 128, 352, 8)
        key = jax.random.key(seed)
        ks = jax.random.split(key, 5)
        return {'hidden_states': jax.random.normal(ks[0], (S, B, H), dtype=jnp.float32), 'router_w': jax.random.normal(ks[1], (E, H), dtype=jnp.float32) * 0.02, 'gate_w': jax.random.normal(ks[2], (E, I, H), dtype=jnp.float32) * 0.02, 'up_w': jax.random.normal(ks[3], (E, I, H), dtype=jnp.float32) * 0.02, 'down_w': jax.random.normal(ks[4], (E, H, I), dtype=jnp.float32) * 0.02}
    _L1_ffn_in = _L1_ffn_setup()
    _d = {'L0_attn_x': _L0_attn_in['x'], 'L0_attn_norm_w': _L0_attn_in['norm_w'], 'L0_attn_Wq': _L0_attn_in['Wq'], 'L0_attn_Wk': _L0_attn_in['Wk'], 'L0_attn_Wv': _L0_attn_in['Wv'], 'L0_attn_Wo': _L0_attn_in['Wo'], 'L0_attn_gate': _L0_attn_in['gate'], 'L0_attn_log_temperature': _L0_attn_in['log_temperature'], 'L0_ffn_Wr': _L0_ffn_in['Wr'], 'L0_ffn_br': _L0_ffn_in['br'], 'L0_ffn_W1': _L0_ffn_in['W1'], 'L0_ffn_b1': _L0_ffn_in['b1'], 'L0_ffn_W2': _L0_ffn_in['W2'], 'L0_ffn_b2': _L0_ffn_in['b2'], 'L1_attn_w_q': _L1_attn_in['w_q'], 'L1_attn_w_k': _L1_attn_in['w_k'], 'L1_attn_w_v': _L1_attn_in['w_v'], 'L1_attn_w_o': _L1_attn_in['w_o'], 'L1_attn_g': _L1_attn_in['g'], 'L1_ffn_router_w': _L1_ffn_in['router_w'], 'L1_ffn_gate_w': _L1_ffn_in['gate_w'], 'L1_ffn_up_w': _L1_ffn_in['up_w'], 'L1_ffn_down_w': _L1_ffn_in['down_w']}
    _x0 = _d['L0_attn_x']
    _d['L0_attn_x'] = jax.random.normal(jax.random.fold_in(jax.random.key(seed), 1), (16, 512, 128), dtype=_x0.dtype)
    del _x0
    return _d

def reference(L0_attn_x, L0_attn_norm_w, L0_attn_Wq, L0_attn_Wk, L0_attn_Wv, L0_attn_Wo, L0_attn_gate, L0_attn_log_temperature, L0_ffn_Wr, L0_ffn_br, L0_ffn_W1, L0_ffn_b1, L0_ffn_W2, L0_ffn_b2, L1_attn_w_q, L1_attn_w_k, L1_attn_w_v, L1_attn_w_o, L1_attn_g, L1_ffn_router_w, L1_ffn_gate_w, L1_ffn_up_w, L1_ffn_down_w):

    def _L0_attn_ref(x, norm_w, Wq, Wk, Wv, Wo, gate, log_temperature):
        import jax, jax.numpy as jnp
        import numpy as np
        D_MODEL = 128
        N_HEADS = 4
        N_KV_HEADS = 2
        HEAD_DIM = D_MODEL // N_HEADS
        N_REP = N_HEADS // N_KV_HEADS
        EPS_RMS = 1e-06
        EPS_NORM = 1e-12

        def _rmsnorm(x, w):
            var = jnp.mean(jnp.square(x), axis=-1, keepdims=True)
            return x * jax.lax.rsqrt(var + EPS_RMS) * w

        def _l2norm(x):
            n = jnp.sqrt(jnp.sum(jnp.square(x), axis=-1, keepdims=True))
            return x / jnp.maximum(n, EPS_NORM)
        B, L, D = x.shape
        h = _rmsnorm(x, norm_w)
        q = (h @ Wq).reshape(B, L, N_HEADS, HEAD_DIM).transpose(0, 2, 1, 3)
        k = (h @ Wk).reshape(B, L, N_KV_HEADS, HEAD_DIM).transpose(0, 2, 1, 3)
        v = (h @ Wv).reshape(B, L, N_KV_HEADS, HEAD_DIM).transpose(0, 2, 1, 3)
        if N_REP > 1:
            k = jnp.repeat(k, N_REP, axis=1)
            v = jnp.repeat(v, N_REP, axis=1)
        q = _l2norm(q)
        k = _l2norm(k)
        scale = jnp.exp(log_temperature)
        attn = jnp.einsum('bhqd,bhkd->bhqk', q, k) * scale
        causal = jnp.tril(jnp.ones((L, L), dtype=bool))
        attn = jnp.where(causal, attn, -jnp.inf)
        attn = jax.nn.softmax(attn, axis=-1)
        out = jnp.einsum('bhqk,bhkd->bhqd', attn, v).transpose(0, 2, 1, 3).reshape(B, L, D)
        out = out @ Wo
        return x + gate * out

    def _L0_ffn_ref(x, Wr, br, W1, b1, W2, b2):
        import jax, jax.numpy as jnp
        import numpy as np
        B, S, D, E, H = (2, 128, 128, 16, 256)
        TOP_K = 2
        TEMP = 1.0
        token_shape = x.shape[:-1]
        d = x.shape[-1]
        xt = x.reshape(-1, d)
        T = xt.shape[0]
        logits = (xt @ Wr + br) / TEMP
        probs = jax.nn.softmax(logits, axis=-1)
        w, idx = jax.lax.top_k(probs, TOP_K)
        w = w / jnp.clip(jnp.sum(w, axis=-1, keepdims=True), 1e-09)
        comb = jnp.zeros((T, E), dtype=xt.dtype)
        comb = comb.at[jnp.arange(T)[:, None], idx].add(w)
        h = jax.nn.gelu(jnp.einsum('td,edh->teh', xt, W1) + b1, approximate=False)
        o = jnp.einsum('teh,eho->teo', h, W2) + b2
        y = jnp.einsum('teo,te->to', o, comb)
        y = xt + y
        return y.reshape(*token_shape, d)

    def _L1_attn_ref(x, w_q, w_k, w_v, w_o, g):
        import jax, jax.numpy as jnp
        import numpy as np
        D_MODEL = 128
        N_HEADS = 16
        KV_HEADS = 4
        D_HEAD = D_MODEL // N_HEADS

        def _rope_factor(n, d_head, dtype):
            i = jnp.arange(d_head)
            theta = jnp.power(jnp.asarray(10000.0, dtype), (-2.0 * (i // 2) / d_head).astype(dtype))
            pos = jnp.arange(n, dtype=dtype)
            ang = pos[:, None] * theta[None, :]
            sign = jnp.where(jnp.arange(n) % 2 == 1, -1.0, 1.0).astype(dtype)
            return jnp.cos(ang) + sign[:, None] * jnp.sin(ang)

        def _rms_norm(x, g):
            eps = jnp.finfo(x.dtype).eps
            inv = jax.lax.rsqrt(jnp.mean(x * x, axis=-1, keepdims=True) + eps)
            return x * inv * g
        b, n, _ = x.shape
        reps = N_HEADS // KV_HEADS
        x_norm = _rms_norm(x, g)
        q = (x_norm @ w_q).reshape(b, n, N_HEADS, D_HEAD).transpose(0, 2, 1, 3)
        k = (x_norm @ w_k).reshape(b, n, KV_HEADS, D_HEAD).transpose(0, 2, 1, 3)
        v = (x_norm @ w_v).reshape(b, n, KV_HEADS, D_HEAD).transpose(0, 2, 1, 3)
        rf = _rope_factor(n, D_HEAD, x.dtype)
        q = q * rf
        k = k * rf
        q5 = q.reshape(b, reps, KV_HEADS, n, D_HEAD)
        scale = jnp.asarray(np.sqrt(D_MODEL), x.dtype)
        qkt = jnp.einsum('brkqa,bkca->brkqc', q5, k) / scale
        attn = jax.nn.softmax(qkt, axis=-1)
        s = jnp.einsum('brkqc,bkca->brkqa', attn, v)
        s = s.reshape(b, N_HEADS, n, D_HEAD).transpose(0, 2, 1, 3).reshape(b, n, D_MODEL)
        o = s @ w_o
        return s + o

    def _L1_ffn_ref(hidden_states, router_w, gate_w, up_w, down_w):
        import jax, jax.numpy as jnp
        import numpy as np
        S, B, H, I, E = (64, 2, 128, 352, 8)
        router_logits = jnp.einsum('sbh,eh->sbe', hidden_states, router_w)
        routing_indices = jnp.argmax(router_logits, axis=-1)
        out = jnp.zeros_like(hidden_states)
        for e in range(E):
            mask = (routing_indices == e)[..., None]
            xe = jnp.where(mask, hidden_states, 0.0)
            g = jnp.einsum('sbh,ih->sbi', xe, gate_w[e])
            u = jnp.einsum('sbh,ih->sbi', xe, up_w[e])
            ye = jnp.einsum('sbi,hi->sbh', jax.nn.silu(g) * u, down_w[e])
            out = out + jnp.where(mask, ye, 0.0)
        return out
    x = L0_attn_x
    xn = _layernorm(x, axis=-1)
    x = x + _L0_attn_ref(xn, L0_attn_norm_w, L0_attn_Wq, L0_attn_Wk, L0_attn_Wv, L0_attn_Wo, L0_attn_gate, L0_attn_log_temperature) + _L0_ffn_ref(xn, L0_ffn_Wr, L0_ffn_br, L0_ffn_W1, L0_ffn_b1, L0_ffn_W2, L0_ffn_b2)
    xn = _layernorm(x, axis=-1)
    x = x + _L1_attn_ref(xn, L1_attn_w_q, L1_attn_w_k, L1_attn_w_v, L1_attn_w_o, L1_attn_g) + _L1_ffn_ref(xn, L1_ffn_router_w, L1_ffn_gate_w, L1_ffn_up_w, L1_ffn_down_w)
    return x

_drawn_inputs = setup_inputs


def setup_inputs(seed=0):
    import zlib

    import numpy as np

    out = dict(_drawn_inputs(seed))
    spreads = {'L0_attn_norm_w': (1.0, 0.6),
     'L0_ffn_br': (0.0, 0.1),
     'L0_ffn_b1': (0.0, 0.485),
     'L0_ffn_b2': (0.0, 0.324),
     'L1_attn_g': (1.0, 0.6)}
    factors = {'L0_attn_Wq': 8.0,
     'L0_attn_Wk': 8.0,
     'L0_attn_Wv': 8.0,
     'L0_attn_Wo': 8.0,
     'L1_attn_w_q': 6.998,
     'L1_attn_w_k': 7.214,
     'L1_attn_w_o': 3.054,
     'L1_ffn_router_w': 8.0,
     'L1_ffn_gate_w': 8.0,
     'L1_ffn_up_w': 8.0,
     'L1_ffn_down_w': 8.0}
    for name, (base, spread) in spreads.items():
        noise = np.random.default_rng([zlib.crc32(name.encode()), seed]).standard_normal(out[name].shape)
        drawn = base * np.exp(spread * noise) if base else spread * noise
        out[name] = jnp.asarray(drawn.astype(out[name].dtype))
    for name, factor in factors.items():
        out[name] = (out[name] * factor).astype(out[name].dtype)
    return out
```

```python
from contextlib import ExitStack

import numpy as np

import concourse.bass as bass
from concourse import mybir

F32 = mybir.dt.float32
BF16 = mybir.dt.bfloat16
U32 = mybir.dt.uint32
ALU = mybir.AluOpType
ACT = mybir.ActivationFunctionType
AX = mybir.AxisListType.X

P = 128
D = 128
NB, L = 16, 512
T = NB * L
NT = L // P
EPS_LN = 1e-5

H0, KV0, DH0 = 4, 2, 32
E0, F0 = 16, 256
QKV0 = D + 2 * KV0 * DH0
PRJ0 = QKV0 + E0
H1, KV1, DH1 = 16, 4, 8
REP1 = H1 // KV1
E1, F1 = 8, 352
FC1 = 3
QKV1 = D + 2 * KV1 * DH1
PRJ1 = QKV1 + E1

GRP = 2 * P
REG = T + GRP
NG0 = 2 * T // GRP + E0
NG1 = T // GRP + E1


class Chain:

    def __init__(self, eng, sem, per, passed_count=None):
        self.eng, self.sem, self.per, self.passed = eng, sem, per, passed_count

    def at(self, b):
        self.base, self.n = b * self.per, 0

    def link(self, ins):
        self.n += 1
        ins.then_inc(self.sem, 1)
        self.eng.wait_ge(self.sem, self.base + self.n)

    def link_apart(self, ins):
        self.n += 1
        ins.then_inc(self.sem, 1)
        self.eng.wait_ge(self.sem, self.base + self.n)
        passed(self.eng, self.passed)

    def end(self):
        assert self.n == self.per, (self.sem, self.n, self.per)


def passed(eng, count):
    eng.sem_inc(count, 1)


def allocators(nc, ctx):
    taken = []

    def clear():
        with nc.Block() as block:

            @block.gpsimd
            def _(pool):
                for num in sorted(taken):
                    if num - 1 not in taken:
                        end = next(n for n in range(num, 999) if n not in taken)
                        pool.sem_clear(range(num, end))

    ctx.callback(lambda: clear() if taken else None)

    def sb(name, shape, dt=F32):
        return ctx.enter_context(nc.sbuf_tensor(name, shape, dt))

    def ps(name, shape, dt=F32):
        return ctx.enter_context(nc.psum_tensor(name, shape, dt))

    def sem(name):
        s = ctx.enter_context(nc.semaphore(name))
        taken.append(s.num)
        return s

    return sb, ps, sem


def setup(nc, k, i):
    with ExitStack() as ctx:
        sb, ps, sem = allocators(nc, ctx)
        loaded = sem("su_loaded")
        pool_made = sem("su_pool")
        dve_made = sem("su_dve")
        act_made = sem("su_act")
        w0 = sb("su_w0", [P, PRJ0])
        w1 = sb("su_w1", [P, PRJ1])
        g0 = sb("su_g0", [P, 2])
        with nc.Block() as block:

            @block.sync
            def _(sp):
                sp.dma_start(w0[:], i["w0cat"]).then_inc(loaded, 16)
                sp.dma_start(w1[:], i["w1cat"]).then_inc(loaded, 16)
                sp.dma_start(k.wo0[:], i["L0_attn_Wo"]).then_inc(loaded, 16)
                sp.dma_start(k.wo1[:], i["L1_attn_w_o"]).then_inc(loaded, 16)
                sp.dma_start(g0[:], i["norms"]).then_inc(loaded, 16)
                sp.dma_start(k.gate[:], i["gate"]).then_inc(loaded, 16)
                sp.dma_start(k.temp[:], i["logt"]).then_inc(loaded, 16)
                sp.dma_start(k.br0[:], i["br0"]).then_inc(loaded, 16)
                sp.wait_ge(loaded, 8 * 16)

            @block.gpsimd
            def _(pool):
                nc.gpsimd.memset(k.ident[:], 0.0).then_inc(pool_made, 1)
                nc.gpsimd.memset(k.tri[:], 1.0).then_inc(pool_made, 1)
                nc.gpsimd.memset(k.mhalf[:], -0.5)
                nc.gpsimd.iota(k.iota_i[:], pattern=[[1, 128]], base=0, channel_multiplier=0).then_inc(pool_made, 1)
                pool.wait_ge(pool_made, 3)
                nc.gpsimd.affine_select(out=k.ident[:], in_=k.ident[:], compare_op=ALU.not_equal, fill=1.0,
                                        base=0, pattern=[[-1, P]], channel_multiplier=1).then_inc(pool_made, 1)
                nc.gpsimd.affine_select(out=k.tri[:], in_=k.tri[:], compare_op=ALU.is_gt, fill=0.0,
                                        base=0, pattern=[[1, P]], channel_multiplier=-1).then_inc(pool_made, 1)
                nc.gpsimd.memset(k.ones_b[:], 1.0)
                nc.gpsimd.memset(k.ones_f[:], 1.0)
                nc.gpsimd.memset(k.zeros[:], 0.0).then_inc(pool_made, 1)

            @block.scalar
            def _(act):
                act.wait_ge(loaded, 8 * 16)
                nc.scalar.activation(k.temp[:, 1:2], k.temp[:, 0:1], ACT.Exp).then_inc(act_made, 1)

            @block.vector
            def _(dve):
                dve.wait_ge(loaded, 8 * 16)
                nc.vector.tensor_scalar(k.w0[:, 0:QKV0], w0[:, 0:QKV0], g0[:, 0:1], None, ALU.mult)
                nc.vector.tensor_scalar(k.w1[:, 0:QKV1], w1[:, 0:QKV1], g0[:, 1:2], None, ALU.mult)
                nc.vector.tensor_copy(k.w0[:, QKV0:PRJ0], w0[:, QKV0:PRJ0])
                nc.vector.tensor_copy(k.w1[:, QKV1:PRJ1], w1[:, QKV1:PRJ1])
                dve.wait_ge(pool_made, 3)
                nc.vector.tensor_copy(k.iota[:], k.iota_i[:]).then_inc(dve_made, 1)
                dve.wait_ge(dve_made, 1)
                nc.vector.tensor_scalar(k.run0[:], k.iota[:, 0:E0], float(REG), None, ALU.mult)
                nc.vector.tensor_scalar(k.run1[:], k.iota[:, 0:E1], float(REG), None, ALU.mult)
                dve.wait_ge(act_made, 1)
                nc.vector.tensor_scalar(k.temp[:, 2:3], k.temp[:, 1:2], -1.0, 80.0, ALU.mult, ALU.add).then_inc(dve_made, 1)
                dve.wait_ge(dve_made, 2)
                nc.vector.tensor_scalar(k.temp[:, 3:4], k.temp[:, 2:3], 0.0, None, ALU.min)


def layer0_attention(nc, k, x_d, base_d, meta_d, xs_d):
    with ExitStack() as ctx:
        sb, ps, sem = allocators(nc, ctx)
        x = sb("a_x", [P, 2, NT, D])
        xn = sb("a_xn", [P, 2, NT, D])
        xs = sb("a_xs", [P, 2, NT, D])
        stats = sb("a_stats", [P, NT, 6])
        mv = sb("a_mv", [P, NT, 2])
        tmp4 = sb("a_tmp4", [P, 3, NT])
        rstd = sb("a_rstd", [P, NT])
        r2 = sb("a_r2", [P, NT])
        r2sq = sb("a_r2sq", [P, NT])
        xnT = sb("a_xnT", [P, L])
        prj = sb("a_prj", [P, NT, PRJ0])
        sq = sb("a_sq", [P, NT * (H0 + KV0), DH0])
        ss = sb("a_ss", [P, NT, H0 + KV0])
        ftmp = sb("a_ftmp", [P, 3, NT, H0 + KV0])
        fac = sb("a_fac", [P, NT, H0 + KV0])
        qn = sb("a_qn", [P, NT, D])
        kn = sb("a_kn", [P, NT, D])
        v = sb("a_v", [P, 2, NT, KV0 * DH0])
        qT = sb("a_qT", [P, 2, L])
        kz = sb("a_kz", [P, 2, H0, L])
        pt = sb("a_pt", [P, 2, H0, L])
        rs = sb("a_rs", [P, L])
        attnT = sb("a_attnT", [P, L])
        bs = sb("a_bs", [P, 2, NT, D])
        lg = sb("a_lg", [P, NT, E0])
        mx8 = sb("a_mx8", [P, NT, 8])
        ix8 = sb("a_ix8", [P, NT, 8], U32)
        ixf = sb("a_ixf", [P, NT, 2])
        oh = sb("a_oh", [P, 2, NT, E0])
        ohb = sb("a_ohb", [P, NT, E0], BF16)
        pos = sb("a_pos", [P, NT, E0])
        ohp = sb("a_ohp", [P, 2, NT, E0])
        slotf = sb("a_slotf", [P, 2, NT])
        dl = sb("a_dl", [P, NT])
        el = sb("a_el", [P, NT])
        ep = sb("a_ep", [P, NT])
        meta = sb("a_meta", [P, 2, 4 * NT], U32)

        ps_t = ps("a_ps_t", [P, L])
        ps_p = ps("a_ps_p", [P, L])
        ps_s = ps("a_ps_s", [P, 2, 2, L])
        ps_v = ps("a_ps_v", [P, L])
        ps_d = ps("a_ps_d", [P, L])
        RT = 288

        x_in = [sem(f"a_x_in{p}") for p in range(2)]
        x_used, stats_ready, rstd_ready, xn_ready = sem("a_x_used"), sem("a_stats"), sem("a_rstd_r"), sem("a_xn_r")
        xT_ps, xT_sb, proj_ps, prj_sb, sq_ready = sem("a_xT_ps"), sem("a_xT_sb"), sem("a_proj"), sem("a_prj_sb"), sem("a_sq_r")
        ss_ready, fac_ready, qkv_ready = sem("a_ss_r"), sem("a_fac_r"), sem("a_qkv_r")
        qT_ps, qT_sb, kT_ps, kT_sb = sem("a_qT_ps"), sem("a_qT_sb"), sem("a_kT_ps"), sem("a_kT_sb")
        oh_ready, rank_ps, rank_used, dl_ready, el_ready, meta_ready = (
            sem("a_oh_r"), sem("a_rank"), sem("a_rank_u"), sem("a_dl_r"), sem("a_el_r"), sem("a_meta_r"))
        scattered = k.scattered0
        meta_out = [sem(f"a_meta_out{p}") for p in range(2)]
        s_ps, exp_done, masked, pv_tile = sem("a_s_ps"), sem("a_exp"), sem("a_masked"), sem("a_pvt")
        norm_done, wo_ps, wo_used = sem("a_norm"), sem("a_wo_ps"), sem("a_wo_used")
        base_out = [sem(f"a_base_out{p}") for p in range(2)]
        dve_pro, dve_main, pool_pro, act_seed = sem("a_dve_pro"), sem("a_dve_main"), sem("a_pool_pro"), sem("a_seed")

        with nc.Block() as block:

            @block.vector
            def _(dve):
                nc.vector.memset(kz[:], 0.0).then_inc(x_used, 2)
                nc.vector.memset(ss[:], 0.0)
                nc.vector.memset(mv[:], 0.0).then_inc(exp_done, 2)
                nc.vector.memset(stats[:], 0.0).then_inc(pv_tile, 2 * NT)
                nc.vector.memset(rs[:], 0.0).then_inc(wo_used, 2)

        with nc.Block() as block:

            @block.sync
            def _(sp):
                def load(b, i, p):
                    sp.wait_ge(x_used, b + 1)
                    passed(sp, k.passed_sp)
                    sp.dma_start(x[:, p], x_d[bass.ds(b * L, L), :].rearrange("(t p) d -> p t d", p=P)).then_inc(x_in[p], 16)

                def store(b, i, p):
                    sp.wait_ge(meta_ready, b + 1)
                    passed(sp, k.passed_sp)
                    sp.dma_start(meta_d[bass.ds(b * P, P), :], meta[:, p]).then_inc(meta_out[p], 16)
                    sp.wait_ge(wo_used, b + 3)
                    passed(sp, k.passed_sp)
                    sp.dma_start(base_d[bass.ds(b * L, L), :].rearrange("(t p) d -> p t d", p=P), bs[:, p]).then_inc(base_out[p], 16)

                load(0, 0, 0)
                load(1, 0, 1)
                with sp.Fori(0, NB // 2 - 1) as i:
                    for p in range(2):
                        load(2 * i + p + 2, i + 1, p)
                        store(2 * i + p, i, p)
                for p in range(2):
                    store(NB - 2 + p, NB // 2 - 1, p)
                for p in range(2):
                    sp.wait_ge(meta_out[p], 16 * (NB // 2))
                    sp.wait_ge(base_out[p], 16 * (NB // 2))

            @block.vector
            def _(dve):
                pro = Chain(dve, dve_pro, PRO_DVE_A, k.passed_dve)
                main = Chain(dve, dve_main, 1, k.passed_dve)

                def prologue(b, i, p):
                    pro.at(b)
                    dve.wait_ge(x_in[p], 16 * (i + 1))
                    dve.wait_ge(rstd_ready, b)
                    for t in range(NT):
                        last = nc.vector.bn_stats(stats[:, t, :], x[:, p, t, :])
                    pro.link_apart(last)
                    for t in range(NT):
                        last = nc.vector.bn_aggr(mv[:, t, :], stats[:, t, :])
                    last.then_inc(stats_ready, 1)
                    dve.wait_ge(rstd_ready, b + 1)
                    dve.wait_ge(scattered[p], 16 * 2 * NT * i)
                    for t in range(NT):
                        last = nc.vector.tensor_scalar(xn[:, p, t, :], x[:, p, t, :], mv[:, t, 0:1], rstd[:, t:t + 1],
                                                       ALU.subtract, ALU.mult)
                    last.then_inc(xn_ready, 1)
                    dve.wait_ge(xn_ready, b + 1)
                    dve.wait_ge(wo_used, b + 1)
                    nc.vector.scalar_tensor_tensor(xs[:, p], xn[:, p], 2.0, x[:, p], ALU.mult, ALU.add).then_inc(x_used, 1)
                    dve.wait_ge(sq_ready, b + 1)
                    nc.vector.tensor_reduce(ss[:].rearrange("p t h -> p (t h)"), sq[:], AX, ALU.add).then_inc(ss_ready, 1)
                    dve.wait_ge(fac_ready, b + 1)
                    dve.wait_ge(kT_ps, b)
                    dve.wait_ge(pv_tile, NT * (b + 1))
                    nc.vector.tensor_tensor(qn[:].rearrange("p t (h d) -> p t h d", h=H0),
                                            prj[:, :, 0:D].rearrange("p t (h d) -> p t h d", h=H0),
                                            fac[:, :, 0:H0].unsqueeze(3).to_broadcast([P, NT, H0, DH0]), ALU.mult)
                    for r in range(H0 // KV0):
                        nc.vector.tensor_tensor(kn[:].rearrange("p t (g r d) -> p t g r d", g=KV0, d=DH0)[:, :, :, r, :],
                                                prj[:, :, D:D + KV0 * DH0].rearrange("p t (h d) -> p t h d", h=KV0),
                                                fac[:, :, H0:H0 + KV0].unsqueeze(3).to_broadcast([P, NT, KV0, DH0]), ALU.mult)
                    nc.vector.tensor_tensor(v[:, p], prj[:, :, D + KV0 * DH0:QKV0],
                                            r2[:].unsqueeze(2).to_broadcast([P, NT, KV0 * DH0]), ALU.mult).then_inc(qkv_ready, 1)
                    pro.link_apart(nc.vector.tensor_tensor(lg[:], prj[:, :, QKV0:PRJ0],
                                                     k.br0[:].unsqueeze(1).to_broadcast([P, NT, E0]), ALU.add))
                    for t in range(NT):
                        last = nc.vector.max(mx8[:, t, :], lg[:, t, :])
                    pro.link_apart(last)
                    for t in range(NT):
                        last = nc.vector.max_index(ix8[:, t, :], mx8[:, t, :], lg[:, t, :])
                    dve.wait_ge(el_ready, b)
                    nc.vector.tensor_tensor(dl[:], mx8[:, :, 1], mx8[:, :, 0], ALU.subtract).then_inc(dl_ready, 1)
                    dve.wait_ge(dl_ready, b + 1)
                    pro.link(nc.vector.tensor_copy(ixf[:], ix8[:, :, 0:2]))
                    for c in range(2):
                        last = nc.vector.tensor_tensor(oh[:, c], k.iota[:, 0:E0].unsqueeze(1).to_broadcast([P, NT, E0]),
                                                       ixf[:, :, c].unsqueeze(2).to_broadcast([P, NT, E0]), ALU.is_equal)
                    pro.link(last)
                    nc.vector.tensor_tensor(ohb[:], oh[:, 0], oh[:, 1], ALU.add).then_inc(oh_ready, 1)
                    dve.wait_ge(rank_ps, b + 1)
                    for t in range(NT):
                        nc.vector.tensor_tensor(pos[:, t], ps_p[:, RT + t * E0:RT + (t + 1) * E0], k.run0[:], ALU.add)
                        last = nc.vector.tensor_tensor(k.run0[:], ps_p[:, RT + (NT + t) * E0:RT + (NT + t + 1) * E0],
                                                       k.run0[:], ALU.add)
                        if t < NT - 1:
                            pro.link(last)
                    last.then_inc(rank_used, 1)
                    dve.wait_ge(rank_used, b + 1)
                    for c in range(2):
                        last = nc.vector.tensor_tensor(ohp[:, c], oh[:, c], pos[:], ALU.mult)
                    pro.link(last)
                    pro.link(nc.vector.tensor_reduce(slotf[:].rearrange("p c t -> p (c t)"),
                                                     ohp[:].rearrange("p c t e -> p (c t) e"), AX, ALU.add))
                    dve.wait_ge(el_ready, b + 1)
                    dve.wait_ge(meta_out[p], 16 * i)
                    pro.link(nc.vector.tensor_scalar(ep[:], el[:], 1.0, None, ALU.add))
                    wts = meta[:, p].bitcast(F32)
                    pro.link(nc.vector.reciprocal(wts[:, 2 * NT:3 * NT], ep[:]))
                    nc.vector.tensor_tensor(wts[:, 3 * NT:4 * NT], el[:], wts[:, 2 * NT:3 * NT], ALU.mult)
                    nc.vector.tensor_copy(meta[:, p, 0:2 * NT], slotf[:].rearrange("p c t -> p (c t)")).then_inc(meta_ready, 1)
                    dve.wait_ge(kT_ps, b + 1)
                    for h in range(H0):
                        r = slice(h * DH0, (h + 1) * DH0)
                        last = nc.vector.tensor_copy(kz[r, p, h, :], ps_t[r, :])
                    last.then_inc(kT_sb, 1)
                    pro.end()

                def finish(b, i, p):
                    main.at(b)
                    dve.wait_ge(pv_tile, NT * (b + 3))
                    main.link(nc.vector.reciprocal(rs[:], ps_d[:]))
                    dve.wait_ge(wo_ps, b)
                    nc.vector.tensor_tensor(attnT[:], ps_v[:], rs[:], ALU.mult).then_inc(norm_done, 1)
                    dve.wait_ge(wo_ps, b + 1)
                    dve.wait_ge(base_out[p], 16 * i)
                    nc.vector.scalar_tensor_tensor(bs[:, p].rearrange("p t d -> p (t d)"), ps_t[:], k.gate[:, 0:1],
                                                   xs[:, p].rearrange("p t d -> p (t d)"), ALU.mult, ALU.add).then_inc(wo_used, 1)
                    main.end()

                prologue(0, 0, 0)
                with dve.Fori(0, NB // 2 - 1) as i:
                    prologue(2 * i + 1, i, 1)
                    finish(2 * i, i, 0)
                    prologue(2 * i + 2, i + 1, 0)
                    finish(2 * i + 1, i, 1)
                prologue(NB - 1, NB // 2 - 1, 1)
                finish(NB - 2, NB // 2 - 1, 0)
                finish(NB - 1, NB // 2 - 1, 1)

            @block.gpsimd
            def _(pool):
                pro = Chain(pool, pool_pro, PRO_POOL_A, k.passed_pool)

                def norms(b, i, p):
                    pro.at(b)
                    pool.wait_ge(stats_ready, b + 1)
                    pool.wait_ge(xn_ready, b)
                    pool.wait_ge(qkv_ready, b)
                    passed(pool, k.passed_pool)
                    pro.link(nc.gpsimd.tensor_scalar(tmp4[:, 0], mv[:, :, 1], EPS_LN, None, ALU.add))
                    pro.link(nc.gpsimd.tensor_tensor(rstd[:], tmp4[:, 0], k.mhalf[:, 0:NT], ALU.pow))
                    pro.link(nc.gpsimd.tensor_tensor(tmp4[:, 1], rstd[:], rstd[:], ALU.mult))
                    pro.link_apart(nc.gpsimd.tensor_tensor(tmp4[:, 2], tmp4[:, 1], mv[:, :, 1], ALU.mult))
                    pro.link(nc.gpsimd.tensor_scalar(tmp4[:, 0], tmp4[:, 2], 1e-6, None, ALU.add))
                    pro.link(nc.gpsimd.tensor_tensor(r2[:], tmp4[:, 0], k.mhalf[:, 0:NT], ALU.pow))
                    nc.gpsimd.tensor_tensor(r2sq[:], r2[:], r2[:], ALU.mult).then_inc(rstd_ready, 1)

                def factors(b, i, p):
                    pool.wait_ge(ss_ready, b + 1)
                    pool.wait_ge(rstd_ready, b + 1)
                    bc = r2sq[:].unsqueeze(2).to_broadcast([P, NT, H0 + KV0])
                    pro.link_apart(nc.gpsimd.tensor_tensor(ftmp[:, 0], ss[:], bc, ALU.mult))
                    pro.link(nc.gpsimd.tensor_scalar(ftmp[:, 1], ftmp[:, 0], 1e-24, None, ALU.max))
                    pro.link(nc.gpsimd.tensor_tensor(ftmp[:, 2].rearrange("p t h -> p (t h)"),
                                                     ftmp[:, 1].rearrange("p t h -> p (t h)"),
                                                     k.mhalf[:, 0:NT * (H0 + KV0)], ALU.pow))
                    nc.gpsimd.tensor_tensor(fac[:], ftmp[:, 2], r2[:].unsqueeze(2).to_broadcast([P, NT, H0 + KV0]),
                                            ALU.mult).then_inc(fac_ready, 1)
                    pro.end()

                def scatter(b, i, p):
                    pool.wait_ge(meta_ready, b + 1)
                    passed(pool, k.passed_pool)
                    for c in range(2):
                        for t in range(NT):
                            nc.gpsimd.indirect_dma_start(
                                xs_d, bass.IndirectOffsetOnAxis(ap=meta[:, p, c * NT + t:c * NT + t + 1], axis=0),
                                xn[:, p, t, :], None).then_inc(scattered[p], 16)

                def mask(b, u):
                    kt, pr = u // 2, u % 2
                    pool.wait_ge(exp_done, 8 * b + u + 3)
                    passed(pool, k.passed_pool)
                    blk = pt[:, kt % 2, 2 * pr:2 * pr + 2, 0:P]
                    nc.gpsimd.affine_select(out=blk, in_=blk, compare_op=ALU.is_ge, fill=0.0, base=0,
                                            pattern=[[0, 2], [1, P]], channel_multiplier=-1).then_inc(masked, 1)

                def body(b, bn, i_n, p_n):
                    norms(bn, i_n, p_n)
                    for u in range(6):
                        mask(b, u)
                    factors(bn, i_n, p_n)
                    mask(b, 6)
                    mask(b, 7)
                    scatter(bn, i_n, p_n)

                norms(0, 0, 0)
                factors(0, 0, 0)
                scatter(0, 0, 0)
                with pool.Fori(0, NB // 2 - 1) as i:
                    body(2 * i, 2 * i + 1, i, 1)
                    body(2 * i + 1, 2 * i + 2, i + 1, 0)
                body(NB - 2, NB - 1, NB // 2 - 1, 1)
                for u in range(8):
                    mask(NB - 1, u)
                for p in range(2):
                    pool.wait_ge(scattered[p], 16 * 2 * NT * (NB // 2))

            @block.scalar
            def _(act):
                def xT_copy(b):
                    act.wait_ge(xT_ps, b + 1)
                    act.wait_ge(proj_ps, NT * b)
                    nc.scalar.activation(xnT[:], ps_t[:], ACT.Copy).then_inc(xT_sb, 1)

                def prj_copy(b, t):
                    act.wait_ge(proj_ps, NT * b + t + 1)
                    if t == 0:
                        act.wait_ge(qkv_ready, b)
                        act.wait_ge(oh_ready, b)
                    nc.scalar.activation(prj[:, t, :], ps_p[:, 0:PRJ0], ACT.Copy).then_inc(prj_sb, 1)

                def squares(b):
                    act.wait_ge(prj_sb, NT * (b + 1))
                    act.wait_ge(ss_ready, b)
                    nc.scalar.activation(sq[:].rearrange("p (t h) d -> p t (h d)", t=NT), prj[:, :, 0:D + KV0 * DH0],
                                         ACT.Square).then_inc(sq_ready, 1)

                def qT_copy(b, p):
                    act.wait_ge(qT_ps, b + 1)
                    act.wait_ge(pv_tile, NT * (b + 1))
                    nc.scalar.activation(qT[:, p, :], ps_t[:], ACT.Copy).then_inc(qT_sb, 1)

                def odds(b):
                    act.wait_ge(dl_ready, b + 1)
                    act.wait_ge(meta_ready, b)
                    nc.scalar.activation(el[:], dl[:], ACT.Exp).then_inc(el_ready, 1)

                def exps(b, u):
                    kt, pr = u // 2, u % 2
                    n = L - kt * P
                    act.wait_ge(s_ps, 8 * b + u + 1)
                    act.wait_ge(pv_tile, NT * (b + 1) + kt + 3)
                    nc.scalar.activation(pt[:, kt % 2, 2 * pr:2 * pr + 2, 0:n], ps_s[:, u % 2, :, 0:n], ACT.Exp,
                                         bias=k.temp[:, 3:4], scale=k.temp[:, 1:2]).then_inc(exp_done, 1)

                def body(b, bn, pn):
                    exps(b, 0)
                    exps(b, 1)
                    xT_copy(bn)
                    exps(b, 2)
                    prj_copy(bn, 0)
                    exps(b, 3)
                    prj_copy(bn, 1)
                    exps(b, 4)
                    prj_copy(bn, 2)
                    exps(b, 5)
                    prj_copy(bn, 3)
                    squares(bn)
                    exps(b, 6)
                    exps(b, 7)
                    qT_copy(bn, pn)
                    odds(bn)

                xT_copy(0)
                for t in range(NT):
                    prj_copy(0, t)
                squares(0)
                qT_copy(0, 0)
                odds(0)
                with act.Fori(0, NB // 2 - 1) as i:
                    body(2 * i, 2 * i + 1, 1)
                    body(2 * i + 1, 2 * i + 2, 0)
                body(NB - 2, NB - 1, 1)
                for u in range(8):
                    exps(NB - 1, u)

            @block.tensor
            def _(pe):
                def transposes(src, done):
                    for t in range(NT):
                        last = nc.tensor.transpose(ps_t[:, t * P:(t + 1) * P], src[:, t, :], k.ident[:])
                    last.then_inc(done, 1)

                def xT(b, p):
                    pe.wait_ge(xn_ready, b + 1)
                    pe.wait_ge(wo_used, b + 1)
                    transposes(xn[:, p], xT_ps)

                def project(b, t):
                    pe.wait_ge(xT_sb, b + 1)
                    pe.wait_ge(prj_sb, NT * b + t)
                    nc.tensor.matmul(ps_p[:, 0:PRJ0], xnT[:, t * P:(t + 1) * P], k.w0[:], start=True, stop=True).then_inc(proj_ps, 1)

                def ranks(b):
                    pe.wait_ge(oh_ready, b + 1)
                    pe.wait_ge(rank_used, b)
                    pe.wait_ge(prj_sb, NT * (b + 1))
                    flat = ohb[:].rearrange("p t e -> p (t e)")
                    nc.tensor.matmul(ps_p[:, RT:RT + NT * E0], k.tri[:], flat, start=True, stop=True)
                    nc.tensor.matmul(ps_p[:, RT + NT * E0:RT + 2 * NT * E0], k.ones_b[:], flat, start=True, stop=True).then_inc(rank_ps, 1)

                def qT_(b):
                    pe.wait_ge(qkv_ready, b + 1)
                    pe.wait_ge(xT_sb, b + 1)
                    transposes(qn, qT_ps)

                def kT_(b):
                    pe.wait_ge(qT_sb, b + 1)
                    transposes(kn, kT_ps)

                def scores(b, p, u):
                    kt, pr = u // 2, u % 2
                    if u == 0:
                        pe.wait_ge(qT_sb, b + 1)
                        pe.wait_ge(kT_sb, b + 1)
                    pe.wait_ge(exp_done, 8 * b + u + 1)
                    for j in range(2):
                        h = 2 * pr + j
                        last = nc.tensor.matmul(ps_s[:, u % 2, j, 0:L - kt * P], kz[:, p, h, kt * P:(kt + 1) * P],
                                                qT[:, p, kt * P:L], start=True, stop=True)
                    last.then_inc(s_ps, 1)

                def values(b, p, kt):
                    pe.wait_ge(masked, 8 * b + 2 * kt + 2)
                    if kt == 0:
                        pe.wait_ge(norm_done, b)
                    n = L - kt * P
                    for dst, ones in ((ps_v, False), (ps_d, True)):
                        for h in range(H0):
                            g = h // (H0 // KV0)
                            w = k.ones_f[:, 0:DH0] if ones else v[:, p, kt, g * DH0:(g + 1) * DH0]
                            last = nc.tensor.matmul(dst[h * DH0:(h + 1) * DH0, kt * P:L], w, pt[:, kt % 2, h, 0:n],
                                                    start=kt == 0, stop=kt == NT - 1)
                    last.then_inc(pv_tile, 1)

                def output(b, kT_batches):
                    pe.wait_ge(norm_done, b + 1)
                    pe.wait_ge(kT_sb, kT_batches)
                    for t in range(NT):
                        last = nc.tensor.matmul(ps_t[:, t * P:(t + 1) * P], attnT[:, t * P:(t + 1) * P], k.wo0[:], start=True, stop=True)
                    last.then_inc(wo_ps, 1)

                def body(b, p, bn, pn):
                    scores(b, p, 0)
                    scores(b, p, 1)
                    xT(bn, pn)
                    scores(b, p, 2)
                    project(bn, 0)
                    values(b, p, 0)
                    scores(b, p, 3)
                    project(bn, 1)
                    scores(b, p, 4)
                    project(bn, 2)
                    values(b, p, 1)
                    scores(b, p, 5)
                    project(bn, 3)
                    scores(b, p, 6)
                    values(b, p, 2)
                    scores(b, p, 7)
                    ranks(bn)
                    qT_(bn)
                    values(b, p, 3)
                    kT_(bn)
                    output(b, b + 2)

                xT(0, 0)
                for t in range(NT):
                    project(0, t)
                ranks(0)
                qT_(0)
                kT_(0)
                with pe.Fori(0, NB // 2 - 1) as i:
                    body(2 * i, 0, 2 * i + 1, 1)
                    body(2 * i + 1, 1, 2 * i + 2, 0)
                body(NB - 2, 0, NB - 1, 1)
                b = NB - 1
                scores(b, 1, 0)
                scores(b, 1, 1)
                scores(b, 1, 2)
                values(b, 1, 0)
                scores(b, 1, 3)
                scores(b, 1, 4)
                values(b, 1, 1)
                scores(b, 1, 5)
                scores(b, 1, 6)
                values(b, 1, 2)
                scores(b, 1, 7)
                values(b, 1, 3)
                output(b, NB)


PRO_DVE_A = 12
PRO_POOL_A = 9


class Kept:

    def __init__(self, nc, ctx):
        sb, _, sem = allocators(nc, ctx)
        self.scattered0, self.gathered1, self.scattered1 = ([sem(f"{n}{p}") for p in range(2)] for n in ("scat0_", "gath1_", "scat1_"))
        self.gathered2 = [sem(f"gath2_{q}") for q in range(4)]
        self.passed_dve, self.passed_pool, self.passed_sp = (sem(f"passed_{e}") for e in ("dve", "pool", "sp"))
        self.ident = sb("ident", [P, P])
        self.tri = sb("tri", [P, P], BF16)
        self.ones_b = sb("ones_b", [P, P], BF16)
        self.ones_f = sb("ones_f", [P, DH0])
        self.zeros = sb("zeros", [P, GRP // P * D])
        self.mhalf = sb("mhalf", [P, 32])
        self.iota_i = sb("iota_i", [P, 128], mybir.dt.int32)
        self.iota = sb("iota", [P, 128])
        self.w0 = sb("w0", [P, PRJ0])
        self.w1 = sb("w1", [P, PRJ1])
        self.wo0 = sb("wo0", [P, D])
        self.wo1 = sb("wo1", [P, D])
        self.gate = sb("gate", [P, 1])
        self.temp = sb("temp", [P, 4])
        self.br0 = sb("br0", [P, E0])
        self.run0 = sb("run0", [P, E0])
        self.run1 = sb("run1", [P, E1])
        self.table = sb("table", [P, max(NG0, NG1), 2], mybir.dt.int32)


def group_table(nc, k, run, n_exp, n_grp, n_slots, xs_d, meta_d, name):
    spare = n_exp * REG
    steps = T // GRP
    with ExitStack() as ctx:
        sb, ps, sem = allocators(nc, ctx)
        chain, fill_ready, zero_out = sem(name + "_chain"), sem(name + "_fill"), sem(name + "_zero")
        fill = sb(name + "_fill", [P, n_exp], U32)
        cnt = sb(name + "_cnt", [P, n_exp])
        lim = sb(name + "_lim", [P, steps])
        more = sb(name + "_more", [P, n_exp, steps])
        ng = sb(name + "_ng", [P, n_exp])
        upto = sb(name + "_upto", [P, n_exp])
        before = sb(name + "_before", [P, n_exp])
        row0 = sb(name + "_row0", [P, n_exp])
        ge = sb(name + "_ge", [P, 2, n_grp, n_exp])
        one = sb(name + "_one", [P, n_grp, n_exp])
        pick = sb(name + "_pick", [P, 2, n_grp, n_exp])
        got = sb(name + "_got", [P, 3, n_grp])
        gj = sb(name + "_gj", [P, 4, n_grp])
        mcols = meta_d.shape[1]
        meta = sb(name + "_meta", [P, NB, mcols], U32)
        slot = sb(name + "_slot", [P, NB, n_slots])
        first = sb(name + "_first", [P, n_exp])
        shift = sb(name + "_shift", [P, n_exp])
        step = sb(name + "_step", [P, n_exp])
        above = sb(name + "_above", [P, NB * n_slots, n_exp])
        total = sb(name + "_total", [P, NB * n_slots])
        meta_in, meta_out, meta_new = sem(name + "_meta_in"), sem(name + "_meta_out"), sem(name + "_meta_new")
        with nc.Block() as block:

            @block.sync
            def _(sp):
                sp.dma_start(meta[:], meta_d.rearrange("(b p) c -> p b c", p=P)).then_inc(meta_in, 16)
                sp.wait_ge(fill_ready, 1)
                sp.dma_start(xs_d[spare:spare + GRP, :].rearrange("(p t) d -> p (t d)", p=P), k.zeros[:]).then_inc(zero_out, 16)
                for e in range(n_exp):
                    row = sp.value_load(fill[0:1, e:e + 1], min_val=0, max_val=n_exp * REG - GRP)
                    sp.dma_start(xs_d[bass.ds(row, GRP), :].rearrange("(p t) d -> p (t d)", p=P), k.zeros[:]).then_inc(zero_out, 16)
                sp.wait_ge(meta_new, 1)
                sp.dma_start(meta_d.rearrange("(b p) c -> p b c", p=P), meta[:]).then_inc(meta_out, 16)
                sp.wait_ge(meta_out, 16)
                sp.wait_ge(zero_out, 16 * (n_exp + 1))

            @block.vector
            def _(dve):
                c = Chain(dve, chain, 0, k.passed_dve)
                c.at(0)
                nc.vector.tensor_copy(fill[:], run[:]).then_inc(fill_ready, 1)
                nc.vector.tensor_scalar(row0[:], k.iota[:, 0:n_exp], float(REG), None, ALU.mult)
                c.link(nc.vector.tensor_scalar(lim[:], k.iota[:, 0:steps], float(GRP), None, ALU.mult))
                c.link(nc.vector.tensor_tensor(cnt[:], run[:], row0[:], ALU.subtract))
                c.link(nc.vector.tensor_tensor(more[:], lim[:].unsqueeze(1).to_broadcast([P, n_exp, steps]),
                                               cnt[:].unsqueeze(2).to_broadcast([P, n_exp, steps]), ALU.is_lt))
                c.link(nc.vector.tensor_reduce(ng[:], more[:], AX, ALU.add))
                c.link(nc.vector.tensor_tensor_scan(upto[:], k.ones_f[:, 0:n_exp], ng[:], 0.0, ALU.mult, ALU.add))
                c.link(nc.vector.tensor_tensor(before[:], upto[:], ng[:], ALU.subtract))
                j3 = k.iota[:, 0:n_grp].unsqueeze(2).to_broadcast([P, n_grp, n_exp])
                for n, edge in enumerate((before, upto)):
                    nc.vector.tensor_tensor(ge[:, n], j3, edge[:].unsqueeze(1).to_broadcast([P, n_grp, n_exp]), ALU.is_ge)
                c.link(nc.vector.scalar_tensor_tensor(row0[:], before[:], -float(GRP), row0[:], ALU.mult, ALU.add))
                c.link(nc.vector.tensor_tensor(one[:], ge[:, 0], ge[:, 1], ALU.subtract))
                nc.vector.tensor_tensor(pick[:, 0], one[:], row0[:].unsqueeze(1).to_broadcast([P, n_grp, n_exp]), ALU.mult)
                c.link(nc.vector.tensor_tensor(pick[:, 1], one[:],
                                               k.iota[:, 0:n_exp].unsqueeze(1).to_broadcast([P, n_grp, n_exp]), ALU.mult))
                nc.vector.tensor_reduce(got[:, 0], pick[:, 0], AX, ALU.add)
                nc.vector.tensor_reduce(got[:, 1], pick[:, 1], AX, ALU.add)
                c.link(nc.vector.tensor_reduce(got[:, 2], one[:], AX, ALU.add))
                nc.vector.tensor_scalar(gj[:, 0], k.iota[:, 0:n_grp], float(GRP), None, ALU.mult)
                c.link(nc.vector.tensor_scalar(gj[:, 1], got[:, 2], -float(spare), float(spare), ALU.mult, ALU.add))
                c.link(nc.vector.tensor_tensor(gj[:, 2], got[:, 0], gj[:, 1], ALU.add))
                c.link(nc.vector.tensor_tensor(gj[:, 3], got[:, 2], gj[:, 0], ALU.mult))
                nc.vector.tensor_tensor(k.table[:, 0:n_grp, 0], gj[:, 2], gj[:, 3], ALU.add)
                nc.vector.tensor_scalar(k.table[:, 0:n_grp, 1], got[:, 1], float(P), None, ALU.mult)
                nc.vector.tensor_scalar(first[:], k.iota[:, 0:n_exp], float(REG), None, ALU.mult)
                nc.vector.tensor_scalar(shift[:], row0[:], -1.0, None, ALU.mult)
                dve.wait_ge(meta_in, 16)
                c.link(nc.vector.tensor_copy(slot[:], meta[:, :, 0:n_slots]))
                flat = slot[:].rearrange("p b s -> p (b s)")
                nc.vector.tensor_copy(step[:, 0:1], shift[:, 0:1])
                nc.vector.tensor_tensor(step[:, 1:n_exp], shift[:, 1:n_exp], shift[:, 0:n_exp - 1], ALU.subtract)
                wide = [P, NB * n_slots, n_exp]
                c.link(nc.vector.tensor_tensor(above[:], flat.unsqueeze(2).to_broadcast(wide),
                                               first[:].unsqueeze(1).to_broadcast(wide), ALU.is_ge))
                c.link(nc.vector.tensor_tensor(above[:], above[:], step[:].unsqueeze(1).to_broadcast(wide), ALU.mult))
                c.link(nc.vector.tensor_reduce(total[:], above[:], AX, ALU.add))
                nc.vector.tensor_tensor(meta[:, :, 0:n_slots], slot[:], total[:].rearrange("p (b s) -> p b s", b=NB),
                                        ALU.add).then_inc(meta_new, 1)


def expert_ffn(nc, k, layer, xs_d, ys_d, w_d, name):
    gated = layer == 1
    n_exp, n_grp, chunks = (E1, NG1, FC1) if gated else (E0, NG0, F0 // P)
    wup = (2 if gated else 1) * chunks * P
    wcols = w_d.shape[1]
    GT = GRP // P
    NBUF = 4
    rows = n_exp * REG
    with ExitStack() as ctx:
        sb, ps, sem = allocators(nc, ctx)
        x = sb(name + "_x", [P, NBUF, GT, D])
        w = sb(name + "_w", [P, NBUF, wcols])
        xT = sb(name + "_xT", [P, 2, GRP])
        g = sb(name + "_g", [P, 2, GRP])
        h = sb(name + "_h", [P, 2, chunks, GRP])
        y = sb(name + "_y", [P, NBUF, GT, D])
        ps_x = [ps(f"{name}_ps_x{n}", [P, 512]) for n in range(2)]
        ps_h = [ps(f"{name}_ps_h{n}", [P, 2, GRP]) for n in range(4)]
        ps_y = [ps(f"{name}_ps_y{n}", [P, 512]) for n in range(2)]
        x_in = [sem(f"{name}_x_in{n}") for n in range(NBUF)]
        w_in = [sem(f"{name}_w_in{n}") for n in range(NBUF)]
        y_out = [sem(f"{name}_y_out{n}") for n in range(NBUF)]
        xT_ps, xT_sb, h_ps, g_sb, h_sb, y_ps, y_sb = (sem(f"{name}_{n}") for n in ("xT_ps", "xT_sb", "h_ps", "g_sb", "h_sb", "y_ps", "y_sb"))
        with nc.Block() as block:

            @block.sync
            def _(sp):
                def load(j, i, q):
                    row = sp.value_load(k.table[0:1, bass.ds(j, 1), 0], min_val=0, max_val=rows)
                    wrow = sp.value_load(k.table[0:1, bass.ds(j, 1), 1], min_val=0, max_val=(n_exp - 1) * P)
                    if not (isinstance(i, int) and i == 0):
                        sp.wait_ge(y_sb, j - NBUF + 1)
                    sp.dma_start(x[:, q], xs_d[bass.ds(row, GRP), :].rearrange("(t p) d -> p t d", p=P)).then_inc(x_in[q], 16)
                    sp.dma_start(w[:, q], w_d[bass.ds(wrow, P), :]).then_inc(w_in[q], 16)

                def store(j, i, q):
                    sp.wait_ge(y_sb, j + 1)
                    sp.dma_start(ys_d[bass.ds(j * GRP, GRP), :].rearrange("(t p) d -> p t d", p=P), y[:, q]).then_inc(y_out[q], 16)

                for q in range(NBUF):
                    load(q, 0, q)
                with sp.Fori(0, n_grp // NBUF - 1) as i:
                    for q in range(NBUF):
                        load(NBUF * i + q + NBUF, i + 1, q)
                        store(NBUF * i + q, i, q)
                for q in range(NBUF):
                    store(n_grp - NBUF + q, n_grp // NBUF - 1, q)
                for q in range(NBUF):
                    sp.wait_ge(y_out[q], 16 * (n_grp // NBUF))

            def pipeline(eng, rows_of, up, down):
                last = n_grp // NBUF - 1

                def turn(i, q, final=False):
                    j = NBUF * i + q
                    if not (final and q >= NBUF - 2):
                        rows_of(j + 2, i + (q + 2) // NBUF, (q + 2) % NBUF)
                    if not (final and q >= NBUF - 1):
                        up(j + 1, i + (q + 1) // NBUF, (q + 1) % NBUF)
                    down(j, i, q)

                rows_of(0, 0, 0)
                rows_of(1, 0, 1)
                up(0, 0, 0)
                for q in range(NBUF):
                    turn(0, q)
                with eng.Fori(1, last) as i:
                    for q in range(NBUF):
                        turn(i, q)
                for q in range(NBUF):
                    turn(last, q, True)

            @block.tensor
            def _(pe):
                def rows_of(j, i, q):
                    pe.wait_ge(x_in[q], 16 * (i + 1))
                    if not isinstance(j, int) or j >= 2:
                        pe.wait_ge(xT_sb, j - 1)
                    for t in range(GT):
                        last = nc.tensor.transpose(ps_x[q % 2][:, t * P:(t + 1) * P], x[:, q, t, :], k.ident[:])
                    last.then_inc(xT_ps, 1)

                def up(j, i, q):
                    pe.wait_ge(w_in[q], 16 * (i + 1))
                    pe.wait_ge(xT_sb, j + 1)
                    for c in range(chunks):
                        u = (q * chunks + c) % 4
                        if not isinstance(j, int) or chunks * j + c >= 4:
                            pe.wait_ge(h_sb, chunks * j + c - 3)
                        for n in range(2 if gated else 1):
                            col = (n * chunks + c) * P
                            last = nc.tensor.matmul(ps_h[u][:, n, :], w[:, q, col:col + P], xT[:, q % 2, :], start=True, stop=True)
                        last.then_inc(h_ps, 1)

                def down(j, i, q):
                    pe.wait_ge(h_sb, chunks * (j + 1))
                    if not isinstance(j, int) or j >= 2:
                        pe.wait_ge(y_sb, j - 1)
                    for t in range(GT):
                        for c in range(chunks):
                            col = wup + c * D
                            last = nc.tensor.matmul(ps_y[q % 2][:, t * D:(t + 1) * D], h[:, q % 2, c, t * P:(t + 1) * P],
                                                    w[:, q, col:col + D], start=c == 0, stop=c == chunks - 1)
                    last.then_inc(y_ps, 1)

                pipeline(pe, rows_of, up, down)

            @block.scalar
            def _(act):
                def rows_of(j, i, q):
                    pass

                def up(j, i, q):
                    if not isinstance(j, int) or j >= 2:
                        act.wait_ge(y_ps, j - 1)
                    for c in range(chunks):
                        u = (q * chunks + c) % 4
                        act.wait_ge(h_ps, chunks * j + c + 1)
                        if gated:
                            if not isinstance(j, int) or chunks * j + c >= 2:
                                act.wait_ge(h_sb, chunks * j + c - 1)
                            nc.scalar.activation(g[:, u % 2, :], ps_h[u][:, 0, :], ACT.Silu).then_inc(g_sb, 1)
                        else:
                            bias = w[:, q, wup + chunks * D + c:wup + chunks * D + c + 1]
                            act.wait_ge(w_in[q], 16 * (i + 1))
                            nc.scalar.activation(h[:, q % 2, c, :], ps_h[u][:, 0, :], ACT.Gelu, bias=bias).then_inc(h_sb, 1)

                def down(j, i, q):
                    pass

                pipeline(act, rows_of, up, down)

            @block.vector
            def _(dve):
                def rows_of(j, i, q):
                    dve.wait_ge(xT_ps, j + 1)
                    if not isinstance(j, int) or j >= 2:
                        dve.wait_ge(h_ps, chunks * (j - 1))
                    nc.vector.tensor_copy(xT[:, q % 2, :], ps_x[q % 2][:, 0:GRP]).then_inc(xT_sb, 1)

                def up(j, i, q):
                    if not gated:
                        return
                    if not isinstance(j, int) or j >= 2:
                        dve.wait_ge(y_ps, j - 1)
                    for c in range(chunks):
                        u = (q * chunks + c) % 4
                        dve.wait_ge(g_sb, chunks * j + c + 1)
                        nc.vector.tensor_tensor(h[:, q % 2, c, :], ps_h[u][:, 1, :], g[:, u % 2, :], ALU.mult).then_inc(h_sb, 1)

                def down(j, i, q):
                    dve.wait_ge(y_ps, j + 1)
                    dve.wait_ge(y_out[q], 16 * i)
                    src = ps_y[q % 2][:, 0:GRP].rearrange("p (t d) -> p t d", t=GT)
                    if gated:
                        nc.vector.tensor_copy(y[:, q], src).then_inc(y_sb, 1)
                    else:
                        b2 = w[:, q, wcols - D:wcols].unsqueeze(1).to_broadcast([P, GT, D])
                        dve.wait_ge(w_in[q], 16 * (i + 1))
                        nc.vector.tensor_tensor(y[:, q], src, b2, ALU.add).then_inc(y_sb, 1)

                pipeline(dve, rows_of, up, down)


TERMS = 9
SROW = TERMS * DH1
KROWS = 96
QSCALE = float(D) ** -0.5
PRO_DVE_C, LN_DVE_C, LN_POOL_C = 9, 1, 8


def batch(i, o):
    return 2 * i + o, i + o // 2, o % 2


def layer1_attention(nc, k, ys_d, base_d, meta_d, rf_d, base2_d, meta2_d, xs2_d):
    HL = KV1
    with ExitStack() as ctx:
        sb, ps, sem = allocators(nc, ctx)
        xb = sb("c_xb", [P, 2, NT, D])
        mt = sb("c_mt", [P, 2, 4 * NT], U32)
        gy = sb("c_gy", [P, 2, 2 * NT, D])
        gsum = sb("c_gsum", [P, NT, D])
        x1 = sb("c_x1", [P, 2, NT, D])
        xr = sb("c_xr", [P, NT, D])
        xn = sb("c_xn", [P, 2, NT, D])
        stats = sb("c_stats", [P, NT, 6])
        mv = sb("c_mv", [P, NT, 2])
        tmp4 = sb("c_tmp4", [P, 3, NT])
        rstd = sb("c_rstd", [P, NT])
        r2 = sb("c_r2", [P, 2, NT])
        xnT = sb("c_xnT", [P, L])
        prj = sb("c_prj", [P, NT, PRJ1])
        rf = sb("c_rf", [P, NT, DH1])
        qk = sb("c_qk", [P, NT, 2 * P])
        vp = sb("c_vp", [P, 2, NT, KV1, 32])
        q32 = sb("c_q32", [P, L])
        qr = sb("c_qr", [P, L])
        qp = sb("c_qp", [P, 3, L], BF16)
        k32 = sb("c_k32", [96, L])
        kr = sb("c_kr", [96, L])
        kh = sb("c_kh", [96, L], BF16)
        km = sb("c_km", [96, L], BF16)
        kl = sb("c_kl", [96, L], BF16)
        kb = sb("c_kb", [96, L], BF16)
        qst = sb("c_qst", [KROWS, 2, H1, L], BF16)
        kmx = sb("c_kmx", [KROWS, 2, KV1, L], BF16)
        kex = sb("c_kex", [KROWS, 2, KV1, L], BF16)
        ones2 = sb("c_ones2", [2, 2 * KV1 * L], BF16)
        mx = sb("c_mx", [P, 2, P])
        shb = sb("c_shb", [NT * HL, 2, 2, P], BF16)
        pt = sb("c_pt", [P, 2, HL, L])
        ov = sb("c_ov", [P, L])
        rcp = sb("c_rcp", [P, NT, HL])
        sall = sb("c_sall", [P, NT, D])
        sT = sb("c_sT", [P, L])
        sx = sb("c_sx", [P, NT, D])
        bs = sb("c_bs", [P, 2, NT, D])
        mx8 = sb("c_mx8", [P, NT, 8])
        ix8 = sb("c_ix8", [P, NT, 8], U32)
        ixf = sb("c_ixf", [P, NT])
        oh = sb("c_oh", [P, NT, E1])
        ohb = sb("c_ohb", [P, NT, E1], BF16)
        pos = sb("c_pos", [P, NT, E1])
        ohp = sb("c_ohp", [P, NT, E1])
        slotf = sb("c_slotf", [P, NT])
        sl = sb("c_sl", [P, 2, NT], U32)

        ps_mx = [ps(f"c_ps_mx{n}", [P, L]) for n in range(2)]
        ps_e = ps("c_ps_e", [P, 2, 2, L])
        ps_v = ps("c_ps_v", [P, L])
        ps_j = ps("c_ps_j", [P, L])

        def sems(*names):
            return [sem("c_" + n) for n in names]

        gathered, scattered = k.gathered1, k.scattered1
        base_in, meta_in, k_in, q_in, sh_in, base2_out, meta2_out = (
            [sem(f"c_{n}{p}") for p in range(2)]
            for n in ("base_in", "meta_in", "k_in", "q_in", "sh_in", "base2_out", "meta2_out"))
        (comb_done, stats_ready, rstd_ready, xn_ready, xr_ready, xT_ps, xT_sb, proj_ps, prj_sb, qk_ready, v_ready,
         kT_ps, kT_sb, kr_ready, km_ready, kl_ready, kb_ready, qT_ps, qT_sb, qr_ready, qm_ready, ql_ready) = sems(
            "comb", "stats_r", "rstd_r", "xn_r", "xr_r", "xT_ps", "xT_sb", "proj", "prj_sb", "qk_r", "v_r",
            "kT_ps", "kT_sb", "kr_r", "km_r", "kl_r", "kb_r", "qT_ps", "qT_sb", "qr_r", "qm_r", "ql_r")
        (mx_ps, mx_done, mt_ps, sh_ready, s_ps, exp_done, pv, ov_sb, ot_ps, ot_sb, sT_ps, sT_sb, wo_ps, wo_sb,
         sx_ready, oh_ready, rank_ps, rank_used, slot_ready, const_in) = sems(
            "mx_ps", "mx_done", "mt_ps", "sh_r", "s_ps", "exp", "pv", "ov_sb", "ot_ps", "ot_sb", "sT_ps", "sT_sb",
            "wo_ps", "wo_sb", "sx_r", "oh_r", "rank_ps", "rank_u", "slot_r", "const")
        dve_pro, dve_ln, dve_sh, dve_ot, pool_ln, made = sems("dve_pro", "dve_ln", "dve_sh", "dve_ot", "pool_ln", "made")

        with nc.Block() as block:

            @block.vector
            def _(dve):
                nc.vector.memset(qst[:], 0.0).then_inc(made, 1)
                nc.vector.memset(kmx[:], 0.0).then_inc(exp_done, 2)
                nc.vector.memset(ones2[:], 1.0).then_inc(made, 1)
                nc.vector.memset(mx[:], 0.0).then_inc(mx_done, 2)

            @block.gpsimd
            def _(pool):
                nc.gpsimd.memset(kex[:], 0.0).then_inc(made, 1)
                nc.gpsimd.memset(qk[:], 0.0).then_inc(pv, 2)
                nc.gpsimd.memset(vp[:], 0.0).then_inc(made, 1)
                pool.wait_ge(made, 4)
                nc.gpsimd.memset(vp[:, :, :, :, DH1:DH1 + 1], 1.0)

            @block.sync
            def _(sp):
                sp.dma_start(rf[:], rf_d.rearrange("(t p) d -> p t d", p=P)).then_inc(const_in, 16)
                sp.wait_ge(made, 4)
                sp.dma_start(kex[SROW:SROW + 2], ones2[:]).then_inc(const_in, 16)
                sp.wait_ge(const_in, 32)

        def bodies(eng, body):
            body(0, 0)
            with eng.Fori(0, 6) as i:
                body(i, 1)
                body(i, 2)
            for o in range(13, NB):
                body(0, o)

        def flags(i, o):
            static = isinstance(i, int)
            return not (static and o == 0), not (static and o == NB - 1), not (static and o >= NB - 2)

        with nc.Block() as block:

            @block.sync
            def _(sp):
                def load(i, o):
                    b, h, p = batch(i, o)
                    if not (isinstance(b, int) and b < 2):
                        sp.wait_ge(comb_done, b - 1)
                        passed(sp, k.passed_sp)
                    sp.dma_start(xb[:, p], base_d[bass.ds(b * L, L), :].rearrange("(t p) d -> p t d", p=P)).then_inc(base_in[p], 16)
                    sp.dma_start(mt[:, p], meta_d[bass.ds(b * P, P), :]).then_inc(meta_in[p], 16)

                def k_stack(i, o):
                    b, h, p = batch(i, o)
                    sp.wait_ge(kl_ready, b + 1)
                    passed(sp, k.passed_sp)
                    sp.wait_ge(kb_ready, b + 1)
                    passed(sp, k.passed_sp)
                    if not (isinstance(b, int) and b < 2):
                        sp.wait_ge(s_ps, 32 * (b - 1))
                        passed(sp, k.passed_sp)
                        sp.wait_ge(mx_ps, 64 * (b - 1))
                        passed(sp, k.passed_sp)
                    for dst in (kmx, kex):
                        for a in range(3):
                            sp.dma_start(dst[3 * DH1 * a:3 * DH1 * (a + 1), p], kb[:]).then_inc(k_in[p], 16)

                def q_stack(i, o):
                    b, h, p = batch(i, o)
                    sp.wait_ge(ql_ready, b + 1)
                    passed(sp, k.passed_sp)
                    for t in range(TERMS):
                        sp.dma_start(qst[DH1 * t:DH1 * (t + 1), p], qp[:, t // 3, :]).then_inc(q_in[p], 16)

                def shift(i, o, g):
                    b, h, p = batch(i, o)
                    sp.wait_ge(sh_ready, 4 * b + g + 1)
                    passed(sp, k.passed_sp)
                    for n in range(2):
                        sp.dma_start(qst[SROW + n:SROW + n + 1, p, HL * g:HL * (g + 1), :],
                                     shb[:, g % 2, n, :]).then_inc(sh_in[g % 2], 16)

                def store_slots(i, o):
                    b, h, p = batch(i, o)
                    sp.wait_ge(slot_ready, b + 1)
                    passed(sp, k.passed_sp)
                    sp.dma_start(meta2_d[bass.ds(b * P, P), :], sl[:, p]).then_inc(meta2_out[p], 16)

                def store_base(i, o):
                    b, h, p = batch(i, o)
                    sp.wait_ge(wo_sb, b + 1)
                    passed(sp, k.passed_sp)
                    sp.dma_start(base2_d[bass.ds(b * L, L), :].rearrange("(t p) d -> p t d", p=P), bs[:, p]).then_inc(base2_out[p], 16)

                def body(i, o):
                    prev, nxt, nxt2 = flags(i, o)
                    if nxt2:
                        load(i, o + 2)
                    shift(i, o, 1)
                    if prev:
                        store_base(i, o - 1)
                    if nxt:
                        k_stack(i, o + 1)
                    shift(i, o, 2)
                    if nxt:
                        q_stack(i, o + 1)
                        store_slots(i, o + 1)
                    shift(i, o, 3)
                    if nxt:
                        shift(i, o + 1, 0)

                load(0, 0)
                load(0, 1)
                k_stack(0, 0)
                q_stack(0, 0)
                store_slots(0, 0)
                shift(0, 0, 0)
                bodies(sp, body)
                store_base(0, NB - 1)
                for p in range(2):
                    sp.wait_ge(base2_out[p], 16 * (NB // 2))
                    sp.wait_ge(meta2_out[p], 16 * (NB // 2))

            @block.gpsimd
            def _(pool):
                def gather(i, o):
                    b, h, p = batch(i, o)
                    pool.wait_ge(meta_in[p], 16 * (h + 1))
                    if not (isinstance(b, int) and b < 2):
                        pool.wait_ge(comb_done, b - 1)
                    passed(pool, k.passed_pool)
                    for n in range(2 * NT):
                        nc.gpsimd.indirect_dma_start(
                            gy[:, p, n, :], None, ys_d,
                            bass.IndirectOffsetOnAxis(ap=mt[:, p, n:n + 1], axis=0)).then_inc(gathered[p], 16)

                def combine(ln, i, o):
                    b, h, p = batch(i, o)
                    ln.at(b)
                    pool.wait_ge(gathered[p], 16 * 2 * NT * (h + 1))
                    pool.wait_ge(base_in[p], 16 * (h + 1))
                    w = mt[:, p, 2 * NT:4 * NT].bitcast(F32).unsqueeze(2).to_broadcast([P, 2 * NT, D])
                    ln.link(nc.gpsimd.tensor_tensor(gy[:, p], gy[:, p], w, ALU.mult))
                    ln.link(nc.gpsimd.tensor_tensor(gsum[:], gy[:, p, 0:NT, :], gy[:, p, NT:2 * NT, :], ALU.add))
                    if not (isinstance(b, int) and b < 2):
                        pool.wait_ge(xr_ready, b - 1)
                    nc.gpsimd.tensor_tensor(x1[:, p], gsum[:], xb[:, p], ALU.add).then_inc(comb_done, 1)

                def norms(ln, i, o):
                    b, h, p = batch(i, o)
                    pool.wait_ge(stats_ready, b + 1)
                    pool.wait_ge(xn_ready, b)
                    if not (isinstance(b, int) and b < 2):
                        pool.wait_ge(prj_sb, NT * (b - 1))
                    passed(pool, k.passed_pool)
                    ln.link(nc.gpsimd.tensor_scalar(tmp4[:, 0], mv[:, :, 1], EPS_LN, None, ALU.add))
                    ln.link(nc.gpsimd.tensor_tensor(rstd[:], tmp4[:, 0], k.mhalf[:, 0:NT], ALU.pow))
                    ln.link(nc.gpsimd.tensor_tensor(tmp4[:, 1], rstd[:], rstd[:], ALU.mult))
                    ln.link_apart(nc.gpsimd.tensor_tensor(tmp4[:, 2], tmp4[:, 1], mv[:, :, 1], ALU.mult))
                    ln.link(nc.gpsimd.tensor_scalar(tmp4[:, 0], tmp4[:, 2], float(np.finfo(np.float32).eps), None, ALU.add))
                    ln.link(nc.gpsimd.tensor_tensor(r2[:, p], tmp4[:, 0], k.mhalf[:, 0:NT], ALU.pow))
                    nc.gpsimd.tensor_tensor(tmp4[:, 1], r2[:, p], r2[:, p], ALU.mult).then_inc(rstd_ready, 1)

                    ln.end()

                def rotate(i, o):
                    b, h, p = batch(i, o)
                    pool.wait_ge(prj_sb, NT * (b + 1))
                    pool.wait_ge(qT_ps, b)
                    qd = prj[:, :, 0:D].rearrange("p t (d h) -> p t d h", d=DH1)
                    nc.gpsimd.tensor_tensor(qk[:, :, 0:D].rearrange("p t (d h) -> p t d h", d=DH1), qd,
                                            rf[:].unsqueeze(3).to_broadcast([P, NT, DH1, H1]), ALU.mult)
                    kd = prj[:, :, D:D + 32].rearrange("p t (d h) -> p t d h", d=DH1)
                    for r in range(3):
                        last = nc.gpsimd.tensor_tensor(
                            qk[:, :, D + 32 * r:D + 32 * (r + 1)].rearrange("p t (d h) -> p t d h", d=DH1), kd,
                            rf[:].unsqueeze(3).to_broadcast([P, NT, DH1, KV1]), ALU.mult)
                    last.then_inc(qk_ready, 1)
                    pool.wait_ge(pv, 16 * (b - 1) + 2 if not (isinstance(b, int) and b < 1) else 2)
                    passed(pool, k.passed_pool)
                    nc.gpsimd.tensor_copy(vp[:, p, :, :, 0:DH1],
                                          prj[:, :, D + 32:QKV1].rearrange("p t (h d) -> p t h d", h=KV1)).then_inc(v_ready, 1)

                def k_parts(i, o):
                    b, h, p = batch(i, o)
                    pool.wait_ge(kT_sb, b + 1)
                    pool.wait_ge(km_ready, b)
                    nc.gpsimd.tensor_tensor(kr[:], k32[:], kh[:], ALU.subtract).then_inc(kr_ready, 1)
                    pool.wait_ge(km_ready, b + 1)
                    pool.wait_ge(kb_ready, b)
                    nc.gpsimd.tensor_tensor(kl[:], kr[:], km[:], ALU.subtract).then_inc(kl_ready, 1)

                def q_parts(i, o):
                    b, h, p = batch(i, o)
                    pool.wait_ge(qT_sb, b + 1)
                    pool.wait_ge(qm_ready, b)
                    nc.gpsimd.tensor_tensor(qr[:], q32[:], qp[:, 0, :], ALU.subtract).then_inc(qr_ready, 1)
                    pool.wait_ge(qm_ready, b + 1)
                    nc.gpsimd.tensor_tensor(qp[:, 2, :], qr[:], qp[:, 1, :], ALU.subtract).then_inc(ql_ready, 1)

                def residual(i, o):
                    b, h, p = batch(i, o)
                    pool.wait_ge(ot_sb, 4 * (b + 1))
                    pool.wait_ge(xr_ready, b + 1)
                    pool.wait_ge(wo_sb, b)
                    nc.gpsimd.tensor_tensor(sx[:], sall[:], xr[:], ALU.add).then_inc(sx_ready, 1)

                def scatter(i, o):
                    b, h, p = batch(i, o)
                    pool.wait_ge(slot_ready, b + 1)
                    passed(pool, k.passed_pool)
                    for t in range(NT):
                        nc.gpsimd.indirect_dma_start(
                            xs2_d, bass.IndirectOffsetOnAxis(ap=sl[:, p, t:t + 1], axis=0),
                            xn[:, p, t, :], None).then_inc(scattered[p], 16)

                ln = Chain(pool, pool_ln, LN_POOL_C, k.passed_pool)

                def body(i, o):
                    prev, nxt, nxt2 = flags(i, o)
                    if prev:
                        residual(i, o - 1)
                    if nxt:
                        rotate(i, o + 1)
                    if nxt2:
                        gather(i, o + 2)
                    if nxt:
                        k_parts(i, o + 1)
                        q_parts(i, o + 1)
                        scatter(i, o + 1)
                    if nxt2:
                        combine(ln, i, o + 2)
                        norms(ln, i, o + 2)

                for o in range(2):
                    gather(0, o)
                for o in range(2):
                    combine(ln, 0, o)
                    norms(ln, 0, o)
                rotate(0, 0)
                k_parts(0, 0)
                q_parts(0, 0)
                scatter(0, 0)
                bodies(pool, body)
                residual(0, NB - 1)
                for p in range(2):
                    pool.wait_ge(scattered[p], 16 * NT * (NB // 2))

            @block.scalar
            def _(act):
                def exps(i, o, s, half):
                    b, h, p = batch(i, o)
                    gs = 16 * b + s
                    act.wait_ge(s_ps, 2 * gs + half + 1)
                    if half == 0:
                        act.wait_ge(pv, gs + 1)
                    nc.scalar.activation(pt[:, s % 2, 2 * half:2 * half + 2, :], ps_e[:, half], ACT.Exp,
                                         scale=QSCALE).then_inc(exp_done, 1)

                def ov_copy(i, o, g):
                    b, h, p = batch(i, o)
                    act.wait_ge(pv, 4 * (4 * b + g + 1) + 2)
                    act.wait_ge(ot_ps, 4 * b + g)
                    nc.scalar.activation(ov[:], ps_v[:], ACT.Copy).then_inc(ov_sb, 1)

                def xT_copy(i, o):
                    b, h, p = batch(i, o)
                    act.wait_ge(xT_ps, b + 1)
                    act.wait_ge(proj_ps, 2 * b)
                    nc.scalar.activation(xnT[:], ps_j[:], ACT.Copy).then_inc(xT_sb, 1)

                def prj_copy(i, o, pair):
                    b, h, p = batch(i, o)
                    act.wait_ge(proj_ps, 2 * b + pair + 1)
                    if pair == 0:
                        act.wait_ge(rstd_ready, b + 1)
                        act.wait_ge(v_ready, b)
                        act.wait_ge(oh_ready, b)
                    for t in (2 * pair, 2 * pair + 1):
                        nc.scalar.activation(prj[:, t, :], ps_j[:, t % 2 * PRJ1:(t % 2 + 1) * PRJ1], ACT.Copy,
                                             scale=r2[:, p, t:t + 1]).then_inc(prj_sb, 1)

                def kT_copy(i, o):
                    b, h, p = batch(i, o)
                    act.wait_ge(kT_ps, b + 1)
                    act.wait_ge(kb_ready, b)
                    act.wait_ge(kr_ready, b)
                    nc.scalar.activation(kh[:], ps_j[0:96, :], ACT.Copy)
                    nc.scalar.activation(k32[:], ps_j[0:96, :], ACT.Copy).then_inc(kT_sb, 1)

                def qT_copy(i, o):
                    b, h, p = batch(i, o)
                    _, hq, pq = batch(i, o + 1)
                    act.wait_ge(qT_ps, b + 1)
                    act.wait_ge(qr_ready, b)
                    if not (isinstance(b, int) and b < 1):
                        act.wait_ge(q_in[pq], 16 * TERMS * hq)
                    nc.scalar.activation(qp[:, 0, :], ps_j[:], ACT.Copy)
                    nc.scalar.activation(q32[:], ps_j[:], ACT.Copy).then_inc(qT_sb, 1)

                def sT_copy(i, o):
                    b, h, p = batch(i, o)
                    act.wait_ge(sT_ps, b + 1)
                    act.wait_ge(wo_ps, b)
                    nc.scalar.activation(sT[:], ps_j[:], ACT.Copy).then_inc(sT_sb, 1)

                def body(i, o):
                    prev, nxt, nxt2 = flags(i, o)
                    for s in range(16):
                        exps(i, o, s, 0)
                        if s == 0 and nxt:
                            xT_copy(i, o + 1)
                        if s == 2 and nxt:
                            prj_copy(i, o + 1, 0)
                        if s == 3 and prev:
                            sT_copy(i, o - 1)
                        if s == 4 and nxt:
                            kT_copy(i, o + 1)
                        if s == 0 and prev:
                            ov_copy(i, o - 1, 3)
                        if s > 0 and s % 4 == 0:
                            ov_copy(i, o, s // 4 - 1)
                        exps(i, o, s, 1)
                        if s == 2 and nxt:
                            prj_copy(i, o + 1, 1)
                        if s == 4 and nxt:
                            qT_copy(i, o + 1)

                xT_copy(0, 0)
                prj_copy(0, 0, 0)
                prj_copy(0, 0, 1)
                kT_copy(0, 0)
                qT_copy(0, 0)
                bodies(act, body)
                ov_copy(0, NB - 1, 3)
                sT_copy(0, NB - 1)

            @block.vector
            def _(dve):
                def row_max(i, o, n):
                    b, h, p = batch(i, o)
                    g = n // 16
                    if n % 16 == 0 and not (isinstance(b, int) and 4 * b + g < 2):
                        dve.wait_ge(mt_ps, 4 * b + g - 1)
                    dve.wait_ge(mx_ps, 64 * b + n + 1)
                    nc.vector.tensor_reduce(mx[:, g % 2, n % 16:n % 16 + 1], ps_mx[n % 2][:], AX, ALU.max).then_inc(mx_done, 1)

                def shifts(i, o, g):
                    b, h, p = batch(i, o)
                    dve.wait_ge(mt_ps, 4 * b + g + 1)
                    if not (isinstance(b, int) and 4 * b + g < 2):
                        dve.wait_ge(sh_in[g % 2], 32 * (2 * b + g // 2))
                    src = ps_j[0:NT * HL, 0:P]
                    nc.vector.tensor_scalar(shb[:, g % 2, 0, :], src, -1.0, None, ALU.mult).then_inc(dve_sh, 1)
                    dve.wait_ge(dve_sh, 4 * b + g + 1)
                    nc.vector.scalar_tensor_tensor(shb[:, g % 2, 1, :], src, -1.0, shb[:, g % 2, 0, :],
                                                   ALU.mult, ALU.subtract).then_inc(sh_ready, 1)

                def normalise(i, o, g):
                    b, h, p = batch(i, o)
                    dve.wait_ge(ot_ps, 4 * b + g + 1)
                    src = ps_j[:].rearrange("p (t h c) -> p t h c", t=NT, h=HL)
                    if g == 0:
                        dve.wait_ge(sx_ready, b)
                        dve.wait_ge(sT_ps, b)
                    nc.vector.reciprocal(rcp[:], src[:, :, :, DH1]).then_inc(dve_ot, 1)
                    dve.wait_ge(dve_ot, 4 * b + g + 1)
                    nc.vector.tensor_tensor(sall[:, :, 32 * g:32 * (g + 1)].rearrange("p t (h d) -> p t h d", h=HL),
                                            src[:, :, :, 0:DH1], rcp[:].unsqueeze(3).to_broadcast([P, NT, HL, DH1]),
                                            ALU.mult).then_inc(ot_sb, 1)

                def output(i, o):
                    b, h, p = batch(i, o)
                    dve.wait_ge(wo_ps, b + 1)
                    dve.wait_ge(sx_ready, b + 1)
                    dve.wait_ge(base2_out[p], 16 * h)
                    nc.vector.tensor_tensor(bs[:, p].rearrange("p t d -> p (t d)"), ps_j[:],
                                            sx[:].rearrange("p t d -> p (t d)"), ALU.add).then_inc(wo_sb, 1)

                def keep_x1(i, o):
                    b, h, p = batch(i, o)
                    dve.wait_ge(sx_ready, b)
                    dve.wait_ge(comb_done, b + 1)
                    nc.vector.tensor_copy(xr[:], x1[:, p]).then_inc(xr_ready, 1)

                def k_mid(i, o):
                    b, h, p = batch(i, o)
                    dve.wait_ge(kr_ready, b + 1)
                    dve.wait_ge(kl_ready, b)
                    nc.vector.tensor_copy(km[:], kr[:]).then_inc(km_ready, 1)

                def k_join(i, o):
                    b, h, p = batch(i, o)
                    _, hq, pq = batch(i, o + 1)
                    if not (isinstance(b, int) and b < 1):
                        dve.wait_ge(k_in[pq], 16 * 6 * hq)
                    dve.wait_ge(km_ready, b + 1)
                    dve.wait_ge(kT_sb, b + 1)
                    dve.wait_ge(kl_ready, b + 1)
                    for n, part in enumerate((kh, km, kl)):
                        rows = slice(32 * n, 32 * (n + 1))
                        last = nc.vector.tensor_copy(kb[rows], part[rows])
                    last.then_inc(kb_ready, 1)

                def q_mid(i, o):
                    b, h, p = batch(i, o)
                    dve.wait_ge(qr_ready, b + 1)
                    nc.vector.tensor_copy(qp[:, 1, :], qr[:]).then_inc(qm_ready, 1)

                pro = Chain(dve, dve_pro, PRO_DVE_C, k.passed_dve)

                def choose(i, o):
                    b, h, p = batch(i, o)
                    pro.at(b)
                    dve.wait_ge(prj_sb, NT * (b + 1))
                    passed(dve, k.passed_dve)
                    lg = prj[:, :, QKV1:PRJ1]
                    for t in range(NT):
                        last = nc.vector.max(mx8[:, t, :], lg[:, t, :])
                    pro.link_apart(last)
                    for t in range(NT):
                        last = nc.vector.max_index(ix8[:, t, :], mx8[:, t, :], lg[:, t, :])
                    pro.link(last)
                    pro.link(nc.vector.tensor_copy(ixf[:], ix8[:, :, 0]))
                    pro.link(nc.vector.tensor_tensor(oh[:], k.iota[:, 0:E1].unsqueeze(1).to_broadcast([P, NT, E1]),
                                                     ixf[:].unsqueeze(2).to_broadcast([P, NT, E1]), ALU.is_equal))
                    dve.wait_ge(rank_ps, b)
                    nc.vector.tensor_copy(ohb[:], oh[:]).then_inc(oh_ready, 1)

                def slots(i, o):
                    b, h, p = batch(i, o)
                    dve.wait_ge(rank_ps, b + 1)
                    for t in range(NT):
                        nc.vector.tensor_tensor(pos[:, t], ps_j[:, t * E1:(t + 1) * E1], k.run1[:], ALU.add)
                        last = nc.vector.tensor_tensor(k.run1[:], ps_j[:, (NT + t) * E1:(NT + t + 1) * E1], k.run1[:], ALU.add)
                        if t < NT - 1:
                            pro.link(last)
                    last.then_inc(rank_used, 1)
                    dve.wait_ge(rank_used, b + 1)
                    pro.link(nc.vector.tensor_tensor(ohp[:], oh[:], pos[:], ALU.mult))
                    pro.link(nc.vector.tensor_reduce(slotf[:], ohp[:], AX, ALU.add))
                    dve.wait_ge(scattered[p], 16 * NT * h)
                    dve.wait_ge(meta2_out[p], 16 * h)
                    nc.vector.tensor_copy(sl[:, p], slotf[:]).then_inc(slot_ready, 1)
                    pro.end()

                ln = Chain(dve, dve_ln, LN_DVE_C, k.passed_dve)

                def statistics(i, o):
                    b, h, p = batch(i, o)
                    ln.at(b)
                    dve.wait_ge(comb_done, b + 1)
                    dve.wait_ge(rstd_ready, b)
                    for t in range(NT):
                        last = nc.vector.bn_stats(stats[:, t, :], x1[:, p, t, :])
                    ln.link_apart(last)
                    for t in range(NT):
                        last = nc.vector.bn_aggr(mv[:, t, :], stats[:, t, :])
                    last.then_inc(stats_ready, 1)
                    ln.end()

                def normal_rows(i, o):
                    b, h, p = batch(i, o)
                    dve.wait_ge(rstd_ready, b + 1)
                    dve.wait_ge(scattered[p], 16 * NT * h)
                    for t in range(NT):
                        last = nc.vector.tensor_scalar(xn[:, p, t, :], x1[:, p, t, :], mv[:, t, 0:1], rstd[:, t:t + 1],
                                                       ALU.subtract, ALU.mult)
                    last.then_inc(xn_ready, 1)

                def maxima(i, o, s, first):
                    m = s + 7
                    if m >= 16 and not flags(i, o)[1]:
                        return
                    for j in (0, 1) if first else (2, 3):
                        row_max(i, o + m // 16, 4 * (m % 16) + j)

                def body(i, o):
                    prev, nxt, nxt2 = flags(i, o)
                    for s in range(16):
                        maxima(i, o, s, True)
                        if s in (1, 5, 9):
                            shifts(i, o, s // 4 + 1)
                        if s == 13 and nxt:
                            shifts(i, o + 1, 0)
                        if s == 5 and nxt:
                            k_mid(i, o + 1)
                        maxima(i, o, s, False)
                        if s == 1 and prev:
                            normalise(i, o - 1, 3)
                        if s == 3:
                            if prev:
                                output(i, o - 1)
                            keep_x1(i, o)
                        if s == 4 and nxt:
                            choose(i, o + 1)
                        if s in (5, 9, 13):
                            normalise(i, o, s // 4 - 1)
                        if s == 6 and nxt:
                            k_join(i, o + 1)
                            q_mid(i, o + 1)
                        if s == 7 and nxt:
                            slots(i, o + 1)
                        if s == 11 and nxt2:
                            statistics(i, o + 2)
                        if s == 14 and nxt2:
                            normal_rows(i, o + 2)

                for o in range(2):
                    statistics(0, o)
                    normal_rows(0, o)
                choose(0, 0)
                k_mid(0, 0)
                k_join(0, 0)
                q_mid(0, 0)
                slots(0, 0)
                for m in range(7):
                    for j in range(4):
                        row_max(0, 0, 4 * m + j)
                    if m == 3:
                        shifts(0, 0, 0)
                bodies(dve, body)
                normalise(0, NB - 1, 3)
                output(0, NB - 1)

            @block.tensor
            def _(pe):
                def scores(i, o, s, half):
                    b, h, p = batch(i, o)
                    g, kt = s // 4, s % 4
                    if kt == 0 and half == 0:
                        pe.wait_ge(sh_in[g % 2], 32 * (2 * b + g // 2 + 1))
                    pe.wait_ge(exp_done, 2 * (16 * b + s) + half + 1)
                    for j in range(2):
                        hl = 2 * half + j
                        last = nc.tensor.matmul(ps_e[:, half, j, :], kex[:, p, hl, kt * P:(kt + 1) * P],
                                                qst[:, p, HL * g + hl, :], start=True, stop=True)
                    last.then_inc(s_ps, 1)

                def values(i, o, s):
                    b, h, p = batch(i, o)
                    gs = 16 * b + s
                    kt = s % 4
                    pe.wait_ge(exp_done, 2 * gs + 4)
                    if kt == 0:
                        pe.wait_ge(ov_sb, 4 * b + s // 4)
                    if s == 0:
                        pe.wait_ge(v_ready, b + 1)
                    for hl in range(HL):
                        last = nc.tensor.matmul(ps_v[32 * hl:32 * (hl + 1), :], vp[:, p, kt, hl, :], pt[:, s % 2, hl, :],
                                                start=kt == 0, stop=kt == NT - 1)
                    last.then_inc(pv, 1)

                def score_max(i, o, n):
                    b, h, p = batch(i, o)
                    g, hl, qt = n // 16, n // 4 % 4, n % 4
                    if n == 0:
                        pe.wait_ge(k_in[p], 16 * 6 * (h + 1))
                        pe.wait_ge(q_in[p], 16 * TERMS * (h + 1))
                    pe.wait_ge(mx_done, 64 * b + n + 1)
                    nc.tensor.matmul(ps_mx[n % 2][:], qst[:, p, HL * g + hl, qt * P:(qt + 1) * P], kmx[:, p, hl, :],
                                     start=True, stop=True).then_inc(mx_ps, 1)

                def maxima(i, o, s, first):
                    m = s + 7
                    if m >= 16 and not flags(i, o)[1]:
                        return
                    for j in (0, 1) if first else (2, 3):
                        score_max(i, o + m // 16, 4 * (m % 16) + j)

                def transposes(src, done):
                    for t in range(NT):
                        last = nc.tensor.transpose(ps_j[:, t * P:(t + 1) * P], src(t), k.ident[:])
                    last.then_inc(done, 1)

                def x_rows(i, o):
                    b, h, p = batch(i, o)
                    pe.wait_ge(xn_ready, b + 1)
                    transposes(lambda t: xn[:, p, t, :], xT_ps)

                def project(i, o, pair):
                    b, h, p = batch(i, o)
                    pe.wait_ge(xT_sb, b + 1)
                    for t in (2 * pair, 2 * pair + 1):
                        last = nc.tensor.matmul(ps_j[:, t % 2 * PRJ1:(t % 2 + 1) * PRJ1], xnT[:, t * P:(t + 1) * P], k.w1[:],
                                                start=True, stop=True)
                    last.then_inc(proj_ps, 1)

                def k_columns(i, o):
                    b, h, p = batch(i, o)
                    pe.wait_ge(qk_ready, b + 1)
                    transposes(lambda t: qk[:, t, P:2 * P], kT_ps)

                def q_columns(i, o):
                    transposes(lambda t: qk[:, t, 0:P], qT_ps)

                def ranks(i, o):
                    b, h, p = batch(i, o)
                    pe.wait_ge(oh_ready, b + 1)
                    flat = ohb[:].rearrange("p t e -> p (t e)")
                    nc.tensor.matmul(ps_j[:, 0:NT * E1], k.tri[:], flat, start=True, stop=True)
                    nc.tensor.matmul(ps_j[:, NT * E1:2 * NT * E1], k.ones_b[:], flat, start=True, stop=True).then_inc(rank_ps, 1)

                def max_columns(i, o, g):
                    b, h, p = batch(i, o)
                    pe.wait_ge(mx_done, 16 * (4 * b + g + 1) + 2)
                    nc.tensor.transpose(ps_j[:, 0:P], mx[:, g % 2, :], k.ident[:]).then_inc(mt_ps, 1)

                def token_rows(i, o, g):
                    b, h, p = batch(i, o)
                    pe.wait_ge(ov_sb, 4 * b + g + 1)
                    transposes(lambda t: ov[:, t * P:(t + 1) * P], ot_ps)

                def s_rows(i, o):
                    b, h, p = batch(i, o)
                    pe.wait_ge(ot_sb, 4 * (b + 1))
                    transposes(lambda t: sall[:, t, :], sT_ps)

                def s_project(i, o):
                    b, h, p = batch(i, o)
                    pe.wait_ge(sT_sb, b + 1)
                    for t in range(NT):
                        last = nc.tensor.matmul(ps_j[:, t * P:(t + 1) * P], sT[:, t * P:(t + 1) * P], k.wo1[:],
                                                start=True, stop=True)
                    last.then_inc(wo_ps, 1)

                def body(i, o):
                    prev, nxt, nxt2 = flags(i, o)
                    b, n = batch(i, o)[0], batch(i, o + 1)[0]
                    for s in range(16):
                        scores(i, o, s, 0)
                        if s == 0 and nxt:
                            pe.wait_ge(*((ot_sb, 4 * b - 1) if prev else (sh_ready, 1)))
                            x_rows(i, o + 1)
                        if s == 1:
                            pe.wait_ge(*((xT_sb, n + 1) if nxt else (ot_sb, 4 * b - 1)))
                            max_columns(i, o, 1)
                        if s == 2 and nxt:
                            pe.wait_ge(*((ot_sb, 4 * b) if prev else (sh_ready, 2)))
                            project(i, o + 1, 0)
                        if s == 3 and prev:
                            pe.wait_ge(*((prj_sb, NT * (n + 1)) if nxt else (ot_sb, 4 * b)))
                            s_rows(i, o - 1)
                        if s == 4 and nxt:
                            pe.wait_ge(*((wo_sb, b) if prev else (prj_sb, NT * (n + 1))))
                            k_columns(i, o + 1)
                        if s == 5:
                            pe.wait_ge(*((qT_sb, n + 1) if nxt else (wo_sb, b)))
                            max_columns(i, o, 2)
                        if s == 7 and nxt:
                            pe.wait_ge(ot_sb, 4 * b + 1)
                            ranks(i, o + 1)
                        if s == 9:
                            pe.wait_ge(*((rank_used, n + 1) if nxt else (ot_sb, 4 * b + 1)))
                            max_columns(i, o, 3)
                        if s == 13 and nxt:
                            pe.wait_ge(ot_sb, 4 * b + 2)
                            max_columns(i, o + 1, 0)
                        maxima(i, o, s, True)
                        if s > 0:
                            values(i, o, s - 1)
                        elif prev:
                            values(i, o - 1, 15)
                        scores(i, o, s, 1)
                        if s == 1 and prev:
                            pe.wait_ge(sh_ready, 4 * b + 2)
                            token_rows(i, o - 1, 3)
                        if s == 2 and nxt:
                            pe.wait_ge(prj_sb, NT * n + 2)
                            project(i, o + 1, 1)
                        if s == 3 and prev:
                            s_project(i, o - 1)
                        if s == 4 and nxt:
                            pe.wait_ge(kT_sb, n + 1)
                            q_columns(i, o + 1)
                        if s in (5, 9):
                            pe.wait_ge(sh_ready, 4 * b + s // 4 + 2)
                            token_rows(i, o, s // 4 - 1)
                        if s == 13:
                            pe.wait_ge(*((sh_ready, 4 * b + 5) if nxt else (ot_sb, 4 * b + 2)))
                            token_rows(i, o, 2)
                        maxima(i, o, s, False)

                x_rows(0, 0)
                project(0, 0, 0)
                pe.wait_ge(prj_sb, 2)
                project(0, 0, 1)
                pe.wait_ge(prj_sb, NT)
                k_columns(0, 0)
                pe.wait_ge(kT_sb, 1)
                q_columns(0, 0)
                pe.wait_ge(qT_sb, 1)
                ranks(0, 0)
                for m in range(7):
                    for j in range(4):
                        score_max(0, 0, 4 * m + j)
                    if m == 3:
                        pe.wait_ge(rank_used, 1)
                        max_columns(0, 0, 0)
                bodies(pe, body)
                values(0, NB - 1, 15)
                pe.wait_ge(ot_sb, 4 * NB - 1)
                token_rows(0, NB - 1, 3)
                s_rows(0, NB - 1)
                s_project(0, NB - 1)


def output_rows(nc, k, ys2_d, base2_d, meta2_d, out_d):
    NBUF = 4
    with ExitStack() as ctx:
        sb, ps, sem = allocators(nc, ctx)
        xb = sb("o_xb", [P, NBUF, NT, D])
        sl = sb("o_sl", [P, NBUF, NT], U32)
        gy = sb("o_gy", [P, NBUF, NT, D])
        ob = sb("o_ob", [P, NBUF, NT, D])
        gathered = k.gathered2
        base_in, slot_in, stored = ([sem(f"o_{n}{q}") for q in range(NBUF)] for n in ("base_in", "slot_in", "stored"))
        added = sem("o_added")
        with nc.Block() as block:

            @block.sync
            def _(sp):
                def load(b, i, q):
                    if not isinstance(i, int):
                        sp.wait_ge(added, b - NBUF + 1)
                        passed(sp, k.passed_sp)
                    sp.dma_start(sl[:, q], meta2_d[bass.ds(b * P, P), :]).then_inc(slot_in[q], 16)
                    sp.dma_start(xb[:, q], base2_d[bass.ds(b * L, L), :].rearrange("(t p) d -> p t d", p=P)).then_inc(base_in[q], 16)

                for q in range(NBUF):
                    load(q, 0, q)
                with sp.Fori(1, NB // NBUF) as i:
                    for q in range(NBUF):
                        load(NBUF * i + q, i, q)

            @block.gpsimd
            def _(pool):
                with pool.Fori(0, NB // NBUF) as i:
                    for q in range(NBUF):
                        pool.wait_ge(slot_in[q], 16 * (i + 1))
                        pool.wait_ge(added, NBUF * i)
                        passed(pool, k.passed_pool)
                        for t in range(NT):
                            nc.gpsimd.indirect_dma_start(
                                gy[:, q, t, :], None, ys2_d,
                                bass.IndirectOffsetOnAxis(ap=sl[:, q, t:t + 1], axis=0)).then_inc(gathered[q], 16)

            @block.vector
            def _(dve):
                with dve.Fori(0, NB // NBUF) as i:
                    for q in range(NBUF):
                        dve.wait_ge(base_in[q], 16 * (i + 1))
                        dve.wait_ge(gathered[q], 16 * NT * (i + 1))
                        dve.wait_ge(stored[q], 16 * i)
                        nc.vector.tensor_tensor(ob[:, q], gy[:, q], xb[:, q], ALU.add).then_inc(added, 1)

            @block.scalar
            def _(act):
                with act.Fori(0, NB // NBUF) as i:
                    for q in range(NBUF):
                        b = NBUF * i + q
                        act.wait_ge(added, b + 1)
                        act.dma_start(out_d[bass.ds(b * L, L), :].rearrange("(t p) d -> p t d", p=P), ob[:, q]).then_inc(stored[q], 16)
                for q in range(NBUF):
                    act.wait_ge(stored[q], 16 * (NB // NBUF))


def build(nc, i, out):
    def dram(name, shape, dt=F32):
        return nc.dram_tensor(name, shape, dt, kind="Internal").ap()

    base = dram("base", [T, D])
    meta = dram("meta", [NB * P, 4 * NT], U32)
    xs = dram("xs", [E0 * REG + GRP, D])
    ys = dram("ys", [NG0 * GRP, D])
    base2 = dram("base2", [T, D])
    meta2 = dram("meta2", [NB * P, NT], U32)
    xs2 = dram("xs2", [E1 * REG + GRP, D])
    ys2 = dram("ys2", [NG1 * GRP, D])
    with ExitStack() as ctx:
        k = Kept(nc, ctx)
        setup(nc, k, i)
        layer0_attention(nc, k, i["x"], base, meta, xs)
        group_table(nc, k, k.run0, E0, NG0, 2 * NT, xs, meta, "gt0")
        expert_ffn(nc, k, 0, xs, ys, i["we0"], "f0")
        layer1_attention(nc, k, ys, base, meta, i["rf"], base2, meta2, xs2)
        group_table(nc, k, k.run1, E1, NG1, NT, xs2, meta2, "gt1")
        expert_ffn(nc, k, 1, xs2, ys2, i["we1"], "f1")
        output_rows(nc, k, ys2, base2, meta2, out)


def rotary_factors():
    d = np.arange(DH1)
    theta = np.power(np.float32(10000.0), (-2.0 * (d // 2) / DH1).astype(np.float32)).astype(np.float32)
    ang = (np.arange(L, dtype=np.float32)[:, None] * theta[None, :]).astype(np.float32)
    sign = np.where(np.arange(L) % 2 == 1, -1.0, 1.0).astype(np.float32)
    return (np.cos(ang) + sign[:, None] * np.sin(ang)).astype(np.float32)


def laid_out(a):
    def heads_last(w, heads):
        return w.reshape(D, heads, DH1).transpose(0, 2, 1).reshape(D, heads * DH1)

    def chunked(w):
        out = np.zeros((E1, D, FC1 * P), w.dtype)
        out[:, :, :F1] = w.transpose(0, 2, 1)
        return out

    down = np.zeros((E1, FC1 * P, D), a["L1_ffn_down_w"].dtype)
    down[:, :F1] = a["L1_ffn_down_w"].transpose(0, 2, 1)
    arrays = {
        "x": a["L0_attn_x"].reshape(T, D),
        "w0cat": np.concatenate([a["L0_attn_Wq"], a["L0_attn_Wk"], a["L0_attn_Wv"], a["L0_ffn_Wr"]], 1),
        "w1cat": np.concatenate([heads_last(a["L1_attn_w_q"], H1), heads_last(a["L1_attn_w_k"], KV1), a["L1_attn_w_v"],
                                 a["L1_ffn_router_w"].T], 1),
        "L0_attn_Wo": a["L0_attn_Wo"],
        "L1_attn_w_o": a["L1_attn_w_o"],
        "norms": np.stack([a["L0_attn_norm_w"], a["L1_attn_g"]], 1),
        "gate": np.broadcast_to(a["L0_attn_gate"], (P, 1)),
        "logt": np.broadcast_to(a["L0_attn_log_temperature"], (P, 4)),
        "br0": np.broadcast_to(a["L0_ffn_br"], (P, E0)),
        "we0": np.concatenate([
            a["L0_ffn_W1"], a["L0_ffn_W2"].reshape(E0, F0 // P, P, D).transpose(0, 2, 1, 3).reshape(E0, P, F0 // P * D),
            a["L0_ffn_b1"].reshape(E0, F0 // P, P).transpose(0, 2, 1),
            np.broadcast_to(a["L0_ffn_b2"][:, None, :], (E0, P, D))], 2).reshape(E0 * P, -1),
        "we1": np.concatenate([
            chunked(a["L1_ffn_gate_w"]), chunked(a["L1_ffn_up_w"]),
            down.reshape(E1, FC1, P, D).transpose(0, 2, 1, 3).reshape(E1, P, FC1 * D)], 2).reshape(E1 * P, -1),
        "rf": rotary_factors(),
    }
    return {n: np.ascontiguousarray(v) for n, v in arrays.items()}


def kernel(**inputs):
    import concourse.bacc as bacc
    from concourse.bass_utils import run_bass_kernel_spmd

    nc = bacc.Bacc("TRN2", target_bir_lowering=False, num_devices=1)
    arrays = {f"in_{n}": v for n, v in laid_out({n: np.asarray(v) for n, v in inputs.items()}).items()}
    aps = {n[3:]: nc.dram_tensor(n, v.shape, mybir.dt.from_np(v.dtype), kind="ExternalInput").ap() for n, v in arrays.items()}
    out = nc.dram_tensor("out", (T, D), F32, kind="ExternalOutput").ap()
    build(nc, aps, out)
    r = run_bass_kernel_spmd(nc, [arrays], core_ids=[0])
    return r.results[0]["out"].reshape(NB, L, D)
```

```python
from contextlib import ExitStack

import numpy as np

import concourse.bass as bass
from concourse import mybir

F32 = mybir.dt.float32
BF16 = mybir.dt.bfloat16
U32 = mybir.dt.uint32
ALU = mybir.AluOpType
ACT = mybir.ActivationFunctionType
AX = mybir.AxisListType.X

P = 128
D = 128
NB, L = 16, 512
T = NB * L
NT = L // P
EPS_LN = 1e-5

H0, KV0, DH0 = 4, 2, 32
E0, F0 = 16, 256
QKV0 = D + 2 * KV0 * DH0
PRJ0 = QKV0 + E0
H1, KV1, DH1 = 16, 4, 8
REP1 = H1 // KV1
E1, F1 = 8, 352
FC1 = 3
QKV1 = D + 2 * KV1 * DH1
PRJ1 = QKV1 + E1

GRP = 2 * P
REG = T + GRP
NG0 = 2 * T // GRP + E0
NG1 = T // GRP + E1


class Chain:

    def __init__(self, eng, sem, per, passed_count=None):
        self.eng, self.sem, self.per, self.passed = eng, sem, per, passed_count

    def at(self, b):
        self.base, self.n = b * self.per, 0

    def link(self, ins):
        self.n += 1
        ins.then_inc(self.sem, 1)
        self.eng.wait_ge(self.sem, self.base + self.n)

    def link_apart(self, ins):
        self.n += 1
        ins.then_inc(self.sem, 1)
        self.eng.wait_ge(self.sem, self.base + self.n)
        passed(self.eng, self.passed)

    def end(self):
        assert self.n == self.per, (self.sem, self.n, self.per)


def passed(eng, count):
    eng.sem_inc(count, 1)


def allocators(nc, ctx):
    taken = []

    def clear():
        with nc.Block() as block:

            @block.gpsimd
            def _(pool):
                for num in sorted(taken):
                    if num - 1 not in taken:
                        end = next(n for n in range(num, 999) if n not in taken)
                        pool.sem_clear(range(num, end))

    ctx.callback(lambda: clear() if taken else None)

    def sb(name, shape, dt=F32):
        return ctx.enter_context(nc.sbuf_tensor(name, shape, dt))

    def ps(name, shape, dt=F32):
        return ctx.enter_context(nc.psum_tensor(name, shape, dt))

    def sem(name):
        s = ctx.enter_context(nc.semaphore(name))
        taken.append(s.num)
        return s

    return sb, ps, sem


def setup(nc, k, i):
    with ExitStack() as ctx:
        sb, ps, sem = allocators(nc, ctx)
        loaded = sem("su_loaded")
        pool_made = sem("su_pool")
        dve_made = sem("su_dve")
        act_made = sem("su_act")
        w0 = sb("su_w0", [P, PRJ0])
        w1 = sb("su_w1", [P, PRJ1])
        g0 = sb("su_g0", [P, 2])
        with nc.Block() as block:

            @block.sync
            def _(sp):
                sp.dma_start(w0[:], i["w0cat"]).then_inc(loaded, 16)
                sp.dma_start(w1[:], i["w1cat"]).then_inc(loaded, 16)
                sp.dma_start(k.wo0[:], i["L0_attn_Wo"]).then_inc(loaded, 16)
                sp.dma_start(k.wo1[:], i["L1_attn_w_o"]).then_inc(loaded, 16)
                sp.dma_start(g0[:], i["norms"]).then_inc(loaded, 16)
                sp.dma_start(k.gate[:], i["gate"]).then_inc(loaded, 16)
                sp.dma_start(k.temp[:], i["logt"]).then_inc(loaded, 16)
                sp.dma_start(k.br0[:], i["br0"]).then_inc(loaded, 16)
                sp.wait_ge(loaded, 8 * 16)

            @block.gpsimd
            def _(pool):
                nc.gpsimd.memset(k.ident[:], 0.0).then_inc(pool_made, 1)
                nc.gpsimd.memset(k.tri[:], 1.0).then_inc(pool_made, 1)
                nc.gpsimd.memset(k.mhalf[:], -0.5)
                nc.gpsimd.iota(k.iota_i[:], pattern=[[1, 128]], base=0, channel_multiplier=0).then_inc(pool_made, 1)
                pool.wait_ge(pool_made, 3)
                nc.gpsimd.affine_select(out=k.ident[:], in_=k.ident[:], compare_op=ALU.not_equal, fill=1.0,
                                        base=0, pattern=[[-1, P]], channel_multiplier=1).then_inc(pool_made, 1)
                nc.gpsimd.affine_select(out=k.tri[:], in_=k.tri[:], compare_op=ALU.is_gt, fill=0.0,
                                        base=0, pattern=[[1, P]], channel_multiplier=-1).then_inc(pool_made, 1)
                nc.gpsimd.memset(k.ones_b[:], 1.0)
                nc.gpsimd.memset(k.ones_f[:], 1.0)
                nc.gpsimd.memset(k.zeros[:], 0.0).then_inc(pool_made, 1)

            @block.scalar
            def _(act):
                act.wait_ge(loaded, 8 * 16)
                nc.scalar.activation(k.temp[:, 1:2], k.temp[:, 0:1], ACT.Exp).then_inc(act_made, 1)

            @block.vector
            def _(dve):
                dve.wait_ge(loaded, 8 * 16)
                nc.vector.tensor_scalar(k.w0[:, 0:QKV0], w0[:, 0:QKV0], g0[:, 0:1], None, ALU.mult)
                nc.vector.tensor_scalar(k.w1[:, 0:QKV1], w1[:, 0:QKV1], g0[:, 1:2], None, ALU.mult)
                nc.vector.tensor_copy(k.w0[:, QKV0:PRJ0], w0[:, QKV0:PRJ0])
                nc.vector.tensor_copy(k.w1[:, QKV1:PRJ1], w1[:, QKV1:PRJ1])
                dve.wait_ge(pool_made, 3)
                nc.vector.tensor_copy(k.iota[:], k.iota_i[:]).then_inc(dve_made, 1)
                dve.wait_ge(dve_made, 1)
                nc.vector.tensor_scalar(k.run0[:], k.iota[:, 0:E0], float(REG), None, ALU.mult)
                nc.vector.tensor_scalar(k.run1[:], k.iota[:, 0:E1], float(REG), None, ALU.mult)
                dve.wait_ge(act_made, 1)
                nc.vector.tensor_scalar(k.temp[:, 2:3], k.temp[:, 1:2], -1.0, 80.0, ALU.mult, ALU.add).then_inc(dve_made, 1)
                dve.wait_ge(dve_made, 2)
                nc.vector.tensor_scalar(k.temp[:, 3:4], k.temp[:, 2:3], 0.0, None, ALU.min)


def batch(i, o):
    return 2 * i + o, i + o // 2, o % 2


def bodies(eng, body):
    for o in range(3):
        body(0, o)
    with eng.Fori(1, 6) as i:
        body(i, 1)
        body(i, 2)
    for o in range(13, NB):
        body(0, o)


def flags(i, o):
    static = isinstance(i, int)
    return (not (static and o == 0), *(not (static and o >= NB - n) for n in (1, 2, 3)))


def layer0_attention(nc, k, x_d, base_d, meta_d, xs_d):
    with ExitStack() as ctx:
        sb, ps, sem = allocators(nc, ctx)
        x = sb("a_x", [P, 2, NT, D])
        xn = sb("a_xn", [P, 2, NT, D])
        xs = sb("a_xs", [P, 2, NT, D])
        stats = sb("a_stats", [P, NT, 6])
        mv = sb("a_mv", [P, NT, 2])
        tmp4 = sb("a_tmp4", [P, 3, NT])
        rstd = sb("a_rstd", [P, NT])
        r2 = sb("a_r2", [P, 2, NT])
        r2sq = sb("a_r2sq", [P, NT])
        xnT = sb("a_xnT", [P, L])
        prj = sb("a_prj", [P, NT, PRJ0])
        sq = sb("a_sq", [P, NT * (H0 + KV0), DH0])
        ss = sb("a_ss", [P, NT, H0 + KV0])
        ftmp = sb("a_ftmp", [P, 3, NT, H0 + KV0])
        fac = sb("a_fac", [P, NT, H0 + KV0])
        qn = sb("a_qn", [P, NT, D])
        kn = sb("a_kn", [P, NT, D])
        v = sb("a_v", [P, 2, NT, KV0 * DH0])
        qT = sb("a_qT", [P, 2, L])
        kz = sb("a_kz", [P, 2, H0, L])
        pt = sb("a_pt", [P, 2, H0, L])
        rs = sb("a_rs", [P, L])
        attnT = sb("a_attnT", [P, L])
        bs = sb("a_bs", [P, 2, NT, D])
        lg = sb("a_lg", [P, NT, E0])
        mx8 = sb("a_mx8", [P, NT, 8])
        ix8 = sb("a_ix8", [P, NT, 8], U32)
        ixf = sb("a_ixf", [P, NT, 2])
        oh = sb("a_oh", [P, 2, NT, E0])
        ohb = sb("a_ohb", [P, NT, E0], BF16)
        pos = sb("a_pos", [P, NT, E0])
        ohp = sb("a_ohp", [P, 2, NT, E0])
        slotf = sb("a_slotf", [P, 2, NT])
        dl = sb("a_dl", [P, NT])
        el = sb("a_el", [P, NT])
        ep = sb("a_ep", [P, NT])
        meta = sb("a_meta", [P, 2, 4 * NT], U32)

        ps_t = ps("a_ps_t", [P, L])
        ps_p = ps("a_ps_p", [P, L])
        ps_s = ps("a_ps_s", [P, 2, 2, L])
        ps_v = ps("a_ps_v", [P, L])
        ps_d = ps("a_ps_d", [P, L])
        RT = 288

        x_in = [sem(f"a_x_in{p}") for p in range(2)]
        x_used, stats_ready, rstd_ready, xn_ready = sem("a_x_used"), sem("a_stats"), sem("a_rstd_r"), sem("a_xn_r")
        xT_ps, xT_sb, proj_ps, prj_sb, sq_ready = sem("a_xT_ps"), sem("a_xT_sb"), sem("a_proj"), sem("a_prj_sb"), sem("a_sq_r")
        ss_ready, fac_ready, qkv_ready = sem("a_ss_r"), sem("a_fac_r"), sem("a_qkv_r")
        qT_ps, qT_sb, kT_ps, kT_sb = sem("a_qT_ps"), sem("a_qT_sb"), sem("a_kT_ps"), sem("a_kT_sb")
        oh_ready, rank_ps, rank_used, dl_ready, el_ready, meta_ready = (
            sem("a_oh_r"), sem("a_rank"), sem("a_rank_u"), sem("a_dl_r"), sem("a_el_r"), sem("a_meta_r"))
        scattered = k.scattered0
        meta_out = [sem(f"a_meta_out{p}") for p in range(2)]
        s_ps, exp_done, masked, pv_tile = sem("a_s_ps"), sem("a_exp"), sem("a_masked"), sem("a_pvt")
        norm_done, wo_ps, wo_used = sem("a_norm"), sem("a_wo_ps"), sem("a_wo_used")
        base_out = [sem(f"a_base_out{p}") for p in range(2)]
        dve_ln, dve_qkv, dve_main, pool_ln, pool_fac = (sem(f"a_{n}") for n in ("dve_ln", "dve_qkv", "dve_main", "pool_ln", "pool_fac"))

        with nc.Block() as block:

            @block.vector
            def _(dve):
                nc.vector.memset(kz[:], 0.0).then_inc(x_used, 2)
                nc.vector.memset(ss[:], 0.0)
                nc.vector.memset(mv[:], 0.0).then_inc(exp_done, 2)
                nc.vector.memset(stats[:], 0.0).then_inc(pv_tile, 2 * NT)
                nc.vector.memset(rs[:], 0.0).then_inc(wo_used, 2)

        with nc.Block() as block:

            @block.sync
            def _(sp):
                def load(i, o):
                    b, h, p = batch(i, o)
                    sp.wait_ge(x_used, b + 1)
                    passed(sp, k.passed_sp)
                    sp.dma_start(x[:, p], x_d[bass.ds(b * L, L), :].rearrange("(t p) d -> p t d", p=P)).then_inc(x_in[p], 16)

                def store_meta(i, o):
                    b, h, p = batch(i, o)
                    sp.wait_ge(meta_ready, b + 1)
                    passed(sp, k.passed_sp)
                    sp.dma_start(meta_d[bass.ds(b * P, P), :], meta[:, p]).then_inc(meta_out[p], 16)

                def store_base(i, o):
                    b, h, p = batch(i, o)
                    sp.wait_ge(wo_used, b + 3)
                    passed(sp, k.passed_sp)
                    sp.dma_start(base_d[bass.ds(b * L, L), :].rearrange("(t p) d -> p t d", p=P), bs[:, p]).then_inc(base_out[p], 16)

                def body(i, o):
                    prev, nxt, nxt2, nxt3 = flags(i, o)
                    if prev:
                        store_base(i, o - 1)
                    if nxt3:
                        load(i, o + 3)
                    if nxt:
                        store_meta(i, o + 1)

                for o in range(3):
                    load(0, o)
                store_meta(0, 0)
                bodies(sp, body)
                store_base(0, NB - 1)
                for p in range(2):
                    sp.wait_ge(meta_out[p], 16 * (NB // 2))
                    sp.wait_ge(base_out[p], 16 * (NB // 2))

            @block.vector
            def _(dve):
                ln = Chain(dve, dve_ln, 1, k.passed_dve)
                heads = Chain(dve, dve_qkv, PRO_DVE_A, k.passed_dve)
                main = Chain(dve, dve_main, 1)

                def statistics(i, o):
                    b, h, p = batch(i, o)
                    ln.at(b)
                    dve.wait_ge(x_in[p], 16 * (h + 1))
                    dve.wait_ge(rstd_ready, b)
                    for t in range(NT):
                        last = nc.vector.bn_stats(stats[:, t, :], x[:, p, t, :])
                    ln.link_apart(last)
                    for t in range(NT):
                        last = nc.vector.bn_aggr(mv[:, t, :], stats[:, t, :])
                    last.then_inc(stats_ready, 1)
                    ln.end()

                def normal_rows(i, o):
                    b, h, p = batch(i, o)
                    dve.wait_ge(rstd_ready, b + 1)
                    dve.wait_ge(scattered[p], 16 * 2 * NT * h)
                    for t in range(NT):
                        last = nc.vector.tensor_scalar(xn[:, p, t, :], x[:, p, t, :], mv[:, t, 0:1], rstd[:, t:t + 1],
                                                       ALU.subtract, ALU.mult)
                    last.then_inc(xn_ready, 1)

                def keep_sum(i, o):
                    b, h, p = batch(i, o)
                    dve.wait_ge(xn_ready, b + 1)
                    dve.wait_ge(wo_used, b + 1)
                    nc.vector.scalar_tensor_tensor(xs[:, p], xn[:, p], 2.0, x[:, p], ALU.mult, ALU.add).then_inc(x_used, 1)

                def square_sums(i, o):
                    b, h, p = batch(i, o)
                    dve.wait_ge(sq_ready, b + 1)
                    dve.wait_ge(fac_ready, b)
                    nc.vector.tensor_reduce(ss[:].rearrange("p t h -> p (t h)"), sq[:], AX, ALU.add).then_inc(ss_ready, 1)

                def heads_rows(i, o):
                    b, h, p = batch(i, o)
                    heads.at(b)
                    dve.wait_ge(fac_ready, b + 1)
                    dve.wait_ge(kT_ps, b)
                    dve.wait_ge(pv_tile, NT * (b + 1))
                    nc.vector.tensor_tensor(qn[:].rearrange("p t (h d) -> p t h d", h=H0),
                                            prj[:, :, 0:D].rearrange("p t (h d) -> p t h d", h=H0),
                                            fac[:, :, 0:H0].unsqueeze(3).to_broadcast([P, NT, H0, DH0]), ALU.mult)
                    for r in range(H0 // KV0):
                        nc.vector.tensor_tensor(kn[:].rearrange("p t (g r d) -> p t g r d", g=KV0, d=DH0)[:, :, :, r, :],
                                                prj[:, :, D:D + KV0 * DH0].rearrange("p t (h d) -> p t h d", h=KV0),
                                                fac[:, :, H0:H0 + KV0].unsqueeze(3).to_broadcast([P, NT, KV0, DH0]), ALU.mult)
                    nc.vector.tensor_tensor(v[:, p], prj[:, :, D + KV0 * DH0:QKV0],
                                            r2[:, p].unsqueeze(2).to_broadcast([P, NT, KV0 * DH0]), ALU.mult).then_inc(qkv_ready, 1)

                def choose(i, o):
                    b, h, p = batch(i, o)
                    heads.link_apart(nc.vector.tensor_tensor(lg[:], prj[:, :, QKV0:PRJ0],
                                                             k.br0[:].unsqueeze(1).to_broadcast([P, NT, E0]), ALU.add))
                    for t in range(NT):
                        last = nc.vector.max(mx8[:, t, :], lg[:, t, :])
                    heads.link_apart(last)
                    for t in range(NT):
                        last = nc.vector.max_index(ix8[:, t, :], mx8[:, t, :], lg[:, t, :])
                    dve.wait_ge(el_ready, b)
                    nc.vector.tensor_tensor(dl[:], mx8[:, :, 1], mx8[:, :, 0], ALU.subtract).then_inc(dl_ready, 1)
                    dve.wait_ge(dl_ready, b + 1)
                    heads.link(nc.vector.tensor_copy(ixf[:], ix8[:, :, 0:2]))
                    for c in range(2):
                        last = nc.vector.tensor_tensor(oh[:, c], k.iota[:, 0:E0].unsqueeze(1).to_broadcast([P, NT, E0]),
                                                       ixf[:, :, c].unsqueeze(2).to_broadcast([P, NT, E0]), ALU.is_equal)
                    heads.link(last)
                    nc.vector.tensor_tensor(ohb[:], oh[:, 0], oh[:, 1], ALU.add).then_inc(oh_ready, 1)

                def kz_rows(i, o):
                    b, h, p = batch(i, o)
                    dve.wait_ge(kT_ps, b + 1)
                    for head in range(H0):
                        r = slice(head * DH0, (head + 1) * DH0)
                        last = nc.vector.tensor_copy(kz[r, p, head, :], ps_t[r, :])
                    last.then_inc(kT_sb, 1)

                def slots(i, o):
                    b, h, p = batch(i, o)
                    dve.wait_ge(rank_ps, b + 1)
                    for t in range(NT):
                        nc.vector.tensor_tensor(pos[:, t], ps_p[:, RT + t * E0:RT + (t + 1) * E0], k.run0[:], ALU.add)
                        last = nc.vector.tensor_tensor(k.run0[:], ps_p[:, RT + (NT + t) * E0:RT + (NT + t + 1) * E0],
                                                       k.run0[:], ALU.add)
                        if t < NT - 1:
                            heads.link(last)
                    last.then_inc(rank_used, 1)
                    dve.wait_ge(rank_used, b + 1)
                    for c in range(2):
                        last = nc.vector.tensor_tensor(ohp[:, c], oh[:, c], pos[:], ALU.mult)
                    heads.link(last)
                    heads.link(nc.vector.tensor_reduce(slotf[:].rearrange("p c t -> p (c t)"),
                                                       ohp[:].rearrange("p c t e -> p (c t) e"), AX, ALU.add))
                    dve.wait_ge(el_ready, b + 1)
                    dve.wait_ge(meta_out[p], 16 * h)
                    dve.wait_ge(scattered[p], 16 * 2 * NT * h)
                    heads.link(nc.vector.tensor_scalar(ep[:], el[:], 1.0, None, ALU.add))
                    wts = meta[:, p].bitcast(F32)
                    heads.link(nc.vector.reciprocal(wts[:, 2 * NT:3 * NT], ep[:]))
                    nc.vector.tensor_tensor(wts[:, 3 * NT:4 * NT], el[:], wts[:, 2 * NT:3 * NT], ALU.mult)
                    nc.vector.tensor_copy(meta[:, p, 0:2 * NT], slotf[:].rearrange("p c t -> p (c t)")).then_inc(meta_ready, 1)
                    heads.end()

                def normalise(i, o):
                    b, h, p = batch(i, o)
                    main.at(b)
                    dve.wait_ge(pv_tile, NT * (b + 3))
                    main.link(nc.vector.reciprocal(rs[:], ps_d[:]))
                    dve.wait_ge(wo_ps, b)
                    nc.vector.tensor_tensor(attnT[:], ps_v[:], rs[:], ALU.mult).then_inc(norm_done, 1)
                    main.end()

                def add_output(i, o):
                    b, h, p = batch(i, o)
                    dve.wait_ge(wo_ps, b + 1)
                    dve.wait_ge(base_out[p], 16 * h)
                    nc.vector.scalar_tensor_tensor(bs[:, p].rearrange("p t d -> p (t d)"), ps_t[:], k.gate[:, 0:1],
                                                   xs[:, p].rearrange("p t d -> p (t d)"), ALU.mult, ALU.add).then_inc(wo_used, 1)

                def body(i, o):
                    prev, nxt, nxt2, nxt3 = flags(i, o)
                    if prev:
                        normalise(i, o - 1)
                    if nxt2:
                        statistics(i, o + 2)
                    if prev:
                        add_output(i, o - 1)
                    if nxt:
                        heads_rows(i, o + 1)
                        choose(i, o + 1)
                        kz_rows(i, o + 1)
                        keep_sum(i, o + 1)
                    if nxt2:
                        normal_rows(i, o + 2)
                    if nxt:
                        slots(i, o + 1)
                    if nxt2:
                        square_sums(i, o + 2)

                statistics(0, 0)
                normal_rows(0, 0)
                square_sums(0, 0)
                heads_rows(0, 0)
                choose(0, 0)
                kz_rows(0, 0)
                keep_sum(0, 0)
                statistics(0, 1)
                normal_rows(0, 1)
                slots(0, 0)
                square_sums(0, 1)
                bodies(dve, body)
                normalise(0, NB - 1)
                add_output(0, NB - 1)

            @block.gpsimd
            def _(pool):
                ln = Chain(pool, pool_ln, 6, k.passed_pool)
                fc = Chain(pool, pool_fac, 3, k.passed_pool)

                def norms(i, o):
                    b, h, p = batch(i, o)
                    ln.at(b)
                    pool.wait_ge(stats_ready, b + 1)
                    pool.wait_ge(xn_ready, b)
                    pool.wait_ge(fac_ready, b)
                    if not (isinstance(b, int) and b < 2):
                        pool.wait_ge(qkv_ready, b - 1)
                    passed(pool, k.passed_pool)
                    ln.link(nc.gpsimd.tensor_scalar(tmp4[:, 0], mv[:, :, 1], EPS_LN, None, ALU.add))
                    ln.link(nc.gpsimd.tensor_tensor(rstd[:], tmp4[:, 0], k.mhalf[:, 0:NT], ALU.pow))
                    ln.link(nc.gpsimd.tensor_tensor(tmp4[:, 1], rstd[:], rstd[:], ALU.mult))
                    ln.link_apart(nc.gpsimd.tensor_tensor(tmp4[:, 2], tmp4[:, 1], mv[:, :, 1], ALU.mult))
                    ln.link(nc.gpsimd.tensor_scalar(tmp4[:, 0], tmp4[:, 2], 1e-6, None, ALU.add))
                    ln.link(nc.gpsimd.tensor_tensor(r2[:, p], tmp4[:, 0], k.mhalf[:, 0:NT], ALU.pow))
                    nc.gpsimd.tensor_tensor(r2sq[:], r2[:, p], r2[:, p], ALU.mult).then_inc(rstd_ready, 1)
                    ln.end()

                def factors(i, o):
                    b, h, p = batch(i, o)
                    fc.at(b)
                    pool.wait_ge(ss_ready, b + 1)
                    pool.wait_ge(rstd_ready, b + 1)
                    pool.wait_ge(qkv_ready, b)
                    bc = r2sq[:].unsqueeze(2).to_broadcast([P, NT, H0 + KV0])
                    fc.link_apart(nc.gpsimd.tensor_tensor(ftmp[:, 0], ss[:], bc, ALU.mult))
                    fc.link(nc.gpsimd.tensor_scalar(ftmp[:, 1], ftmp[:, 0], 1e-24, None, ALU.max))
                    fc.link(nc.gpsimd.tensor_tensor(ftmp[:, 2].rearrange("p t h -> p (t h)"),
                                                    ftmp[:, 1].rearrange("p t h -> p (t h)"),
                                                    k.mhalf[:, 0:NT * (H0 + KV0)], ALU.pow))
                    nc.gpsimd.tensor_tensor(fac[:], ftmp[:, 2], r2[:, p].unsqueeze(2).to_broadcast([P, NT, H0 + KV0]),
                                            ALU.mult).then_inc(fac_ready, 1)
                    fc.end()

                def scatter(i, o, c):
                    b, h, p = batch(i, o)
                    if c == 0:
                        pool.wait_ge(meta_ready, b + 1)
                        passed(pool, k.passed_pool)
                    for t in range(NT):
                        nc.gpsimd.indirect_dma_start(
                            xs_d, bass.IndirectOffsetOnAxis(ap=meta[:, p, c * NT + t:c * NT + t + 1], axis=0),
                            xn[:, p, t, :], None).then_inc(scattered[p], 16)

                def mask(i, o, u):
                    b, h, p = batch(i, o)
                    kt, pr = u // 2, u % 2
                    pool.wait_ge(exp_done, 8 * b + u + 3)
                    passed(pool, k.passed_pool)
                    blk = pt[:, kt % 2, 2 * pr:2 * pr + 2, 0:P]
                    nc.gpsimd.affine_select(out=blk, in_=blk, compare_op=ALU.is_ge, fill=0.0, base=0,
                                            pattern=[[0, 2], [1, P]], channel_multiplier=-1).then_inc(masked, 1)

                def body(i, o):
                    prev, nxt, nxt2, nxt3 = flags(i, o)
                    if nxt:
                        factors(i, o + 1)
                    for u in range(3):
                        mask(i, o, u)
                    if nxt2:
                        norms(i, o + 2)
                    for u in range(3, 6):
                        mask(i, o, u)
                    if nxt:
                        scatter(i, o + 1, 0)
                    mask(i, o, 6)
                    mask(i, o, 7)
                    if nxt:
                        scatter(i, o + 1, 1)

                norms(0, 0)
                factors(0, 0)
                norms(0, 1)
                scatter(0, 0, 0)
                scatter(0, 0, 1)
                bodies(pool, body)
                for p in range(2):
                    pool.wait_ge(scattered[p], 16 * 2 * NT * (NB // 2))

            @block.scalar
            def _(act):
                def xT_copy(i, o):
                    b, h, p = batch(i, o)
                    act.wait_ge(xT_ps, b + 1)
                    act.wait_ge(proj_ps, NT * b)
                    nc.scalar.activation(xnT[:], ps_t[:], ACT.Copy).then_inc(xT_sb, 1)

                def prj_copy(i, o, t):
                    b, h, p = batch(i, o)
                    act.wait_ge(proj_ps, NT * b + t + 1)
                    if t == 0:
                        act.wait_ge(qkv_ready, b)
                        act.wait_ge(oh_ready, b)
                    nc.scalar.activation(prj[:, t, :], ps_p[:, 0:PRJ0], ACT.Copy).then_inc(prj_sb, 1)

                def squares(i, o):
                    b, h, p = batch(i, o)
                    act.wait_ge(prj_sb, NT * (b + 1))
                    act.wait_ge(ss_ready, b)
                    nc.scalar.activation(sq[:].rearrange("p (t h) d -> p t (h d)", t=NT), prj[:, :, 0:D + KV0 * DH0],
                                         ACT.Square).then_inc(sq_ready, 1)

                def qT_copy(i, o):
                    b, h, p = batch(i, o)
                    act.wait_ge(qT_ps, b + 1)
                    act.wait_ge(pv_tile, NT * (b + 1))
                    nc.scalar.activation(qT[:, p, :], ps_t[:], ACT.Copy).then_inc(qT_sb, 1)

                def odds(i, o):
                    b, h, p = batch(i, o)
                    act.wait_ge(dl_ready, b + 1)
                    act.wait_ge(meta_ready, b)
                    nc.scalar.activation(el[:], dl[:], ACT.Exp).then_inc(el_ready, 1)

                def exps(i, o, u):
                    b, h, p = batch(i, o)
                    kt, pr = u // 2, u % 2
                    n = L - kt * P
                    act.wait_ge(s_ps, 8 * b + u + 1)
                    act.wait_ge(pv_tile, NT * (b + 1) + kt + 3)
                    nc.scalar.activation(pt[:, kt % 2, 2 * pr:2 * pr + 2, 0:n], ps_s[:, u % 2, :, 0:n], ACT.Exp,
                                         bias=k.temp[:, 3:4], scale=k.temp[:, 1:2]).then_inc(exp_done, 1)

                def body(i, o):
                    prev, nxt, nxt2, nxt3 = flags(i, o)
                    for u in range(4):
                        exps(i, o, u)
                    if nxt:
                        qT_copy(i, o + 1)
                    exps(i, o, 4)
                    if nxt:
                        odds(i, o + 1)
                    exps(i, o, 5)
                    if nxt2:
                        xT_copy(i, o + 2)
                    exps(i, o, 6)
                    if nxt2:
                        prj_copy(i, o + 2, 0)
                    exps(i, o, 7)
                    if nxt2:
                        for t in range(1, NT):
                            prj_copy(i, o + 2, t)
                        squares(i, o + 2)

                def rows(o):
                    xT_copy(0, o)
                    for t in range(NT):
                        prj_copy(0, o, t)
                    squares(0, o)

                rows(0)
                odds(0, 0)
                qT_copy(0, 0)
                rows(1)
                bodies(act, body)

            @block.tensor
            def _(pe):
                def transposes(src, done):
                    for t in range(NT):
                        last = nc.tensor.transpose(ps_t[:, t * P:(t + 1) * P], src[:, t, :], k.ident[:])
                    last.then_inc(done, 1)

                def x_rows(i, o):
                    b, h, p = batch(i, o)
                    pe.wait_ge(xn_ready, b + 1)
                    pe.wait_ge(kT_sb, b)
                    transposes(xn[:, p], xT_ps)

                def project(i, o, t):
                    b, h, p = batch(i, o)
                    pe.wait_ge(xT_sb, b + 1)
                    pe.wait_ge(prj_sb, NT * b + t)
                    if t == 0:
                        pe.wait_ge(rank_used, b)
                    nc.tensor.matmul(ps_p[:, 0:PRJ0], xnT[:, t * P:(t + 1) * P], k.w0[:], start=True, stop=True).then_inc(proj_ps, 1)

                def ranks(i, o):
                    b, h, p = batch(i, o)
                    pe.wait_ge(oh_ready, b + 1)
                    pe.wait_ge(rank_used, b)
                    pe.wait_ge(prj_sb, NT * (b + 1))
                    flat = ohb[:].rearrange("p t e -> p (t e)")
                    nc.tensor.matmul(ps_p[:, RT:RT + NT * E0], k.tri[:], flat, start=True, stop=True)
                    nc.tensor.matmul(ps_p[:, RT + NT * E0:RT + 2 * NT * E0], k.ones_b[:], flat, start=True, stop=True).then_inc(rank_ps, 1)

                def q_columns(i, o):
                    b, h, p = batch(i, o)
                    pe.wait_ge(qkv_ready, b + 1)
                    pe.wait_ge(xT_sb, b + 1)
                    pe.wait_ge(wo_used, b + 1)
                    transposes(qn, qT_ps)

                def k_columns(i, o):
                    b, h, p = batch(i, o)
                    pe.wait_ge(qT_sb, b + 1)
                    transposes(kn, kT_ps)

                def scores(i, o, u):
                    b, h, p = batch(i, o)
                    kt, pr = u // 2, u % 2
                    if u == 0:
                        pe.wait_ge(qT_sb, b + 1)
                        pe.wait_ge(kT_sb, b + 1)
                    pe.wait_ge(exp_done, 8 * b + u + 1)
                    for j in range(2):
                        head = 2 * pr + j
                        last = nc.tensor.matmul(ps_s[:, u % 2, j, 0:L - kt * P], kz[:, p, head, kt * P:(kt + 1) * P],
                                                qT[:, p, kt * P:L], start=True, stop=True)
                    last.then_inc(s_ps, 1)

                def values(i, o, kt):
                    b, h, p = batch(i, o)
                    pe.wait_ge(masked, 8 * b + 2 * kt + 2)
                    if kt == 0:
                        pe.wait_ge(norm_done, b)
                    n = L - kt * P
                    for dst, ones in ((ps_v, False), (ps_d, True)):
                        for head in range(H0):
                            g = head // (H0 // KV0)
                            w = k.ones_f[:, 0:DH0] if ones else v[:, p, kt, g * DH0:(g + 1) * DH0]
                            last = nc.tensor.matmul(dst[head * DH0:(head + 1) * DH0, kt * P:L], w, pt[:, kt % 2, head, 0:n],
                                                    start=kt == 0, stop=kt == NT - 1)
                    last.then_inc(pv_tile, 1)

                def output(i, o):
                    b, h, p = batch(i, o)
                    pe.wait_ge(norm_done, b + 1)
                    if isinstance(b, int) and b >= NB - 2:
                        pe.wait_ge(kT_sb, NB)
                    else:
                        pe.wait_ge(xT_sb, b + 3)
                    for t in range(NT):
                        last = nc.tensor.matmul(ps_t[:, t * P:(t + 1) * P], attnT[:, t * P:(t + 1) * P], k.wo0[:], start=True, stop=True)
                    last.then_inc(wo_ps, 1)

                def body(i, o):
                    prev, nxt, nxt2, nxt3 = flags(i, o)
                    for u in range(3):
                        scores(i, o, u)
                    if prev:
                        output(i, o - 1)
                    values(i, o, 0)
                    scores(i, o, 3)
                    if nxt:
                        q_columns(i, o + 1)
                    scores(i, o, 4)
                    if nxt:
                        k_columns(i, o + 1)
                    values(i, o, 1)
                    if nxt:
                        ranks(i, o + 1)
                    scores(i, o, 5)
                    if nxt2:
                        x_rows(i, o + 2)
                    scores(i, o, 6)
                    if nxt2:
                        project(i, o + 2, 0)
                    values(i, o, 2)
                    scores(i, o, 7)
                    if nxt2:
                        project(i, o + 2, 1)
                        project(i, o + 2, 2)
                    values(i, o, 3)
                    if nxt2:
                        project(i, o + 2, 3)

                def rows(o):
                    x_rows(0, o)
                    for t in range(NT):
                        project(0, o, t)

                rows(0)
                ranks(0, 0)
                q_columns(0, 0)
                k_columns(0, 0)
                rows(1)
                bodies(pe, body)
                output(0, NB - 1)


PRO_DVE_A = 11


class Kept:

    def __init__(self, nc, ctx):
        sb, _, sem = allocators(nc, ctx)
        self.scattered0, self.gathered1, self.scattered1 = ([sem(f"{n}{p}") for p in range(2)] for n in ("scat0_", "gath1_", "scat1_"))
        self.gathered2 = [sem(f"gath2_{q}") for q in range(4)]
        self.passed_dve, self.passed_pool, self.passed_sp = (sem(f"passed_{e}") for e in ("dve", "pool", "sp"))
        self.ident = sb("ident", [P, P])
        self.tri = sb("tri", [P, P], BF16)
        self.ones_b = sb("ones_b", [P, P], BF16)
        self.ones_f = sb("ones_f", [P, DH0])
        self.zeros = sb("zeros", [P, GRP // P * D])
        self.mhalf = sb("mhalf", [P, 32])
        self.iota_i = sb("iota_i", [P, 128], mybir.dt.int32)
        self.iota = sb("iota", [P, 128])
        self.w0 = sb("w0", [P, PRJ0])
        self.w1 = sb("w1", [P, PRJ1])
        self.wo0 = sb("wo0", [P, D])
        self.wo1 = sb("wo1", [P, D])
        self.gate = sb("gate", [P, 1])
        self.temp = sb("temp", [P, 4])
        self.br0 = sb("br0", [P, E0])
        self.run0 = sb("run0", [P, E0])
        self.run1 = sb("run1", [P, E1])
        self.table = sb("table", [P, max(NG0, NG1), 2], mybir.dt.int32)


def group_table(nc, k, run, n_exp, n_grp, n_slots, xs_d, meta_d, name):
    spare = n_exp * REG
    steps = T // GRP
    with ExitStack() as ctx:
        sb, ps, sem = allocators(nc, ctx)
        chain, fill_ready, zero_out = sem(name + "_chain"), sem(name + "_fill"), sem(name + "_zero")
        fill = sb(name + "_fill", [P, n_exp], U32)
        cnt = sb(name + "_cnt", [P, n_exp])
        lim = sb(name + "_lim", [P, steps])
        more = sb(name + "_more", [P, n_exp, steps])
        ng = sb(name + "_ng", [P, n_exp])
        upto = sb(name + "_upto", [P, n_exp])
        before = sb(name + "_before", [P, n_exp])
        row0 = sb(name + "_row0", [P, n_exp])
        ge = sb(name + "_ge", [P, 2, n_grp, n_exp])
        one = sb(name + "_one", [P, n_grp, n_exp])
        pick = sb(name + "_pick", [P, 2, n_grp, n_exp])
        got = sb(name + "_got", [P, 3, n_grp])
        gj = sb(name + "_gj", [P, 4, n_grp])
        mcols = meta_d.shape[1]
        meta = sb(name + "_meta", [P, NB, mcols], U32)
        slot = sb(name + "_slot", [P, NB, n_slots])
        first = sb(name + "_first", [P, n_exp])
        shift = sb(name + "_shift", [P, n_exp])
        step = sb(name + "_step", [P, n_exp])
        above = sb(name + "_above", [P, NB * n_slots, n_exp])
        total = sb(name + "_total", [P, NB * n_slots])
        meta_in, meta_out, meta_new = sem(name + "_meta_in"), sem(name + "_meta_out"), sem(name + "_meta_new")
        with nc.Block() as block:

            @block.sync
            def _(sp):
                sp.dma_start(meta[:], meta_d.rearrange("(b p) c -> p b c", p=P)).then_inc(meta_in, 16)
                sp.wait_ge(fill_ready, 1)
                sp.dma_start(xs_d[spare:spare + GRP, :].rearrange("(p t) d -> p (t d)", p=P), k.zeros[:]).then_inc(zero_out, 16)
                for e in range(n_exp):
                    row = sp.value_load(fill[0:1, e:e + 1], min_val=0, max_val=n_exp * REG - GRP)
                    sp.dma_start(xs_d[bass.ds(row, GRP), :].rearrange("(p t) d -> p (t d)", p=P), k.zeros[:]).then_inc(zero_out, 16)
                sp.wait_ge(meta_new, 1)
                sp.dma_start(meta_d.rearrange("(b p) c -> p b c", p=P), meta[:]).then_inc(meta_out, 16)
                sp.wait_ge(meta_out, 16)
                sp.wait_ge(zero_out, 16 * (n_exp + 1))

            @block.vector
            def _(dve):
                c = Chain(dve, chain, 0, k.passed_dve)
                c.at(0)
                nc.vector.tensor_copy(fill[:], run[:]).then_inc(fill_ready, 1)
                nc.vector.tensor_scalar(row0[:], k.iota[:, 0:n_exp], float(REG), None, ALU.mult)
                c.link(nc.vector.tensor_scalar(lim[:], k.iota[:, 0:steps], float(GRP), None, ALU.mult))
                c.link(nc.vector.tensor_tensor(cnt[:], run[:], row0[:], ALU.subtract))
                c.link(nc.vector.tensor_tensor(more[:], lim[:].unsqueeze(1).to_broadcast([P, n_exp, steps]),
                                               cnt[:].unsqueeze(2).to_broadcast([P, n_exp, steps]), ALU.is_lt))
                c.link(nc.vector.tensor_reduce(ng[:], more[:], AX, ALU.add))
                c.link(nc.vector.tensor_tensor_scan(upto[:], k.ones_f[:, 0:n_exp], ng[:], 0.0, ALU.mult, ALU.add))
                c.link(nc.vector.tensor_tensor(before[:], upto[:], ng[:], ALU.subtract))
                j3 = k.iota[:, 0:n_grp].unsqueeze(2).to_broadcast([P, n_grp, n_exp])
                for n, edge in enumerate((before, upto)):
                    nc.vector.tensor_tensor(ge[:, n], j3, edge[:].unsqueeze(1).to_broadcast([P, n_grp, n_exp]), ALU.is_ge)
                c.link(nc.vector.scalar_tensor_tensor(row0[:], before[:], -float(GRP), row0[:], ALU.mult, ALU.add))
                c.link(nc.vector.tensor_tensor(one[:], ge[:, 0], ge[:, 1], ALU.subtract))
                nc.vector.tensor_tensor(pick[:, 0], one[:], row0[:].unsqueeze(1).to_broadcast([P, n_grp, n_exp]), ALU.mult)
                c.link(nc.vector.tensor_tensor(pick[:, 1], one[:],
                                               k.iota[:, 0:n_exp].unsqueeze(1).to_broadcast([P, n_grp, n_exp]), ALU.mult))
                nc.vector.tensor_reduce(got[:, 0], pick[:, 0], AX, ALU.add)
                nc.vector.tensor_reduce(got[:, 1], pick[:, 1], AX, ALU.add)
                c.link(nc.vector.tensor_reduce(got[:, 2], one[:], AX, ALU.add))
                nc.vector.tensor_scalar(gj[:, 0], k.iota[:, 0:n_grp], float(GRP), None, ALU.mult)
                c.link(nc.vector.tensor_scalar(gj[:, 1], got[:, 2], -float(spare), float(spare), ALU.mult, ALU.add))
                c.link(nc.vector.tensor_tensor(gj[:, 2], got[:, 0], gj[:, 1], ALU.add))
                c.link(nc.vector.tensor_tensor(gj[:, 3], got[:, 2], gj[:, 0], ALU.mult))
                nc.vector.tensor_tensor(k.table[:, 0:n_grp, 0], gj[:, 2], gj[:, 3], ALU.add)
                nc.vector.tensor_scalar(k.table[:, 0:n_grp, 1], got[:, 1], float(P), None, ALU.mult)
                nc.vector.tensor_scalar(first[:], k.iota[:, 0:n_exp], float(REG), None, ALU.mult)
                nc.vector.tensor_scalar(shift[:], row0[:], -1.0, None, ALU.mult)
                dve.wait_ge(meta_in, 16)
                c.link(nc.vector.tensor_copy(slot[:], meta[:, :, 0:n_slots]))
                flat = slot[:].rearrange("p b s -> p (b s)")
                nc.vector.tensor_copy(step[:, 0:1], shift[:, 0:1])
                nc.vector.tensor_tensor(step[:, 1:n_exp], shift[:, 1:n_exp], shift[:, 0:n_exp - 1], ALU.subtract)
                wide = [P, NB * n_slots, n_exp]
                c.link(nc.vector.tensor_tensor(above[:], flat.unsqueeze(2).to_broadcast(wide),
                                               first[:].unsqueeze(1).to_broadcast(wide), ALU.is_ge))
                c.link(nc.vector.tensor_tensor(above[:], above[:], step[:].unsqueeze(1).to_broadcast(wide), ALU.mult))
                c.link(nc.vector.tensor_reduce(total[:], above[:], AX, ALU.add))
                nc.vector.tensor_tensor(meta[:, :, 0:n_slots], slot[:], total[:].rearrange("p (b s) -> p b s", b=NB),
                                        ALU.add).then_inc(meta_new, 1)


def expert_ffn(nc, k, layer, xs_d, ys_d, w_d, name):
    gated = layer == 1
    n_exp, n_grp, chunks = (E1, NG1, FC1) if gated else (E0, NG0, F0 // P)
    wup = (2 if gated else 1) * chunks * P
    wcols = w_d.shape[1]
    GT = GRP // P
    NBUF = 8
    rows = n_exp * REG
    with ExitStack() as ctx:
        sb, ps, sem = allocators(nc, ctx)
        x = sb(name + "_x", [P, NBUF, GT, D])
        w = sb(name + "_w", [P, NBUF, wcols])
        xT = sb(name + "_xT", [P, 2, GRP])
        g = sb(name + "_g", [P, 2, GRP])
        h = sb(name + "_h", [P, 2, chunks, GRP])
        y = sb(name + "_y", [P, NBUF, GT, D])
        ps_x = [ps(f"{name}_ps_x{n}", [P, 512]) for n in range(2)]
        ps_h = [ps(f"{name}_ps_h{n}", [P, 2, GRP]) for n in range(4)]
        ps_y = [ps(f"{name}_ps_y{n}", [P, 512]) for n in range(2)]
        x_in = [sem(f"{name}_x_in{n}") for n in range(NBUF)]
        w_in = [sem(f"{name}_w_in{n}") for n in range(NBUF)]
        y_out = [sem(f"{name}_y_out{n}") for n in range(NBUF)]
        xT_ps, xT_sb, h_ps, g_sb, h_sb, y_ps, y_sb = (sem(f"{name}_{n}") for n in ("xT_ps", "xT_sb", "h_ps", "g_sb", "h_sb", "y_ps", "y_sb"))
        with nc.Block() as block:

            @block.sync
            def _(sp):
                def load(j, i, q):
                    row = sp.value_load(k.table[0:1, bass.ds(j, 1), 0], min_val=0, max_val=rows)
                    wrow = sp.value_load(k.table[0:1, bass.ds(j, 1), 1], min_val=0, max_val=(n_exp - 1) * P)
                    if not (isinstance(i, int) and i == 0):
                        sp.wait_ge(y_sb, j - NBUF + 1)
                    sp.dma_start(x[:, q], xs_d[bass.ds(row, GRP), :].rearrange("(t p) d -> p t d", p=P)).then_inc(x_in[q], 16)
                    sp.dma_start(w[:, q], w_d[bass.ds(wrow, P), :]).then_inc(w_in[q], 16)

                for q in range(NBUF):
                    load(q, 0, q)
                with sp.Fori(1, n_grp // NBUF) as i:
                    for q in range(NBUF):
                        load(NBUF * i + q, i, q)

            def pipeline(eng, rows_of, up, down):
                last = n_grp // NBUF - 1

                def turn(i, q, final=False):
                    j = NBUF * i + q
                    if not (final and q >= NBUF - 2):
                        rows_of(j + 2, i + (q + 2) // NBUF, (q + 2) % NBUF)
                    if not (final and q >= NBUF - 1):
                        up(j + 1, i + (q + 1) // NBUF, (q + 1) % NBUF)
                    down(j, i, q)

                rows_of(0, 0, 0)
                rows_of(1, 0, 1)
                up(0, 0, 0)
                for q in range(NBUF):
                    turn(0, q)
                with eng.Fori(1, last) as i:
                    for q in range(NBUF):
                        turn(i, q)
                for q in range(NBUF):
                    turn(last, q, True)

            @block.tensor
            def _(pe):
                def rows_of(j, i, q):
                    pe.wait_ge(x_in[q], 16 * (i + 1))
                    if not isinstance(j, int) or j >= 2:
                        pe.wait_ge(xT_sb, j - 1)
                    for t in range(GT):
                        last = nc.tensor.transpose(ps_x[q % 2][:, t * P:(t + 1) * P], x[:, q, t, :], k.ident[:])
                    last.then_inc(xT_ps, 1)

                def up(j, i, q):
                    pe.wait_ge(w_in[q], 16 * (i + 1))
                    pe.wait_ge(xT_sb, j + 1)
                    for c in range(chunks):
                        u = (q * chunks + c) % 4
                        if not isinstance(j, int) or chunks * j + c >= 4:
                            pe.wait_ge(h_sb, chunks * j + c - 3)
                        for n in range(2 if gated else 1):
                            col = (n * chunks + c) * P
                            last = nc.tensor.matmul(ps_h[u][:, n, :], w[:, q, col:col + P], xT[:, q % 2, :], start=True, stop=True)
                        last.then_inc(h_ps, 1)

                def down(j, i, q):
                    pe.wait_ge(h_sb, chunks * (j + 1))
                    if not isinstance(j, int) or j >= 2:
                        pe.wait_ge(y_sb, j - 1)
                    for t in range(GT):
                        for c in range(chunks):
                            col = wup + c * D
                            last = nc.tensor.matmul(ps_y[q % 2][:, t * D:(t + 1) * D], h[:, q % 2, c, t * P:(t + 1) * P],
                                                    w[:, q, col:col + D], start=c == 0, stop=c == chunks - 1)
                    last.then_inc(y_ps, 1)

                pipeline(pe, rows_of, up, down)

            @block.scalar
            def _(act):
                def rows_of(j, i, q):
                    pass

                def up(j, i, q):
                    if not isinstance(j, int) or j >= 2:
                        act.wait_ge(y_ps, j - 1)
                    for c in range(chunks):
                        u = (q * chunks + c) % 4
                        act.wait_ge(h_ps, chunks * j + c + 1)
                        if gated:
                            if not isinstance(j, int) or chunks * j + c >= 2:
                                act.wait_ge(h_sb, chunks * j + c - 1)
                            nc.scalar.activation(g[:, u % 2, :], ps_h[u][:, 0, :], ACT.Silu).then_inc(g_sb, 1)
                        else:
                            bias = w[:, q, wup + chunks * D + c:wup + chunks * D + c + 1]
                            act.wait_ge(w_in[q], 16 * (i + 1))
                            nc.scalar.activation(h[:, q % 2, c, :], ps_h[u][:, 0, :], ACT.Gelu, bias=bias).then_inc(h_sb, 1)

                def down(j, i, q):
                    act.wait_ge(y_sb, j + 1)
                    act.dma_start(ys_d[bass.ds(j * GRP, GRP), :].rearrange("(t p) d -> p t d", p=P), y[:, q]).then_inc(y_out[q], 16)

                pipeline(act, rows_of, up, down)
                for q in range(NBUF):
                    act.wait_ge(y_out[q], 16 * (n_grp // NBUF))

            @block.vector
            def _(dve):
                def rows_of(j, i, q):
                    dve.wait_ge(xT_ps, j + 1)
                    if not isinstance(j, int) or j >= 2:
                        dve.wait_ge(h_ps, chunks * (j - 1))
                    nc.vector.tensor_copy(xT[:, q % 2, :], ps_x[q % 2][:, 0:GRP]).then_inc(xT_sb, 1)

                def up(j, i, q):
                    if not gated:
                        return
                    if not isinstance(j, int) or j >= 2:
                        dve.wait_ge(y_ps, j - 1)
                    for c in range(chunks):
                        u = (q * chunks + c) % 4
                        dve.wait_ge(g_sb, chunks * j + c + 1)
                        nc.vector.tensor_tensor(h[:, q % 2, c, :], ps_h[u][:, 1, :], g[:, u % 2, :], ALU.mult).then_inc(h_sb, 1)

                def down(j, i, q):
                    dve.wait_ge(y_ps, j + 1)
                    dve.wait_ge(y_out[q], 16 * i)
                    src = ps_y[q % 2][:, 0:GRP].rearrange("p (t d) -> p t d", t=GT)
                    if gated:
                        nc.vector.tensor_copy(y[:, q], src).then_inc(y_sb, 1)
                    else:
                        b2 = w[:, q, wcols - D:wcols].unsqueeze(1).to_broadcast([P, GT, D])
                        dve.wait_ge(w_in[q], 16 * (i + 1))
                        nc.vector.tensor_tensor(y[:, q], src, b2, ALU.add).then_inc(y_sb, 1)

                pipeline(dve, rows_of, up, down)


TERMS = 9
SROW = TERMS * DH1
KROWS = 96
QSCALE = float(D) ** -0.5
PRO_DVE_C, LN_DVE_C, LN_POOL_C = 9, 1, 8


def layer1_attention(nc, k, ys_d, base_d, meta_d, rf_d, base2_d, meta2_d, xs2_d):
    HL = KV1
    with ExitStack() as ctx:
        sb, ps, sem = allocators(nc, ctx)
        xb = sb("c_xb", [P, 2, NT, D])
        mt = sb("c_mt", [P, 2, 4 * NT], U32)
        gy = sb("c_gy", [P, 2, 2 * NT, D])
        gsum = sb("c_gsum", [P, NT, D])
        x1 = sb("c_x1", [P, 2, NT, D])
        xr = sb("c_xr", [P, 2, NT, D])
        xn = sb("c_xn", [P, 2, NT, D])
        stats = sb("c_stats", [P, NT, 6])
        mv = sb("c_mv", [P, NT, 2])
        tmp4 = sb("c_tmp4", [P, 3, NT])
        rstd = sb("c_rstd", [P, NT])
        r2 = sb("c_r2", [P, 2, NT])
        xnT = sb("c_xnT", [P, L])
        prj = sb("c_prj", [P, NT, PRJ1])
        rf = sb("c_rf", [P, NT, DH1])
        qk = sb("c_qk", [P, NT, 2 * P])
        vp = sb("c_vp", [P, 2, NT, KV1, 32])
        q32 = sb("c_q32", [P, L])
        qr = sb("c_qr", [P, L])
        qp = sb("c_qp", [P, 3, L], BF16)
        k32 = sb("c_k32", [96, L])
        kr = sb("c_kr", [96, L])
        kh = sb("c_kh", [96, L], BF16)
        km = sb("c_km", [96, L], BF16)
        kl = sb("c_kl", [96, L], BF16)
        kb = sb("c_kb", [96, L], BF16)
        qst = sb("c_qst", [KROWS, 2, H1, L], BF16)
        kmx = sb("c_kmx", [KROWS, 2, KV1, L], BF16)
        kex = sb("c_kex", [KROWS, 2, KV1, L], BF16)
        ones2 = sb("c_ones2", [2, 2 * KV1 * L], BF16)
        mx = sb("c_mx", [P, 2, P])
        shb = sb("c_shb", [NT * HL, 2, 2, P], BF16)
        pt = sb("c_pt", [P, 2, HL, L])
        ov = sb("c_ov", [P, L])
        rcp = sb("c_rcp", [P, NT, HL])
        sall = sb("c_sall", [P, NT, D])
        sT = sb("c_sT", [P, L])
        sx = sb("c_sx", [P, NT, D])
        bs = sb("c_bs", [P, 2, NT, D])
        mx8 = sb("c_mx8", [P, NT, 8])
        ix8 = sb("c_ix8", [P, NT, 8], U32)
        ixf = sb("c_ixf", [P, NT])
        oh = sb("c_oh", [P, NT, E1])
        ohb = sb("c_ohb", [P, NT, E1], BF16)
        pos = sb("c_pos", [P, NT, E1])
        ohp = sb("c_ohp", [P, NT, E1])
        slotf = sb("c_slotf", [P, NT])
        sl = sb("c_sl", [P, 2, NT], U32)

        ps_mx = [ps(f"c_ps_mx{n}", [P, L]) for n in range(2)]
        ps_e = ps("c_ps_e", [P, 2, 2, L])
        ps_v = ps("c_ps_v", [P, L])
        ps_j = ps("c_ps_j", [P, L])

        def sems(*names):
            return [sem("c_" + n) for n in names]

        gathered, scattered = k.gathered1, k.scattered1
        base_in, meta_in, k_in, q_in, sh_in, base2_out, meta2_out = (
            [sem(f"c_{n}{p}") for p in range(2)]
            for n in ("base_in", "meta_in", "k_in", "q_in", "sh_in", "base2_out", "meta2_out"))
        (comb_done, stats_ready, rstd_ready, xn_ready, xr_ready, xT_ps, xT_sb, proj_ps, prj_sb, qk_ready, v_ready,
         kT_ps, kT_sb, kr_ready, km_ready, kl_ready, kb_ready, qT_ps, qT_sb, qr_ready, qm_ready, ql_ready) = sems(
            "comb", "stats_r", "rstd_r", "xn_r", "xr_r", "xT_ps", "xT_sb", "proj", "prj_sb", "qk_r", "v_r",
            "kT_ps", "kT_sb", "kr_r", "km_r", "kl_r", "kb_r", "qT_ps", "qT_sb", "qr_r", "qm_r", "ql_r")
        (mx_ps, mx_done, mt_ps, sh_ready, s_ps, exp_done, pv, ov_sb, ot_ps, ot_sb, sT_ps, sT_sb, wo_ps, wo_sb,
         sx_ready, oh_ready, rank_ps, rank_used, slot_ready, const_in) = sems(
            "mx_ps", "mx_done", "mt_ps", "sh_r", "s_ps", "exp", "pv", "ov_sb", "ot_ps", "ot_sb", "sT_ps", "sT_sb",
            "wo_ps", "wo_sb", "sx_r", "oh_r", "rank_ps", "rank_u", "slot_r", "const")
        dve_pro, dve_ln, dve_sh, dve_ot, pool_ln, made = sems("dve_pro", "dve_ln", "dve_sh", "dve_ot", "pool_ln", "made")

        with nc.Block() as block:

            @block.vector
            def _(dve):
                nc.vector.memset(qst[:], 0.0).then_inc(made, 1)
                nc.vector.memset(kmx[:], 0.0).then_inc(exp_done, 2)
                nc.vector.memset(ones2[:], 1.0).then_inc(made, 1)
                nc.vector.memset(mx[:], 0.0).then_inc(mx_done, 2)

            @block.gpsimd
            def _(pool):
                nc.gpsimd.memset(kex[:], 0.0).then_inc(made, 1)
                nc.gpsimd.memset(qk[:], 0.0).then_inc(pv, 2)
                nc.gpsimd.memset(vp[:], 0.0).then_inc(made, 1)
                pool.wait_ge(made, 4)
                nc.gpsimd.memset(vp[:, :, :, :, DH1:DH1 + 1], 1.0)

            @block.sync
            def _(sp):
                sp.dma_start(rf[:], rf_d.rearrange("(t p) d -> p t d", p=P)).then_inc(const_in, 16)
                sp.wait_ge(made, 4)
                sp.dma_start(kex[SROW:SROW + 2], ones2[:]).then_inc(const_in, 16)
                sp.wait_ge(const_in, 32)

        with nc.Block() as block:

            @block.sync
            def _(sp):
                def load(i, o):
                    b, h, p = batch(i, o)
                    if not (isinstance(b, int) and b < 2):
                        sp.wait_ge(comb_done, b - 1)
                        passed(sp, k.passed_sp)
                    sp.dma_start(xb[:, p], base_d[bass.ds(b * L, L), :].rearrange("(t p) d -> p t d", p=P)).then_inc(base_in[p], 16)
                    sp.dma_start(mt[:, p], meta_d[bass.ds(b * P, P), :]).then_inc(meta_in[p], 16)

                def k_stack(i, o):
                    b, h, p = batch(i, o)
                    sp.wait_ge(kl_ready, b + 1)
                    passed(sp, k.passed_sp)
                    sp.wait_ge(kb_ready, b + 1)
                    passed(sp, k.passed_sp)
                    if not (isinstance(b, int) and b < 2):
                        sp.wait_ge(s_ps, 32 * (b - 1))
                        passed(sp, k.passed_sp)
                        sp.wait_ge(mx_ps, 64 * (b - 1))
                        passed(sp, k.passed_sp)
                    for dst in (kmx, kex):
                        for a in range(3):
                            sp.dma_start(dst[3 * DH1 * a:3 * DH1 * (a + 1), p], kb[:]).then_inc(k_in[p], 16)

                def q_stack(i, o):
                    b, h, p = batch(i, o)
                    sp.wait_ge(ql_ready, b + 1)
                    passed(sp, k.passed_sp)
                    for t in range(TERMS):
                        sp.dma_start(qst[DH1 * t:DH1 * (t + 1), p], qp[:, t // 3, :]).then_inc(q_in[p], 16)

                def shift(i, o, g):
                    b, h, p = batch(i, o)
                    sp.wait_ge(sh_ready, 4 * b + g + 1)
                    passed(sp, k.passed_sp)
                    for n in range(2):
                        sp.dma_start(qst[SROW + n:SROW + n + 1, p, HL * g:HL * (g + 1), :],
                                     shb[:, g % 2, n, :]).then_inc(sh_in[g % 2], 16)

                def store_slots(i, o):
                    b, h, p = batch(i, o)
                    sp.wait_ge(slot_ready, b + 1)
                    passed(sp, k.passed_sp)
                    sp.dma_start(meta2_d[bass.ds(b * P, P), :], sl[:, p]).then_inc(meta2_out[p], 16)

                def store_base(i, o):
                    b, h, p = batch(i, o)
                    sp.wait_ge(wo_sb, b + 1)
                    passed(sp, k.passed_sp)
                    sp.dma_start(base2_d[bass.ds(b * L, L), :].rearrange("(t p) d -> p t d", p=P), bs[:, p]).then_inc(base2_out[p], 16)

                def body(i, o):
                    prev, nxt, nxt2, nxt3 = flags(i, o)
                    shift(i, o, 1)
                    if nxt:
                        k_stack(i, o + 1)
                        q_stack(i, o + 1)
                    if nxt3:
                        load(i, o + 3)
                    if prev:
                        store_base(i, o - 1)
                    shift(i, o, 2)
                    if nxt:
                        store_slots(i, o + 1)
                    shift(i, o, 3)
                    if nxt:
                        shift(i, o + 1, 0)

                load(0, 0)
                load(0, 1)
                load(0, 2)
                k_stack(0, 0)
                q_stack(0, 0)
                store_slots(0, 0)
                shift(0, 0, 0)
                bodies(sp, body)
                store_base(0, NB - 1)
                for p in range(2):
                    sp.wait_ge(base2_out[p], 16 * (NB // 2))
                    sp.wait_ge(meta2_out[p], 16 * (NB // 2))

            @block.gpsimd
            def _(pool):
                def gather(i, o):
                    b, h, p = batch(i, o)
                    pool.wait_ge(meta_in[p], 16 * (h + 1))
                    if not (isinstance(b, int) and b < 2):
                        pool.wait_ge(comb_done, b - 1)
                    passed(pool, k.passed_pool)
                    for n in range(2 * NT):
                        nc.gpsimd.indirect_dma_start(
                            gy[:, p, n, :], None, ys_d,
                            bass.IndirectOffsetOnAxis(ap=mt[:, p, n:n + 1], axis=0)).then_inc(gathered[p], 16)

                def combine(ln, i, o):
                    b, h, p = batch(i, o)
                    ln.at(b)
                    pool.wait_ge(gathered[p], 16 * 2 * NT * (h + 1))
                    pool.wait_ge(base_in[p], 16 * (h + 1))
                    w = mt[:, p, 2 * NT:4 * NT].bitcast(F32).unsqueeze(2).to_broadcast([P, 2 * NT, D])
                    ln.link(nc.gpsimd.tensor_tensor(gy[:, p], gy[:, p], w, ALU.mult))
                    ln.link(nc.gpsimd.tensor_tensor(gsum[:], gy[:, p, 0:NT, :], gy[:, p, NT:2 * NT, :], ALU.add))
                    if not (isinstance(b, int) and b < 2):
                        pool.wait_ge(xr_ready, b - 1)
                    nc.gpsimd.tensor_tensor(x1[:, p], gsum[:], xb[:, p], ALU.add).then_inc(comb_done, 1)

                def norms(ln, i, o):
                    b, h, p = batch(i, o)
                    pool.wait_ge(stats_ready, b + 1)
                    pool.wait_ge(xn_ready, b)
                    if not (isinstance(b, int) and b < 2):
                        pool.wait_ge(prj_sb, NT * (b - 1))
                    passed(pool, k.passed_pool)
                    ln.link(nc.gpsimd.tensor_scalar(tmp4[:, 0], mv[:, :, 1], EPS_LN, None, ALU.add))
                    ln.link(nc.gpsimd.tensor_tensor(rstd[:], tmp4[:, 0], k.mhalf[:, 0:NT], ALU.pow))
                    ln.link(nc.gpsimd.tensor_tensor(tmp4[:, 1], rstd[:], rstd[:], ALU.mult))
                    ln.link_apart(nc.gpsimd.tensor_tensor(tmp4[:, 2], tmp4[:, 1], mv[:, :, 1], ALU.mult))
                    ln.link(nc.gpsimd.tensor_scalar(tmp4[:, 0], tmp4[:, 2], float(np.finfo(np.float32).eps), None, ALU.add))
                    ln.link(nc.gpsimd.tensor_tensor(r2[:, p], tmp4[:, 0], k.mhalf[:, 0:NT], ALU.pow))
                    nc.gpsimd.tensor_tensor(tmp4[:, 1], r2[:, p], r2[:, p], ALU.mult).then_inc(rstd_ready, 1)

                    ln.end()

                def rotate(i, o):
                    b, h, p = batch(i, o)
                    pool.wait_ge(prj_sb, NT * (b + 1))
                    pool.wait_ge(qT_ps, b)
                    qd = prj[:, :, 0:D].rearrange("p t (d h) -> p t d h", d=DH1)
                    nc.gpsimd.tensor_tensor(qk[:, :, 0:D].rearrange("p t (d h) -> p t d h", d=DH1), qd,
                                            rf[:].unsqueeze(3).to_broadcast([P, NT, DH1, H1]), ALU.mult)
                    kd = prj[:, :, D:D + 32].rearrange("p t (d h) -> p t d h", d=DH1)
                    for r in range(3):
                        last = nc.gpsimd.tensor_tensor(
                            qk[:, :, D + 32 * r:D + 32 * (r + 1)].rearrange("p t (d h) -> p t d h", d=DH1), kd,
                            rf[:].unsqueeze(3).to_broadcast([P, NT, DH1, KV1]), ALU.mult)
                    last.then_inc(qk_ready, 1)

                def v_rows(i, o):
                    b, h, p = batch(i, o)
                    pool.wait_ge(prj_sb, NT * (b + 1))
                    pool.wait_ge(pv, 16 * (b - 1) + 2 if not (isinstance(b, int) and b < 1) else 2)
                    passed(pool, k.passed_pool)
                    nc.gpsimd.tensor_copy(vp[:, p, :, :, 0:DH1],
                                          prj[:, :, D + 32:QKV1].rearrange("p t (h d) -> p t h d", h=KV1)).then_inc(v_ready, 1)

                def parts(i, o):
                    b, h, p = batch(i, o)
                    pool.wait_ge(kT_sb, b + 1)
                    pool.wait_ge(km_ready, b)
                    nc.gpsimd.tensor_tensor(kr[:], k32[:], kh[:], ALU.subtract).then_inc(kr_ready, 1)
                    pool.wait_ge(qT_sb, b + 1)
                    pool.wait_ge(qm_ready, b)
                    nc.gpsimd.tensor_tensor(qr[:], q32[:], qp[:, 0, :], ALU.subtract).then_inc(qr_ready, 1)
                    pool.wait_ge(km_ready, b + 1)
                    pool.wait_ge(kb_ready, b)
                    nc.gpsimd.tensor_tensor(kl[:], kr[:], km[:], ALU.subtract).then_inc(kl_ready, 1)
                    pool.wait_ge(qm_ready, b + 1)
                    nc.gpsimd.tensor_tensor(qp[:, 2, :], qr[:], qp[:, 1, :], ALU.subtract).then_inc(ql_ready, 1)

                def residual(i, o):
                    b, h, p = batch(i, o)
                    pool.wait_ge(ot_sb, 4 * (b + 1))
                    pool.wait_ge(xr_ready, b + 1)
                    pool.wait_ge(wo_sb, b)
                    nc.gpsimd.tensor_tensor(sx[:], sall[:], xr[:, p], ALU.add).then_inc(sx_ready, 1)

                def scatter(i, o):
                    b, h, p = batch(i, o)
                    pool.wait_ge(slot_ready, b + 1)
                    passed(pool, k.passed_pool)
                    for t in range(NT):
                        nc.gpsimd.indirect_dma_start(
                            xs2_d, bass.IndirectOffsetOnAxis(ap=sl[:, p, t:t + 1], axis=0),
                            xn[:, p, t, :], None).then_inc(scattered[p], 16)

                ln = Chain(pool, pool_ln, LN_POOL_C, k.passed_pool)

                def body(i, o):
                    prev, nxt, nxt2, nxt3 = flags(i, o)
                    if nxt:
                        parts(i, o + 1)
                        v_rows(i, o + 1)
                    if prev:
                        residual(i, o - 1)
                    if nxt2:
                        combine(ln, i, o + 2)
                        norms(ln, i, o + 2)
                    if nxt:
                        scatter(i, o + 1)
                    if nxt3:
                        gather(i, o + 3)
                    if nxt2:
                        rotate(i, o + 2)

                for o in range(2):
                    gather(0, o)
                for o in range(2):
                    combine(ln, 0, o)
                    norms(ln, 0, o)
                rotate(0, 0)
                v_rows(0, 0)
                parts(0, 0)
                rotate(0, 1)
                scatter(0, 0)
                gather(0, 2)
                bodies(pool, body)
                residual(0, NB - 1)
                for p in range(2):
                    pool.wait_ge(scattered[p], 16 * NT * (NB // 2))

            @block.scalar
            def _(act):
                def exps(i, o, s, half):
                    b, h, p = batch(i, o)
                    gs = 16 * b + s
                    act.wait_ge(s_ps, 2 * gs + half + 1)
                    if half == 0:
                        act.wait_ge(pv, gs + 1)
                    nc.scalar.activation(pt[:, s % 2, 2 * half:2 * half + 2, :], ps_e[:, half], ACT.Exp,
                                         scale=QSCALE).then_inc(exp_done, 1)

                def ov_copy(i, o, g):
                    b, h, p = batch(i, o)
                    act.wait_ge(pv, 4 * (4 * b + g + 1) + 2)
                    act.wait_ge(ot_ps, 4 * b + g)
                    nc.scalar.activation(ov[:], ps_v[:], ACT.Copy).then_inc(ov_sb, 1)

                def xT_copy(i, o):
                    b, h, p = batch(i, o)
                    act.wait_ge(xT_ps, b + 1)
                    act.wait_ge(proj_ps, 2 * b)
                    nc.scalar.activation(xnT[:], ps_j[:], ACT.Copy).then_inc(xT_sb, 1)

                def prj_copy(i, o, pair):
                    b, h, p = batch(i, o)
                    act.wait_ge(proj_ps, 2 * b + pair + 1)
                    if pair == 0:
                        act.wait_ge(rstd_ready, b + 1)
                        act.wait_ge(v_ready, b)
                        act.wait_ge(oh_ready, b)
                    for t in (2 * pair, 2 * pair + 1):
                        nc.scalar.activation(prj[:, t, :], ps_j[:, t % 2 * PRJ1:(t % 2 + 1) * PRJ1], ACT.Copy,
                                             scale=r2[:, p, t:t + 1]).then_inc(prj_sb, 1)

                def kT_copy(i, o):
                    b, h, p = batch(i, o)
                    act.wait_ge(kT_ps, b + 1)
                    act.wait_ge(kb_ready, b)
                    act.wait_ge(kr_ready, b)
                    nc.scalar.activation(kh[:], ps_j[0:96, :], ACT.Copy)
                    nc.scalar.activation(k32[:], ps_j[0:96, :], ACT.Copy).then_inc(kT_sb, 1)

                def qT_copy(i, o):
                    b, h, p = batch(i, o)
                    _, hq, pq = batch(i, o + 1)
                    act.wait_ge(qT_ps, b + 1)
                    act.wait_ge(qr_ready, b)
                    if not (isinstance(b, int) and b < 1):
                        act.wait_ge(q_in[pq], 16 * TERMS * hq)
                    nc.scalar.activation(qp[:, 0, :], ps_j[:], ACT.Copy)
                    nc.scalar.activation(q32[:], ps_j[:], ACT.Copy).then_inc(qT_sb, 1)

                def sT_copy(i, o):
                    b, h, p = batch(i, o)
                    act.wait_ge(sT_ps, b + 1)
                    act.wait_ge(wo_ps, b)
                    nc.scalar.activation(sT[:], ps_j[:], ACT.Copy).then_inc(sT_sb, 1)

                def body(i, o):
                    prev, nxt, nxt2, nxt3 = flags(i, o)
                    for s in range(16):
                        exps(i, o, s, 0)
                        if s == 11 and nxt2:
                            xT_copy(i, o + 2)
                        if s == 12 and nxt2:
                            prj_copy(i, o + 2, 1)
                        if s == 15 and nxt2:
                            kT_copy(i, o + 2)
                        if s == 3 and prev:
                            sT_copy(i, o - 1)
                        if s == 0 and prev:
                            ov_copy(i, o - 1, 3)
                        if s > 0 and s % 4 == 0:
                            ov_copy(i, o, s // 4 - 1)
                        exps(i, o, s, 1)
                        if s == 11 and nxt2:
                            prj_copy(i, o + 2, 0)
                        if s == 15 and nxt2:
                            qT_copy(i, o + 2)

                for o in range(2):
                    xT_copy(0, o)
                    prj_copy(0, o, 0)
                    prj_copy(0, o, 1)
                    kT_copy(0, o)
                    qT_copy(0, o)
                bodies(act, body)
                ov_copy(0, NB - 1, 3)
                sT_copy(0, NB - 1)

            @block.vector
            def _(dve):
                def row_max(i, o, n):
                    b, h, p = batch(i, o)
                    g = n // 16
                    if n % 16 == 0 and not (isinstance(b, int) and 4 * b + g < 2):
                        dve.wait_ge(mt_ps, 4 * b + g - 1)
                    dve.wait_ge(mx_ps, 64 * b + n + 1)
                    nc.vector.tensor_reduce(mx[:, g % 2, n % 16:n % 16 + 1], ps_mx[n % 2][:], AX, ALU.max).then_inc(mx_done, 1)

                def shifts(i, o, g):
                    b, h, p = batch(i, o)
                    dve.wait_ge(mt_ps, 4 * b + g + 1)
                    if not (isinstance(b, int) and 4 * b + g < 2):
                        dve.wait_ge(sh_in[g % 2], 32 * (2 * b + g // 2))
                    src = ps_j[0:NT * HL, 0:P]
                    nc.vector.tensor_scalar(shb[:, g % 2, 0, :], src, -1.0, None, ALU.mult).then_inc(dve_sh, 1)
                    dve.wait_ge(dve_sh, 4 * b + g + 1)
                    nc.vector.scalar_tensor_tensor(shb[:, g % 2, 1, :], src, -1.0, shb[:, g % 2, 0, :],
                                                   ALU.mult, ALU.subtract).then_inc(sh_ready, 1)

                def normalise(i, o, g):
                    b, h, p = batch(i, o)
                    dve.wait_ge(ot_ps, 4 * b + g + 1)
                    src = ps_j[:].rearrange("p (t h c) -> p t h c", t=NT, h=HL)
                    if g == 0:
                        dve.wait_ge(sx_ready, b)
                        dve.wait_ge(sT_ps, b)
                    nc.vector.reciprocal(rcp[:], src[:, :, :, DH1]).then_inc(dve_ot, 1)
                    dve.wait_ge(dve_ot, 4 * b + g + 1)
                    nc.vector.tensor_tensor(sall[:, :, 32 * g:32 * (g + 1)].rearrange("p t (h d) -> p t h d", h=HL),
                                            src[:, :, :, 0:DH1], rcp[:].unsqueeze(3).to_broadcast([P, NT, HL, DH1]),
                                            ALU.mult).then_inc(ot_sb, 1)

                def output(i, o):
                    b, h, p = batch(i, o)
                    dve.wait_ge(wo_ps, b + 1)
                    dve.wait_ge(sx_ready, b + 1)
                    dve.wait_ge(base2_out[p], 16 * h)
                    nc.vector.tensor_tensor(bs[:, p].rearrange("p t d -> p (t d)"), ps_j[:],
                                            sx[:].rearrange("p t d -> p (t d)"), ALU.add).then_inc(wo_sb, 1)

                def keep_x1(i, o):
                    b, h, p = batch(i, o)
                    if not (isinstance(b, int) and b < 2):
                        dve.wait_ge(sx_ready, b - 1)
                    dve.wait_ge(comb_done, b + 1)
                    nc.vector.tensor_copy(xr[:, p], x1[:, p]).then_inc(xr_ready, 1)

                def k_mid(i, o):
                    b, h, p = batch(i, o)
                    dve.wait_ge(kr_ready, b + 1)
                    dve.wait_ge(kl_ready, b)
                    nc.vector.tensor_copy(km[:], kr[:]).then_inc(km_ready, 1)

                def k_join(i, o):
                    b, h, p = batch(i, o)
                    _, hq, pq = batch(i, o + 1)
                    if not (isinstance(b, int) and b < 1):
                        dve.wait_ge(k_in[pq], 16 * 6 * hq)
                    dve.wait_ge(km_ready, b + 1)
                    dve.wait_ge(kT_sb, b + 1)
                    dve.wait_ge(kl_ready, b + 1)
                    for n, part in enumerate((kh, km, kl)):
                        rows = slice(32 * n, 32 * (n + 1))
                        last = nc.vector.tensor_copy(kb[rows], part[rows])
                    last.then_inc(kb_ready, 1)

                def q_mid(i, o):
                    b, h, p = batch(i, o)
                    dve.wait_ge(qr_ready, b + 1)
                    nc.vector.tensor_copy(qp[:, 1, :], qr[:]).then_inc(qm_ready, 1)

                pro = Chain(dve, dve_pro, PRO_DVE_C, k.passed_dve)

                def choose(i, o):
                    b, h, p = batch(i, o)
                    pro.at(b)
                    dve.wait_ge(prj_sb, NT * (b + 1))
                    passed(dve, k.passed_dve)
                    lg = prj[:, :, QKV1:PRJ1]
                    for t in range(NT):
                        last = nc.vector.max(mx8[:, t, :], lg[:, t, :])
                    pro.link_apart(last)
                    for t in range(NT):
                        last = nc.vector.max_index(ix8[:, t, :], mx8[:, t, :], lg[:, t, :])
                    pro.link(last)
                    pro.link(nc.vector.tensor_copy(ixf[:], ix8[:, :, 0]))
                    pro.link(nc.vector.tensor_tensor(oh[:], k.iota[:, 0:E1].unsqueeze(1).to_broadcast([P, NT, E1]),
                                                     ixf[:].unsqueeze(2).to_broadcast([P, NT, E1]), ALU.is_equal))
                    dve.wait_ge(rank_ps, b)
                    nc.vector.tensor_copy(ohb[:], oh[:]).then_inc(oh_ready, 1)

                def slots(i, o):
                    b, h, p = batch(i, o)
                    dve.wait_ge(rank_ps, b + 1)
                    for t in range(NT):
                        nc.vector.tensor_tensor(pos[:, t], ps_j[:, t * E1:(t + 1) * E1], k.run1[:], ALU.add)
                        last = nc.vector.tensor_tensor(k.run1[:], ps_j[:, (NT + t) * E1:(NT + t + 1) * E1], k.run1[:], ALU.add)
                        if t < NT - 1:
                            pro.link(last)
                    last.then_inc(rank_used, 1)
                    dve.wait_ge(rank_used, b + 1)
                    pro.link(nc.vector.tensor_tensor(ohp[:], oh[:], pos[:], ALU.mult))
                    pro.link(nc.vector.tensor_reduce(slotf[:], ohp[:], AX, ALU.add))
                    dve.wait_ge(scattered[p], 16 * NT * h)
                    dve.wait_ge(meta2_out[p], 16 * h)
                    nc.vector.tensor_copy(sl[:, p], slotf[:]).then_inc(slot_ready, 1)
                    pro.end()

                ln = Chain(dve, dve_ln, LN_DVE_C, k.passed_dve)

                def statistics(i, o):
                    b, h, p = batch(i, o)
                    ln.at(b)
                    dve.wait_ge(comb_done, b + 1)
                    dve.wait_ge(rstd_ready, b)
                    for t in range(NT):
                        last = nc.vector.bn_stats(stats[:, t, :], x1[:, p, t, :])
                    ln.link_apart(last)
                    for t in range(NT):
                        last = nc.vector.bn_aggr(mv[:, t, :], stats[:, t, :])
                    last.then_inc(stats_ready, 1)
                    ln.end()

                def normal_rows(i, o):
                    b, h, p = batch(i, o)
                    dve.wait_ge(rstd_ready, b + 1)
                    dve.wait_ge(scattered[p], 16 * NT * h)
                    for t in range(NT):
                        last = nc.vector.tensor_scalar(xn[:, p, t, :], x1[:, p, t, :], mv[:, t, 0:1], rstd[:, t:t + 1],
                                                       ALU.subtract, ALU.mult)
                    last.then_inc(xn_ready, 1)

                def maxima(i, o, s, first):
                    m = s + 7
                    if m >= 16 and not flags(i, o)[1]:
                        return
                    for j in (0, 1) if first else (2, 3):
                        row_max(i, o + m // 16, 4 * (m % 16) + j)

                def body(i, o):
                    prev, nxt, nxt2, nxt3 = flags(i, o)
                    for s in range(16):
                        maxima(i, o, s, True)
                        if s in (1, 5, 9):
                            shifts(i, o, s // 4 + 1)
                        if s == 2 and nxt:
                            choose(i, o + 1)
                        if s == 4 and prev:
                            output(i, o - 1)
                        if s == 8 and nxt:
                            keep_x1(i, o + 1)
                        if s == 6 and nxt2:
                            statistics(i, o + 2)
                        if s == 13 and nxt:
                            shifts(i, o + 1, 0)
                        maxima(i, o, s, False)
                        if s == 0 and nxt:
                            k_mid(i, o + 1)
                            q_mid(i, o + 1)
                        if s == 1 and prev:
                            normalise(i, o - 1, 3)
                        if s == 2 and nxt:
                            k_join(i, o + 1)
                        if s == 6 and nxt:
                            slots(i, o + 1)
                        if s in (5, 9, 13):
                            normalise(i, o, s // 4 - 1)
                        if s == 9 and nxt2:
                            normal_rows(i, o + 2)

                for o in range(2):
                    statistics(0, o)
                    normal_rows(0, o)
                choose(0, 0)
                k_mid(0, 0)
                q_mid(0, 0)
                k_join(0, 0)
                keep_x1(0, 0)
                slots(0, 0)
                for m in range(7):
                    for j in range(4):
                        row_max(0, 0, 4 * m + j)
                    if m == 3:
                        shifts(0, 0, 0)
                bodies(dve, body)
                normalise(0, NB - 1, 3)
                output(0, NB - 1)

            @block.tensor
            def _(pe):
                def scores(i, o, s, half):
                    b, h, p = batch(i, o)
                    g, kt = s // 4, s % 4
                    if kt == 0 and half == 0:
                        pe.wait_ge(sh_in[g % 2], 32 * (2 * b + g // 2 + 1))
                    pe.wait_ge(exp_done, 2 * (16 * b + s) + half + 1)
                    for j in range(2):
                        hl = 2 * half + j
                        last = nc.tensor.matmul(ps_e[:, half, j, :], kex[:, p, hl, kt * P:(kt + 1) * P],
                                                qst[:, p, HL * g + hl, :], start=True, stop=True)
                    last.then_inc(s_ps, 1)

                def values(i, o, s):
                    b, h, p = batch(i, o)
                    gs = 16 * b + s
                    kt = s % 4
                    pe.wait_ge(exp_done, 2 * gs + 4)
                    if kt == 0:
                        pe.wait_ge(ov_sb, 4 * b + s // 4)
                    if s == 0:
                        pe.wait_ge(v_ready, b + 1)
                    for hl in range(HL):
                        last = nc.tensor.matmul(ps_v[32 * hl:32 * (hl + 1), :], vp[:, p, kt, hl, :], pt[:, s % 2, hl, :],
                                                start=kt == 0, stop=kt == NT - 1)
                    last.then_inc(pv, 1)

                def score_max(i, o, n):
                    b, h, p = batch(i, o)
                    g, hl, qt = n // 16, n // 4 % 4, n % 4
                    if n == 0:
                        pe.wait_ge(k_in[p], 16 * 6 * (h + 1))
                        pe.wait_ge(q_in[p], 16 * TERMS * (h + 1))
                    pe.wait_ge(mx_done, 64 * b + n + 1)
                    nc.tensor.matmul(ps_mx[n % 2][:], qst[:, p, HL * g + hl, qt * P:(qt + 1) * P], kmx[:, p, hl, :],
                                     start=True, stop=True).then_inc(mx_ps, 1)

                def maximum(i, o, s, j):
                    m = s + 7
                    if m < 16 or flags(i, o)[1]:
                        score_max(i, o + m // 16, 4 * (m % 16) + j)

                def transposes(src, done):
                    for t in range(NT):
                        last = nc.tensor.transpose(ps_j[:, t * P:(t + 1) * P], src(t), k.ident[:])
                    last.then_inc(done, 1)

                def x_rows(free, i, o):
                    b, h, p = batch(i, o)
                    pe.wait_ge(*free)
                    pe.wait_ge(xn_ready, b + 1)
                    transposes(lambda t: xn[:, p, t, :], xT_ps)
                    return xT_sb, b + 1

                def project(free, i, o, pair):
                    b, h, p = batch(i, o)
                    pe.wait_ge(*free)
                    pe.wait_ge(xT_sb, b + 1)
                    for t in (2 * pair, 2 * pair + 1):
                        last = nc.tensor.matmul(ps_j[:, t % 2 * PRJ1:(t % 2 + 1) * PRJ1], xnT[:, t * P:(t + 1) * P], k.w1[:],
                                                start=True, stop=True)
                    last.then_inc(proj_ps, 1)
                    return prj_sb, NT * b + 2 * (pair + 1)

                def k_columns(free, i, o):
                    b, h, p = batch(i, o)
                    pe.wait_ge(*free)
                    pe.wait_ge(qk_ready, b + 1)
                    transposes(lambda t: qk[:, t, P:2 * P], kT_ps)
                    return kT_sb, b + 1

                def q_columns(free, i, o):
                    b, h, p = batch(i, o)
                    pe.wait_ge(*free)
                    pe.wait_ge(qk_ready, b + 1)
                    transposes(lambda t: qk[:, t, 0:P], qT_ps)
                    return qT_sb, b + 1

                def ranks(free, i, o):
                    b, h, p = batch(i, o)
                    pe.wait_ge(*free)
                    pe.wait_ge(oh_ready, b + 1)
                    flat = ohb[:].rearrange("p t e -> p (t e)")
                    nc.tensor.matmul(ps_j[:, 0:NT * E1], k.tri[:], flat, start=True, stop=True)
                    nc.tensor.matmul(ps_j[:, NT * E1:2 * NT * E1], k.ones_b[:], flat, start=True, stop=True).then_inc(rank_ps, 1)
                    return rank_used, b + 1

                def max_columns(free, i, o, g):
                    b, h, p = batch(i, o)
                    pe.wait_ge(*free)
                    pe.wait_ge(mx_done, 16 * (4 * b + g + 1) + 2)
                    nc.tensor.transpose(ps_j[:, 0:P], mx[:, g % 2, :], k.ident[:]).then_inc(mt_ps, 1)
                    return sh_ready, 4 * b + g + 1

                def token_rows(free, i, o, g):
                    b, h, p = batch(i, o)
                    pe.wait_ge(*free)
                    pe.wait_ge(ov_sb, 4 * b + g + 1)
                    transposes(lambda t: ov[:, t * P:(t + 1) * P], ot_ps)
                    return ot_sb, 4 * b + g + 1

                def s_rows(free, i, o):
                    b, h, p = batch(i, o)
                    pe.wait_ge(*free)
                    pe.wait_ge(ot_sb, 4 * (b + 1))
                    transposes(lambda t: sall[:, t, :], sT_ps)
                    return sT_sb, b + 1

                def s_project(free, i, o):
                    b, h, p = batch(i, o)
                    pe.wait_ge(*free)
                    pe.wait_ge(sT_sb, b + 1)
                    for t in range(NT):
                        last = nc.tensor.matmul(ps_j[:, t * P:(t + 1) * P], sT[:, t * P:(t + 1) * P], k.wo1[:],
                                                start=True, stop=True)
                    last.then_inc(wo_ps, 1)
                    return wo_sb, b + 1

                def body(i, o):
                    prev, nxt, nxt2, nxt3 = flags(i, o)
                    b = batch(i, o)[0]
                    free = (qT_sb, b + 2) if nxt else (ot_sb, 4 * b - 1)
                    for s in range(16):
                        maximum(i, o, s, 0)
                        scores(i, o, s, 0)
                        maximum(i, o, s, 1)
                        if s in (1, 5, 9):
                            free = max_columns(free, i, o, s // 4 + 1)
                        if s == 3 and prev:
                            free = s_rows(free, i, o - 1)
                        if s == 6 and nxt:
                            free = ranks(free, i, o + 1)
                        if s == 11 and nxt2:
                            free = x_rows(free, i, o + 2)
                        if s == 12 and nxt2:
                            free = project(free, i, o + 2, 1)
                        if s == 13 and nxt:
                            free = max_columns(free, i, o + 1, 0)
                        if s == 15 and nxt2:
                            free = k_columns(free, i, o + 2)
                        if s > 0:
                            values(i, o, s - 1)
                        elif prev:
                            values(i, o - 1, 15)
                        maximum(i, o, s, 2)
                        scores(i, o, s, 1)
                        maximum(i, o, s, 3)
                        if s == 1 and prev:
                            free = token_rows(free, i, o - 1, 3)
                        if s == 3 and prev:
                            free = s_project(free, i, o - 1)
                        if s in (5, 9, 13):
                            free = token_rows(free, i, o, s // 4 - 1)
                        if s == 11 and nxt2:
                            free = project(free, i, o + 2, 0)
                        if s == 15 and nxt2:
                            free = q_columns(free, i, o + 2)

                def columns(free, o):
                    free = x_rows(free, 0, o)
                    free = project(free, 0, o, 0)
                    free = project(free, 0, o, 1)
                    free = k_columns(free, 0, o)
                    return q_columns(free, 0, o)

                free = columns((xn_ready, 1), 0)
                free = ranks(free, 0, 0)
                for m in range(7):
                    for j in range(4):
                        score_max(0, 0, 4 * m + j)
                    if m == 3:
                        free = max_columns(free, 0, 0, 0)
                columns(free, 1)
                bodies(pe, body)
                values(0, NB - 1, 15)
                free = token_rows((ot_sb, 4 * NB - 1), 0, NB - 1, 3)
                free = s_rows(free, 0, NB - 1)
                s_project(free, 0, NB - 1)


def output_rows(nc, k, ys2_d, base2_d, meta2_d, out_d):
    NBUF = 4
    with ExitStack() as ctx:
        sb, ps, sem = allocators(nc, ctx)
        xb = sb("o_xb", [P, NBUF, NT, D])
        sl = sb("o_sl", [P, NBUF, NT], U32)
        gy = sb("o_gy", [P, NBUF, NT, D])
        ob = sb("o_ob", [P, NBUF, NT, D])
        gathered = k.gathered2
        base_in, slot_in, stored = ([sem(f"o_{n}{q}") for q in range(NBUF)] for n in ("base_in", "slot_in", "stored"))
        added = sem("o_added")
        with nc.Block() as block:

            @block.sync
            def _(sp):
                def load(b, i, q):
                    if not isinstance(i, int):
                        sp.wait_ge(added, b - NBUF + 1)
                        passed(sp, k.passed_sp)
                    sp.dma_start(sl[:, q], meta2_d[bass.ds(b * P, P), :]).then_inc(slot_in[q], 16)
                    sp.dma_start(xb[:, q], base2_d[bass.ds(b * L, L), :].rearrange("(t p) d -> p t d", p=P)).then_inc(base_in[q], 16)

                for q in range(NBUF):
                    load(q, 0, q)
                with sp.Fori(1, NB // NBUF) as i:
                    for q in range(NBUF):
                        load(NBUF * i + q, i, q)

            @block.gpsimd
            def _(pool):
                with pool.Fori(0, NB // NBUF) as i:
                    for q in range(NBUF):
                        pool.wait_ge(slot_in[q], 16 * (i + 1))
                        pool.wait_ge(added, NBUF * i)
                        passed(pool, k.passed_pool)
                        for t in range(NT):
                            nc.gpsimd.indirect_dma_start(
                                gy[:, q, t, :], None, ys2_d,
                                bass.IndirectOffsetOnAxis(ap=sl[:, q, t:t + 1], axis=0)).then_inc(gathered[q], 16)

            @block.vector
            def _(dve):
                with dve.Fori(0, NB // NBUF) as i:
                    for q in range(NBUF):
                        dve.wait_ge(base_in[q], 16 * (i + 1))
                        dve.wait_ge(gathered[q], 16 * NT * (i + 1))
                        dve.wait_ge(stored[q], 16 * i)
                        nc.vector.tensor_tensor(ob[:, q], gy[:, q], xb[:, q], ALU.add).then_inc(added, 1)

            @block.scalar
            def _(act):
                with act.Fori(0, NB // NBUF) as i:
                    for q in range(NBUF):
                        b = NBUF * i + q
                        act.wait_ge(added, b + 1)
                        act.dma_start(out_d[bass.ds(b * L, L), :].rearrange("(t p) d -> p t d", p=P), ob[:, q]).then_inc(stored[q], 16)
                for q in range(NBUF):
                    act.wait_ge(stored[q], 16 * (NB // NBUF))


def build(nc, i, out):
    def dram(name, shape, dt=F32):
        return nc.dram_tensor(name, shape, dt, kind="Internal").ap()

    base = dram("base", [T, D])
    meta = dram("meta", [NB * P, 4 * NT], U32)
    xs = dram("xs", [E0 * REG + GRP, D])
    ys = dram("ys", [NG0 * GRP, D])
    base2 = dram("base2", [T, D])
    meta2 = dram("meta2", [NB * P, NT], U32)
    xs2 = dram("xs2", [E1 * REG + GRP, D])
    ys2 = dram("ys2", [NG1 * GRP, D])
    with ExitStack() as ctx:
        k = Kept(nc, ctx)
        setup(nc, k, i)
        layer0_attention(nc, k, i["x"], base, meta, xs)
        group_table(nc, k, k.run0, E0, NG0, 2 * NT, xs, meta, "gt0")
        expert_ffn(nc, k, 0, xs, ys, i["we0"], "f0")
        layer1_attention(nc, k, ys, base, meta, i["rf"], base2, meta2, xs2)
        group_table(nc, k, k.run1, E1, NG1, NT, xs2, meta2, "gt1")
        expert_ffn(nc, k, 1, xs2, ys2, i["we1"], "f1")
        output_rows(nc, k, ys2, base2, meta2, out)


def rotary_factors():
    d = np.arange(DH1)
    theta = np.power(np.float32(10000.0), (-2.0 * (d // 2) / DH1).astype(np.float32)).astype(np.float32)
    ang = (np.arange(L, dtype=np.float32)[:, None] * theta[None, :]).astype(np.float32)
    sign = np.where(np.arange(L) % 2 == 1, -1.0, 1.0).astype(np.float32)
    return (np.cos(ang) + sign[:, None] * np.sin(ang)).astype(np.float32)


def laid_out(a):
    def heads_last(w, heads):
        return w.reshape(D, heads, DH1).transpose(0, 2, 1).reshape(D, heads * DH1)

    def chunked(w):
        out = np.zeros((E1, D, FC1 * P), w.dtype)
        out[:, :, :F1] = w.transpose(0, 2, 1)
        return out

    down = np.zeros((E1, FC1 * P, D), a["L1_ffn_down_w"].dtype)
    down[:, :F1] = a["L1_ffn_down_w"].transpose(0, 2, 1)
    arrays = {
        "x": a["L0_attn_x"].reshape(T, D),
        "w0cat": np.concatenate([a["L0_attn_Wq"], a["L0_attn_Wk"], a["L0_attn_Wv"], a["L0_ffn_Wr"]], 1),
        "w1cat": np.concatenate([heads_last(a["L1_attn_w_q"], H1), heads_last(a["L1_attn_w_k"], KV1), a["L1_attn_w_v"],
                                 a["L1_ffn_router_w"].T], 1),
        "L0_attn_Wo": a["L0_attn_Wo"],
        "L1_attn_w_o": a["L1_attn_w_o"],
        "norms": np.stack([a["L0_attn_norm_w"], a["L1_attn_g"]], 1),
        "gate": np.broadcast_to(a["L0_attn_gate"], (P, 1)),
        "logt": np.broadcast_to(a["L0_attn_log_temperature"], (P, 4)),
        "br0": np.broadcast_to(a["L0_ffn_br"], (P, E0)),
        "we0": np.concatenate([
            a["L0_ffn_W1"], a["L0_ffn_W2"].reshape(E0, F0 // P, P, D).transpose(0, 2, 1, 3).reshape(E0, P, F0 // P * D),
            a["L0_ffn_b1"].reshape(E0, F0 // P, P).transpose(0, 2, 1),
            np.broadcast_to(a["L0_ffn_b2"][:, None, :], (E0, P, D))], 2).reshape(E0 * P, -1),
        "we1": np.concatenate([
            chunked(a["L1_ffn_gate_w"]), chunked(a["L1_ffn_up_w"]),
            down.reshape(E1, FC1, P, D).transpose(0, 2, 1, 3).reshape(E1, P, FC1 * D)], 2).reshape(E1 * P, -1),
        "rf": rotary_factors(),
    }
    return {n: np.ascontiguousarray(v) for n, v in arrays.items()}


def kernel(**inputs):
    import concourse.bacc as bacc
    from concourse.bass_utils import run_bass_kernel_spmd

    nc = bacc.Bacc("TRN2", target_bir_lowering=False, num_devices=1)
    arrays = {f"in_{n}": v for n, v in laid_out({n: np.asarray(v) for n, v in inputs.items()}).items()}
    aps = {n[3:]: nc.dram_tensor(n, v.shape, mybir.dt.from_np(v.dtype), kind="ExternalInput").ap() for n, v in arrays.items()}
    out = nc.dram_tensor("out", (T, D), F32, kind="ExternalOutput").ap()
    build(nc, aps, out)
    r = run_bass_kernel_spmd(nc, [arrays], core_ids=[0])
    return r.results[0]["out"].reshape(NB, L, D)
```

```python
from contextlib import ExitStack

import numpy as np

import concourse.bass as bass
from concourse import mybir

F32 = mybir.dt.float32
BF16 = mybir.dt.bfloat16
U32 = mybir.dt.uint32
ALU = mybir.AluOpType
ACT = mybir.ActivationFunctionType
AX = mybir.AxisListType.X

P = 128
D = 128
NB, L = 16, 512
T = NB * L
NT = L // P
EPS_LN = 1e-5

H0, KV0, DH0 = 4, 2, 32
E0, F0 = 16, 256
QKV0 = D + 2 * KV0 * DH0
PRJ0 = QKV0 + E0
H1, KV1, DH1 = 16, 4, 8
REP1 = H1 // KV1
E1, F1 = 8, 352
FC1 = 3
QKV1 = D + 2 * KV1 * DH1
PRJ1 = QKV1 + E1

GRP = 2 * P
REG = T + GRP
NG0 = 2 * T // GRP + E0
NG1 = T // GRP + E1
PAD = 2 * E1 * GRP
NBUF = 8


HEADS_LINKS0 = 11
ROUTE_LINKS1 = 9
NORM_LINKS1 = 8


class Chain:

    def __init__(self, eng, sem, per, passed_count=None):
        self.eng, self.sem, self.per, self.passed = eng, sem, per, passed_count

    def at(self, b):
        self.base, self.n = b * self.per, 0

    def link(self, ins):
        self.n += 1
        ins.then_inc(self.sem, 1)
        self.eng.wait_ge(self.sem, self.base + self.n)

    def link_apart(self, ins):
        self.n += 1
        ins.then_inc(self.sem, 1)
        self.eng.wait_ge(self.sem, self.base + self.n)
        passed(self.eng, self.passed)

    def end(self):
        assert self.n == self.per, (self.sem, self.n, self.per)


def passed(eng, count):
    eng.sem_inc(count, 1)


def allocators(nc, ctx):
    taken = []

    def clear():
        with nc.Block() as block:

            @block.gpsimd
            def _(pool):
                for num in sorted(taken):
                    if num - 1 not in taken:
                        end = next(n for n in range(num, 999) if n not in taken)
                        pool.sem_clear(range(num, end))

    ctx.callback(lambda: clear() if taken else None)

    def sb(name, shape, dt=F32):
        return ctx.enter_context(nc.sbuf_tensor(name, shape, dt))

    def ps(name, shape, dt=F32):
        return ctx.enter_context(nc.psum_tensor(name, shape, dt))

    def sem(name):
        s = ctx.enter_context(nc.semaphore(name))
        taken.append(s.num)
        return s

    return sb, ps, sem


def setup(nc, k, i, xs2_d, base2_d):
    with ExitStack() as ctx:
        sb, ps, sem = allocators(nc, ctx)
        loaded = sem("su_loaded")
        pool_made = sem("su_pool")
        dve_made = sem("su_dve")
        act_made = sem("su_act")
        w0 = sb("su_w0", [P, PRJ0])
        w1 = sb("su_w1", [P, PRJ1])
        g0 = sb("su_g0", [P, 2])
        with nc.Block() as block:

            @block.sync
            def _(sp):
                sp.dma_start(w0[:], i["w0cat"]).then_inc(loaded, 16)
                sp.dma_start(w1[:], i["w1cat"]).then_inc(loaded, 16)
                sp.dma_start(k.wo0[:], i["L0_attn_Wo"]).then_inc(loaded, 16)
                sp.dma_start(k.wo1[:], i["L1_attn_w_o"]).then_inc(loaded, 16)
                sp.dma_start(g0[:], i["norms"]).then_inc(loaded, 16)
                sp.dma_start(k.gate[:], i["gate"]).then_inc(loaded, 16)
                sp.dma_start(k.temp[:], i["logt"]).then_inc(loaded, 16)
                sp.dma_start(k.br0[:], i["br0"]).then_inc(loaded, 16)
                sp.wait_ge(loaded, 8 * 16)
                sp.wait_ge(pool_made, 6)
                for e in range(E1):
                    sp.dma_start(xs2_d[E1 * REG + e * GRP:E1 * REG + (e + 1) * GRP, :].rearrange("(p t) d -> p (t d)", p=P),
                                 k.zeros[:]).then_inc(k.spares_out, 16)
                sp.wait_ge(dve_made, 1)
                sp.dma_start(base2_d[E1 * REG:, :].rearrange("(e p t) d -> p e (t d)", p=P, e=E1),
                             k.pads[:, E1:].rearrange("p e t d -> p e (t d)")).then_inc(k.spares_out, 16)

            @block.gpsimd
            def _(pool):
                nc.gpsimd.memset(k.ident_b[:], 0.0)
                nc.gpsimd.memset(k.causal[:], 0.0)
                nc.gpsimd.memset(k.ident[:], 0.0).then_inc(pool_made, 1)
                nc.gpsimd.memset(k.tri[:], 1.0).then_inc(pool_made, 1)
                nc.gpsimd.memset(k.mhalf[:], -0.5)
                nc.gpsimd.memset(k.pads[:], 0.0)
                nc.gpsimd.iota(k.pad_ids[:], pattern=[[GRP, 2 * E1], [1, GRP // P]], base=T, channel_multiplier=GRP // P)
                nc.gpsimd.iota(k.token_i[:], pattern=[[P, NT]], base=0, channel_multiplier=1)
                nc.gpsimd.iota(k.iota_i[:], pattern=[[1, 128]], base=0, channel_multiplier=0).then_inc(pool_made, 1)
                pool.wait_ge(pool_made, 3)
                nc.gpsimd.affine_select(out=k.ident[:], in_=k.ident[:], compare_op=ALU.not_equal, fill=1.0,
                                        base=0, pattern=[[-1, P]], channel_multiplier=1).then_inc(pool_made, 1)
                nc.gpsimd.affine_select(out=k.ident_b[:], in_=k.ident_b[:], compare_op=ALU.not_equal, fill=1.0,
                                        base=0, pattern=[[-1, P]], channel_multiplier=1)
                nc.gpsimd.affine_select(out=k.causal[:], in_=k.causal[:], compare_op=ALU.is_ge, fill=-1e30,
                                        base=0, pattern=[[1, P]], channel_multiplier=-1)
                nc.gpsimd.affine_select(out=k.tri[:], in_=k.tri[:], compare_op=ALU.is_gt, fill=0.0,
                                        base=0, pattern=[[1, P]], channel_multiplier=-1).then_inc(pool_made, 1)
                nc.gpsimd.memset(k.ones_b[:], 1.0)
                nc.gpsimd.memset(k.ones_f[:], 1.0)
                nc.gpsimd.memset(k.zeros[:], 0.0).then_inc(pool_made, 1)

            @block.scalar
            def _(act):
                act.wait_ge(loaded, 8 * 16)
                nc.scalar.activation(k.temp[:, 1:2], k.temp[:, 0:1], ACT.Exp).then_inc(act_made, 1)

            @block.vector
            def _(dve):
                dve.wait_ge(loaded, 8 * 16)
                nc.vector.tensor_scalar(k.w0[:, 0:QKV0], w0[:, 0:QKV0], g0[:, 0:1], None, ALU.mult)
                nc.vector.tensor_scalar(k.w1[:, 0:QKV1], w1[:, 0:QKV1], g0[:, 1:2], None, ALU.mult)
                nc.vector.tensor_copy(k.w0[:, QKV0:PRJ0], w0[:, QKV0:PRJ0])
                nc.vector.tensor_copy(k.w1[:, QKV1:PRJ1], w1[:, QKV1:PRJ1])
                dve.wait_ge(pool_made, 3)
                nc.vector.tensor_copy(k.pads[:, :, :, D].bitcast(mybir.dt.int32), k.pad_ids[:])
                nc.vector.tensor_copy(k.token[:], k.token_i[:])
                nc.vector.tensor_copy(k.iota[:], k.iota_i[:]).then_inc(dve_made, 1)
                dve.wait_ge(dve_made, 1)
                nc.vector.tensor_scalar(k.run0[:], k.iota[:, 0:E0], float(REG), None, ALU.mult)
                nc.vector.tensor_scalar(k.run1[:], k.iota[:, 0:E1], float(REG), None, ALU.mult)
                dve.wait_ge(act_made, 1)
                nc.vector.tensor_scalar(k.temp[:, 2:3], k.temp[:, 1:2], -1.0, 80.0, ALU.mult, ALU.add).then_inc(dve_made, 1)
                dve.wait_ge(dve_made, 2)
                nc.vector.tensor_scalar(k.temp[:, 3:4], k.temp[:, 2:3], 0.0, None, ALU.min)


def batch(i, o):
    return 2 * i + o, i + o // 2, o % 2


def bodies(eng, body):
    for o in range(3):
        body(0, o)
    with eng.Fori(1, 6) as i:
        body(i, 1)
        body(i, 2)
    for o in range(13, NB):
        body(0, o)


def flags(i, o):
    static = isinstance(i, int)
    return (not (static and o == 0), *(not (static and o >= NB - n) for n in (1, 2, 3)))


def layer0_attention(nc, k, x_d, base_d, meta_d, xs_d):
    with ExitStack() as ctx:
        sb, ps, sem = allocators(nc, ctx)
        x = sb("a_x", [P, 2, NT, D])
        xn = sb("a_xn", [P, 2, NT, D])
        xs = sb("a_xs", [P, 2, NT, D])
        stats = sb("a_stats", [P, NT, 6])
        mv = sb("a_mv", [P, NT, 2])
        tmp4 = sb("a_tmp4", [P, 3, NT])
        rstd = sb("a_rstd", [P, NT])
        r2 = sb("a_r2", [P, 2, NT])
        r2sq = sb("a_r2sq", [P, NT])
        xnT = sb("a_xnT", [P, L])
        prj = sb("a_prj", [P, NT, PRJ0])
        sq = sb("a_sq", [P, NT * (H0 + KV0), DH0])
        ss = sb("a_ss", [P, NT, H0 + KV0])
        ftmp = sb("a_ftmp", [P, 3, NT, H0 + KV0])
        fac = sb("a_fac", [P, NT, H0 + KV0])
        qn = sb("a_qn", [P, NT, D])
        kn = sb("a_kn", [P, NT, D])
        v = sb("a_v", [P, 2, NT, KV0 * DH0])
        qT = sb("a_qT", [P, 2, L])
        kz = sb("a_kz", [P, 2, H0, L])
        pt = sb("a_pt", [P, 2, H0, L])
        rs = sb("a_rs", [P, L])
        attnT = sb("a_attnT", [P, L])
        bs = sb("a_bs", [P, 2, NT, D])
        lg = sb("a_lg", [P, NT, E0])
        mx8 = sb("a_mx8", [P, NT, 8])
        ix8 = sb("a_ix8", [P, NT, 8], U32)
        ixf = sb("a_ixf", [P, NT, 2])
        oh = sb("a_oh", [P, 2, NT, E0])
        ohb = sb("a_ohb", [P, NT, E0], BF16)
        pos = sb("a_pos", [P, NT, E0])
        ohp = sb("a_ohp", [P, 2, NT, E0])
        slotf = sb("a_slotf", [P, 2, NT])
        dl = sb("a_dl", [P, NT])
        el = sb("a_el", [P, NT])
        ep = sb("a_ep", [P, NT])
        meta = sb("a_meta", [P, 2, 4 * NT], U32)

        ps_t = ps("a_ps_t", [P, L])
        ps_p = ps("a_ps_p", [P, L])
        ps_s = ps("a_ps_s", [P, 2, 2, L])
        ps_v = ps("a_ps_v", [P, L])
        ps_d = ps("a_ps_d", [P, L])
        RT = 288

        x_in = [sem(f"a_x_in{p}") for p in range(2)]
        x_used, stats_ready, rstd_ready, xn_ready = sem("a_x_used"), sem("a_stats"), sem("a_rstd_r"), sem("a_xn_r")
        xT_ps, xT_sb, proj_ps, prj_sb, sq_ready = sem("a_xT_ps"), sem("a_xT_sb"), sem("a_proj"), sem("a_prj_sb"), sem("a_sq_r")
        ss_ready, fac_ready, qkv_ready = sem("a_ss_r"), sem("a_fac_r"), sem("a_qkv_r")
        qT_ps, qT_sb, kT_ps, kT_sb = sem("a_qT_ps"), sem("a_qT_sb"), sem("a_kT_ps"), sem("a_kT_sb")
        oh_ready, rank_ps, rank_used, dl_ready, el_ready, meta_ready = (
            sem("a_oh_r"), sem("a_rank"), sem("a_rank_u"), sem("a_dl_r"), sem("a_el_r"), sem("a_meta_r"))
        scattered = k.scattered0
        meta_out = [sem(f"a_meta_out{p}") for p in range(2)]
        s_ps, exp_done, pv_tile = sem("a_s_ps"), sem("a_exp"), sem("a_pvt")
        norm_done, wo_ps, wo_used = sem("a_norm"), sem("a_wo_ps"), sem("a_wo_used")
        base_out = [sem(f"a_base_out{p}") for p in range(2)]
        dve_ln, dve_qkv, dve_main, pool_ln, pool_fac = (sem(f"a_{n}") for n in ("dve_ln", "dve_qkv", "dve_main", "pool_ln", "pool_fac"))

        with nc.Block() as block:

            @block.vector
            def _(dve):
                nc.vector.memset(kz[:], 0.0).then_inc(x_used, 2)
                nc.vector.memset(ss[:], 0.0)
                nc.vector.memset(mv[:], 0.0).then_inc(exp_done, 2)
                nc.vector.memset(stats[:], 0.0).then_inc(pv_tile, 2 * NT)
                nc.vector.memset(rs[:], 0.0).then_inc(wo_used, 2)

        with nc.Block() as block:

            @block.sync
            def _(sp):
                def load(i, o):
                    b, h, p = batch(i, o)
                    sp.wait_ge(x_used, b + 1)
                    passed(sp, k.passed_sp)
                    sp.dma_start(x[:, p], x_d[bass.ds(b * L, L), :].rearrange("(t p) d -> p t d", p=P)).then_inc(x_in[p], 16)

                def store_meta(i, o):
                    b, h, p = batch(i, o)
                    sp.wait_ge(meta_ready, b + 1)
                    passed(sp, k.passed_sp)
                    sp.dma_start(meta_d[bass.ds(b * P, P), :], meta[:, p]).then_inc(meta_out[p], 16)

                def store_base(i, o):
                    b, h, p = batch(i, o)
                    sp.wait_ge(wo_used, b + 3)
                    passed(sp, k.passed_sp)
                    sp.dma_start(base_d[bass.ds(b * L, L), :].rearrange("(t p) d -> p t d", p=P), bs[:, p]).then_inc(base_out[p], 16)

                def body(i, o):
                    prev, nxt, nxt2, nxt3 = flags(i, o)
                    if prev:
                        store_base(i, o - 1)
                    if nxt3:
                        load(i, o + 3)
                    if nxt:
                        store_meta(i, o + 1)

                for o in range(3):
                    load(0, o)
                store_meta(0, 0)
                bodies(sp, body)
                store_base(0, NB - 1)
                for p in range(2):
                    sp.wait_ge(meta_out[p], 16 * (NB // 2))
                    sp.wait_ge(base_out[p], 16 * (NB // 2))

            @block.vector
            def _(dve):
                ln = Chain(dve, dve_ln, 1, k.passed_dve)
                heads = Chain(dve, dve_qkv, HEADS_LINKS0, k.passed_dve)
                main = Chain(dve, dve_main, 1)

                def statistics(i, o):
                    b, h, p = batch(i, o)
                    ln.at(b)
                    dve.wait_ge(x_in[p], 16 * (h + 1))
                    dve.wait_ge(rstd_ready, b)
                    for t in range(NT):
                        last = nc.vector.bn_stats(stats[:, t, :], x[:, p, t, :])
                    ln.link_apart(last)
                    for t in range(NT):
                        last = nc.vector.bn_aggr(mv[:, t, :], stats[:, t, :])
                    last.then_inc(stats_ready, 1)
                    ln.end()

                def normal_rows(i, o):
                    b, h, p = batch(i, o)
                    dve.wait_ge(rstd_ready, b + 1)
                    dve.wait_ge(scattered[p], 16 * 2 * NT * h)
                    for t in range(NT):
                        last = nc.vector.tensor_scalar(xn[:, p, t, :], x[:, p, t, :], mv[:, t, 0:1], rstd[:, t:t + 1],
                                                       ALU.subtract, ALU.mult)
                    last.then_inc(xn_ready, 1)

                def keep_sum(i, o):
                    b, h, p = batch(i, o)
                    dve.wait_ge(xn_ready, b + 1)
                    dve.wait_ge(wo_used, b + 1)
                    nc.vector.scalar_tensor_tensor(xs[:, p], xn[:, p], 2.0, x[:, p], ALU.mult, ALU.add).then_inc(x_used, 1)

                def square_sums(i, o):
                    b, h, p = batch(i, o)
                    dve.wait_ge(sq_ready, b + 1)
                    dve.wait_ge(fac_ready, b)
                    nc.vector.tensor_reduce(ss[:].rearrange("p t h -> p (t h)"), sq[:], AX, ALU.add).then_inc(ss_ready, 1)

                def heads_rows(i, o):
                    b, h, p = batch(i, o)
                    heads.at(b)
                    dve.wait_ge(fac_ready, b + 1)
                    dve.wait_ge(kT_ps, b)
                    dve.wait_ge(pv_tile, NT * (b + 1))
                    nc.vector.tensor_tensor(qn[:].rearrange("p t (h d) -> p t h d", h=H0),
                                            prj[:, :, 0:D].rearrange("p t (h d) -> p t h d", h=H0),
                                            fac[:, :, 0:H0].unsqueeze(3).to_broadcast([P, NT, H0, DH0]), ALU.mult)
                    for r in range(H0 // KV0):
                        nc.vector.tensor_tensor(kn[:].rearrange("p t (g r d) -> p t g r d", g=KV0, d=DH0)[:, :, :, r, :],
                                                prj[:, :, D:D + KV0 * DH0].rearrange("p t (h d) -> p t h d", h=KV0),
                                                fac[:, :, H0:H0 + KV0].unsqueeze(3).to_broadcast([P, NT, KV0, DH0]), ALU.mult)
                    nc.vector.tensor_tensor(v[:, p], prj[:, :, D + KV0 * DH0:QKV0],
                                            r2[:, p].unsqueeze(2).to_broadcast([P, NT, KV0 * DH0]), ALU.mult).then_inc(qkv_ready, 1)

                def choose(i, o):
                    b, h, p = batch(i, o)
                    heads.link_apart(nc.vector.tensor_tensor(lg[:], prj[:, :, QKV0:PRJ0],
                                                             k.br0[:].unsqueeze(1).to_broadcast([P, NT, E0]), ALU.add))
                    for t in range(NT):
                        last = nc.vector.max(mx8[:, t, :], lg[:, t, :])
                    heads.link_apart(last)
                    for t in range(NT):
                        last = nc.vector.max_index(ix8[:, t, :], mx8[:, t, :], lg[:, t, :])
                    dve.wait_ge(el_ready, b)
                    nc.vector.tensor_tensor(dl[:], mx8[:, :, 1], mx8[:, :, 0], ALU.subtract).then_inc(dl_ready, 1)
                    dve.wait_ge(dl_ready, b + 1)
                    heads.link(nc.vector.tensor_copy(ixf[:], ix8[:, :, 0:2]))
                    for c in range(2):
                        last = nc.vector.tensor_tensor(oh[:, c], k.iota[:, 0:E0].unsqueeze(1).to_broadcast([P, NT, E0]),
                                                       ixf[:, :, c].unsqueeze(2).to_broadcast([P, NT, E0]), ALU.is_equal)
                    heads.link(last)
                    nc.vector.tensor_tensor(ohb[:], oh[:, 0], oh[:, 1], ALU.add).then_inc(oh_ready, 1)

                def kz_rows(i, o):
                    b, h, p = batch(i, o)
                    dve.wait_ge(kT_ps, b + 1)
                    for head in range(H0):
                        r = slice(head * DH0, (head + 1) * DH0)
                        last = nc.vector.tensor_copy(kz[r, p, head, :], ps_t[r, :])
                    last.then_inc(kT_sb, 1)

                def slots(i, o):
                    b, h, p = batch(i, o)
                    dve.wait_ge(rank_ps, b + 1)
                    for t in range(NT):
                        nc.vector.tensor_tensor(pos[:, t], ps_p[:, RT + t * E0:RT + (t + 1) * E0], k.run0[:], ALU.add)
                        last = nc.vector.tensor_tensor(k.run0[:], ps_p[:, RT + (NT + t) * E0:RT + (NT + t + 1) * E0],
                                                       k.run0[:], ALU.add)
                        if t < NT - 1:
                            heads.link(last)
                    last.then_inc(rank_used, 1)
                    dve.wait_ge(rank_used, b + 1)
                    for c in range(2):
                        last = nc.vector.tensor_tensor(ohp[:, c], oh[:, c], pos[:], ALU.mult)
                    heads.link(last)
                    heads.link(nc.vector.tensor_reduce(slotf[:].rearrange("p c t -> p (c t)"),
                                                       ohp[:].rearrange("p c t e -> p (c t) e"), AX, ALU.add))
                    dve.wait_ge(el_ready, b + 1)
                    dve.wait_ge(meta_out[p], 16 * h)
                    dve.wait_ge(scattered[p], 16 * 2 * NT * h)
                    heads.link(nc.vector.tensor_scalar(ep[:], el[:], 1.0, None, ALU.add))
                    wts = meta[:, p].bitcast(F32)
                    heads.link(nc.vector.reciprocal(wts[:, 2 * NT:3 * NT], ep[:]))
                    nc.vector.tensor_tensor(wts[:, 3 * NT:4 * NT], el[:], wts[:, 2 * NT:3 * NT], ALU.mult)
                    nc.vector.tensor_copy(meta[:, p, 0:2 * NT], slotf[:].rearrange("p c t -> p (c t)")).then_inc(meta_ready, 1)
                    heads.end()

                def normalise(i, o):
                    b, h, p = batch(i, o)
                    main.at(b)
                    dve.wait_ge(pv_tile, NT * (b + 3))
                    main.link(nc.vector.reciprocal(rs[:], ps_d[:]))
                    dve.wait_ge(wo_ps, b)
                    nc.vector.tensor_tensor(attnT[:], ps_v[:], rs[:], ALU.mult).then_inc(norm_done, 1)
                    main.end()

                def add_output(i, o):
                    b, h, p = batch(i, o)
                    dve.wait_ge(wo_ps, b + 1)
                    dve.wait_ge(base_out[p], 16 * h)
                    nc.vector.scalar_tensor_tensor(bs[:, p].rearrange("p t d -> p (t d)"), ps_t[:], k.gate[:, 0:1],
                                                   xs[:, p].rearrange("p t d -> p (t d)"), ALU.mult, ALU.add).then_inc(wo_used, 1)

                def body(i, o):
                    prev, nxt, nxt2, nxt3 = flags(i, o)
                    if prev:
                        normalise(i, o - 1)
                    if nxt2:
                        statistics(i, o + 2)
                    if prev:
                        add_output(i, o - 1)
                    if nxt:
                        heads_rows(i, o + 1)
                        choose(i, o + 1)
                        kz_rows(i, o + 1)
                    if nxt2:
                        normal_rows(i, o + 2)
                    if nxt:
                        slots(i, o + 1)
                        keep_sum(i, o + 1)
                    if nxt2:
                        square_sums(i, o + 2)

                statistics(0, 0)
                normal_rows(0, 0)
                square_sums(0, 0)
                heads_rows(0, 0)
                choose(0, 0)
                kz_rows(0, 0)
                keep_sum(0, 0)
                statistics(0, 1)
                normal_rows(0, 1)
                slots(0, 0)
                square_sums(0, 1)
                bodies(dve, body)
                normalise(0, NB - 1)
                add_output(0, NB - 1)

            @block.gpsimd
            def _(pool):
                ln = Chain(pool, pool_ln, 6, k.passed_pool)
                fc = Chain(pool, pool_fac, 3, k.passed_pool)

                def norms(i, o):
                    b, h, p = batch(i, o)
                    ln.at(b)
                    pool.wait_ge(stats_ready, b + 1)
                    pool.wait_ge(xn_ready, b)
                    pool.wait_ge(fac_ready, b)
                    if not (isinstance(b, int) and b < 2):
                        pool.wait_ge(qkv_ready, b - 1)
                    passed(pool, k.passed_pool)
                    ln.link(nc.gpsimd.tensor_scalar(tmp4[:, 0], mv[:, :, 1], EPS_LN, None, ALU.add))
                    ln.link(nc.gpsimd.tensor_tensor(rstd[:], tmp4[:, 0], k.mhalf[:, 0:NT], ALU.pow))
                    ln.link(nc.gpsimd.tensor_tensor(tmp4[:, 1], rstd[:], rstd[:], ALU.mult))
                    ln.link_apart(nc.gpsimd.tensor_tensor(tmp4[:, 2], tmp4[:, 1], mv[:, :, 1], ALU.mult))
                    ln.link(nc.gpsimd.tensor_scalar(tmp4[:, 0], tmp4[:, 2], 1e-6, None, ALU.add))
                    ln.link(nc.gpsimd.tensor_tensor(r2[:, p], tmp4[:, 0], k.mhalf[:, 0:NT], ALU.pow))
                    nc.gpsimd.tensor_tensor(r2sq[:], r2[:, p], r2[:, p], ALU.mult).then_inc(rstd_ready, 1)
                    ln.end()

                def factors(i, o):
                    b, h, p = batch(i, o)
                    fc.at(b)
                    pool.wait_ge(ss_ready, b + 1)
                    pool.wait_ge(rstd_ready, b + 1)
                    pool.wait_ge(qkv_ready, b)
                    bc = r2sq[:].unsqueeze(2).to_broadcast([P, NT, H0 + KV0])
                    fc.link_apart(nc.gpsimd.tensor_tensor(ftmp[:, 0], ss[:], bc, ALU.mult))
                    fc.link(nc.gpsimd.tensor_scalar(ftmp[:, 1], ftmp[:, 0], 1e-24, None, ALU.max))
                    fc.link(nc.gpsimd.tensor_tensor(ftmp[:, 2].rearrange("p t h -> p (t h)"),
                                                    ftmp[:, 1].rearrange("p t h -> p (t h)"),
                                                    k.mhalf[:, 0:NT * (H0 + KV0)], ALU.pow))
                    nc.gpsimd.tensor_tensor(fac[:], ftmp[:, 2], r2[:, p].unsqueeze(2).to_broadcast([P, NT, H0 + KV0]),
                                            ALU.mult).then_inc(fac_ready, 1)
                    fc.end()

                def scatter(i, o, c):
                    b, h, p = batch(i, o)
                    if c == 0:
                        pool.wait_ge(meta_ready, b + 1)
                        passed(pool, k.passed_pool)
                    for t in range(NT):
                        nc.gpsimd.indirect_dma_start(
                            xs_d, bass.IndirectOffsetOnAxis(ap=meta[:, p, c * NT + t:c * NT + t + 1], axis=0),
                            xn[:, p, t, :], None).then_inc(scattered[p], 16)

                def body(i, o):
                    prev, nxt, nxt2, nxt3 = flags(i, o)
                    if nxt:
                        factors(i, o + 1)
                    scatter(i, o, 1)
                    if nxt2:
                        norms(i, o + 2)
                    if nxt:
                        scatter(i, o + 1, 0)

                norms(0, 0)
                factors(0, 0)
                norms(0, 1)
                scatter(0, 0, 0)
                bodies(pool, body)
                for p in range(2):
                    pool.wait_ge(scattered[p], 16 * 2 * NT * (NB // 2))

            @block.scalar
            def _(act):
                def xT_copy(i, o):
                    b, h, p = batch(i, o)
                    act.wait_ge(xT_ps, b + 1)
                    act.wait_ge(proj_ps, NT * b)
                    nc.scalar.activation(xnT[:], ps_t[:], ACT.Copy).then_inc(xT_sb, 1)

                def prj_copy(i, o, t):
                    b, h, p = batch(i, o)
                    act.wait_ge(proj_ps, NT * b + t + 1)
                    if t == 0:
                        act.wait_ge(qkv_ready, b)
                        act.wait_ge(oh_ready, b)
                    nc.scalar.activation(prj[:, t, :], ps_p[:, 0:PRJ0], ACT.Copy).then_inc(prj_sb, 1)

                def squares(i, o):
                    b, h, p = batch(i, o)
                    act.wait_ge(prj_sb, NT * (b + 1))
                    act.wait_ge(ss_ready, b)
                    nc.scalar.activation(sq[:].rearrange("p (t h) d -> p t (h d)", t=NT), prj[:, :, 0:D + KV0 * DH0],
                                         ACT.Square).then_inc(sq_ready, 1)

                def qT_copy(i, o):
                    b, h, p = batch(i, o)
                    act.wait_ge(qT_ps, b + 1)
                    act.wait_ge(pv_tile, NT * (b + 1))
                    nc.scalar.activation(qT[:, p, :], ps_t[:], ACT.Copy).then_inc(qT_sb, 1)

                def odds(i, o):
                    b, h, p = batch(i, o)
                    act.wait_ge(dl_ready, b + 1)
                    act.wait_ge(meta_ready, b)
                    nc.scalar.activation(el[:], dl[:], ACT.Exp).then_inc(el_ready, 1)

                def exps(i, o, u):
                    b, h, p = batch(i, o)
                    kt, pr = u // 2, u % 2
                    n = L - kt * P
                    act.wait_ge(s_ps, 8 * b + u + 1)
                    act.wait_ge(pv_tile, NT * (b + 1) + kt + 3)
                    nc.scalar.activation(pt[:, kt % 2, 2 * pr:2 * pr + 2, 0:n], ps_s[:, u % 2, :, 0:n], ACT.Exp,
                                         bias=k.temp[:, 3:4], scale=k.temp[:, 1:2]).then_inc(exp_done, 1)

                def body(i, o):
                    prev, nxt, nxt2, nxt3 = flags(i, o)
                    for u in range(4):
                        exps(i, o, u)
                    if nxt:
                        qT_copy(i, o + 1)
                    exps(i, o, 4)
                    if nxt:
                        odds(i, o + 1)
                    exps(i, o, 5)
                    if nxt2:
                        xT_copy(i, o + 2)
                    exps(i, o, 6)
                    if nxt2:
                        prj_copy(i, o + 2, 0)
                    exps(i, o, 7)
                    if nxt2:
                        for t in range(1, NT):
                            prj_copy(i, o + 2, t)
                        squares(i, o + 2)

                def rows(o):
                    xT_copy(0, o)
                    for t in range(NT):
                        prj_copy(0, o, t)
                    squares(0, o)

                rows(0)
                odds(0, 0)
                qT_copy(0, 0)
                rows(1)
                bodies(act, body)

            @block.tensor
            def _(pe):
                def transposes(src, done):
                    for t in range(NT):
                        last = nc.tensor.transpose(ps_t[:, t * P:(t + 1) * P], src[:, t, :], k.ident[:])
                    last.then_inc(done, 1)

                def x_rows(i, o):
                    b, h, p = batch(i, o)
                    pe.wait_ge(xn_ready, b + 1)
                    pe.wait_ge(kT_sb, b)
                    transposes(xn[:, p], xT_ps)

                def project(i, o, t):
                    b, h, p = batch(i, o)
                    pe.wait_ge(xT_sb, b + 1)
                    pe.wait_ge(prj_sb, NT * b + t)
                    if t == 0:
                        pe.wait_ge(rank_used, b)
                    nc.tensor.matmul(ps_p[:, 0:PRJ0], xnT[:, t * P:(t + 1) * P], k.w0[:], start=True, stop=True).then_inc(proj_ps, 1)

                def ranks(i, o):
                    b, h, p = batch(i, o)
                    pe.wait_ge(oh_ready, b + 1)
                    pe.wait_ge(rank_used, b)
                    pe.wait_ge(prj_sb, NT * (b + 1))
                    flat = ohb[:].rearrange("p t e -> p (t e)")
                    nc.tensor.matmul(ps_p[:, RT:RT + NT * E0], k.tri[:], flat, start=True, stop=True)
                    nc.tensor.matmul(ps_p[:, RT + NT * E0:RT + 2 * NT * E0], k.ones_b[:], flat, start=True, stop=True).then_inc(rank_ps, 1)

                def q_columns(i, o):
                    b, h, p = batch(i, o)
                    pe.wait_ge(qkv_ready, b + 1)
                    pe.wait_ge(xT_sb, b + 1)
                    pe.wait_ge(wo_used, b + 1)
                    transposes(qn, qT_ps)

                def k_columns(i, o):
                    b, h, p = batch(i, o)
                    pe.wait_ge(qT_sb, b + 1)
                    transposes(kn, kT_ps)

                def scores(i, o, u):
                    b, h, p = batch(i, o)
                    kt, pr = u // 2, u % 2
                    if u == 0:
                        pe.wait_ge(qT_sb, b + 1)
                        pe.wait_ge(kT_sb, b + 1)
                    pe.wait_ge(exp_done, 8 * b + u + 1)
                    for j in range(2):
                        head = 2 * pr + j
                        nc.tensor.matmul(ps_s[:, u % 2, j, 0:L - kt * P], kz[:, p, head, kt * P:(kt + 1) * P],
                                         qT[:, p, kt * P:L], start=True, stop=False)
                        last = nc.tensor.matmul(ps_s[:, u % 2, j, 0:P], k.ident_b[:], k.causal[:], start=False, stop=True)
                    last.then_inc(s_ps, 1)

                def values(i, o, kt):
                    b, h, p = batch(i, o)
                    pe.wait_ge(exp_done, 8 * b + 2 * kt + 4)
                    if kt == 0:
                        pe.wait_ge(norm_done, b)
                    n = L - kt * P
                    for dst, ones in ((ps_v, False), (ps_d, True)):
                        for head in range(H0):
                            g = head // (H0 // KV0)
                            w = k.ones_f[:, 0:DH0] if ones else v[:, p, kt, g * DH0:(g + 1) * DH0]
                            last = nc.tensor.matmul(dst[head * DH0:(head + 1) * DH0, kt * P:L], w, pt[:, kt % 2, head, 0:n],
                                                    start=kt == 0, stop=kt == NT - 1)
                    last.then_inc(pv_tile, 1)

                def output(i, o):
                    b, h, p = batch(i, o)
                    pe.wait_ge(norm_done, b + 1)
                    if isinstance(b, int) and b >= NB - 2:
                        pe.wait_ge(kT_sb, NB)
                    else:
                        pe.wait_ge(xT_sb, b + 3)
                    for t in range(NT):
                        last = nc.tensor.matmul(ps_t[:, t * P:(t + 1) * P], attnT[:, t * P:(t + 1) * P], k.wo0[:], start=True, stop=True)
                    last.then_inc(wo_ps, 1)

                def body(i, o):
                    prev, nxt, nxt2, nxt3 = flags(i, o)
                    for u in range(3):
                        scores(i, o, u)
                    if prev:
                        output(i, o - 1)
                    values(i, o, 0)
                    scores(i, o, 3)
                    if nxt:
                        q_columns(i, o + 1)
                    scores(i, o, 4)
                    if nxt:
                        k_columns(i, o + 1)
                    values(i, o, 1)
                    if nxt:
                        ranks(i, o + 1)
                    scores(i, o, 5)
                    if nxt2:
                        x_rows(i, o + 2)
                    scores(i, o, 6)
                    if nxt2:
                        project(i, o + 2, 0)
                    values(i, o, 2)
                    scores(i, o, 7)
                    if nxt2:
                        project(i, o + 2, 1)
                        project(i, o + 2, 2)
                    values(i, o, 3)
                    if nxt2:
                        project(i, o + 2, 3)

                def rows(o):
                    x_rows(0, o)
                    for t in range(NT):
                        project(0, o, t)

                rows(0)
                ranks(0, 0)
                q_columns(0, 0)
                k_columns(0, 0)
                rows(1)
                bodies(pe, body)
                output(0, NB - 1)


class Kept:

    def __init__(self, nc, ctx):
        sb, _, sem = allocators(nc, ctx)
        self.scattered0, self.gathered1, self.scattered1, self.based = (
            [sem(f"{n}{p}") for p in range(2)] for n in ("scat0_", "gath1_", "scat1_", "based_"))
        self.put = [sem(f"put{q}") for q in range(NBUF)]
        self.spares_out = sem("spares_out")
        self.passed_dve, self.passed_pool, self.passed_sp = (sem(f"passed_{e}") for e in ("dve", "pool", "sp"))
        self.ident = sb("ident", [P, P])
        self.ident_b = sb("ident_b", [P, P], BF16)
        self.causal = sb("causal", [P, P], BF16)
        self.tri = sb("tri", [P, P], BF16)
        self.ones_b = sb("ones_b", [P, P], BF16)
        self.ones_f = sb("ones_f", [P, DH0])
        self.zeros = sb("zeros", [P, GRP // P * D])
        self.pads = sb("pads", [P, 2 * E1, GRP // P, D + 1])
        self.pad_ids = sb("pad_ids", [P, 2 * E1, GRP // P], mybir.dt.int32)
        self.token_i = sb("token_i", [P, NT], mybir.dt.int32)
        self.token = sb("token", [P, NT])
        self.mhalf = sb("mhalf", [P, 32])
        self.iota_i = sb("iota_i", [P, 128], mybir.dt.int32)
        self.iota = sb("iota", [P, 128])
        self.w0 = sb("w0", [P, PRJ0])
        self.w1 = sb("w1", [P, PRJ1])
        self.wo0 = sb("wo0", [P, D])
        self.wo1 = sb("wo1", [P, D])
        self.gate = sb("gate", [P, 1])
        self.temp = sb("temp", [P, 4])
        self.br0 = sb("br0", [P, E0])
        self.run0 = sb("run0", [P, E0])
        self.step = sb("step", [P, E0])
        self.run1 = sb("run1", [P, E1])
        self.table = sb("table", [P, max(NG0, NG1), 2], mybir.dt.int32)


def group_table(nc, k, run, n_exp, n_grp, xs_d, name, base_d=None):
    spare = n_exp * REG
    steps = T // GRP
    with ExitStack() as ctx:
        sb, ps, sem = allocators(nc, ctx)
        chain, fill_ready, zero_out = sem(name + "_chain"), sem(name + "_fill"), sem(name + "_zero")
        fill = sb(name + "_fill", [P, n_exp], U32)
        cnt = sb(name + "_cnt", [P, n_exp])
        lim = sb(name + "_lim", [P, steps])
        more = sb(name + "_more", [P, n_exp, steps])
        ng = sb(name + "_ng", [P, n_exp])
        upto = sb(name + "_upto", [P, n_exp])
        before = sb(name + "_before", [P, n_exp])
        row0 = sb(name + "_row0", [P, 2, n_exp])
        begun = sb(name + "_begun", [P, n_grp, n_exp])
        move = sb(name + "_move", [P, n_grp, n_exp])
        moved = sb(name + "_moved", [P, 3, n_grp])
        experts = sb(name + "_experts", [P, n_grp])
        live = sb(name + "_live", [P, n_grp])
        ahead = sb(name + "_ahead", [P, 3, n_grp])
        with nc.Block() as block:

            def zero_tails(eng, experts):
                eng.wait_ge(fill_ready, 1)
                for e in experts:
                    row = eng.value_load(fill[0:1, e:e + 1], min_val=0, max_val=n_exp * REG - GRP)
                    eng.dma_start(xs_d[bass.ds(row, GRP), :].rearrange("(p t) d -> p (t d)", p=P), k.zeros[:]).then_inc(zero_out, 16)
                    if base_d is not None:
                        eng.dma_start(base_d[bass.ds(row, GRP), :].rearrange("(p t) d -> p (t d)", p=P),
                                      k.pads[:, e].rearrange("p t d -> p (t d)")).then_inc(zero_out, 16)

            @block.sync
            def _(sp):
                zero_tails(sp, range(0, n_exp, 2))
                sp.wait_ge(zero_out, 16 * (n_exp + 1 if base_d is None else 2 * n_exp))
                if base_d is not None:
                    sp.wait_ge(k.spares_out, 16 * (E1 + 1))

            @block.scalar
            def _(act):
                if base_d is None:
                    act.dma_start(xs_d[spare:spare + GRP, :].rearrange("(p t) d -> p (t d)", p=P), k.zeros[:]).then_inc(zero_out, 16)
                zero_tails(act, range(1, n_exp, 2))

            @block.vector
            def _(dve):
                c = Chain(dve, chain, 0)
                c.at(0)
                nc.vector.tensor_copy(fill[:], run[:]).then_inc(fill_ready, 1)
                nc.vector.tensor_scalar(row0[:, 0], k.iota[:, 0:n_exp], float(REG), None, ALU.mult)
                c.link(nc.vector.tensor_scalar(lim[:], k.iota[:, 0:steps], float(GRP), None, ALU.mult))
                c.link(nc.vector.tensor_tensor(cnt[:], run[:], row0[:, 0], ALU.subtract))
                c.link(nc.vector.tensor_tensor(more[:], lim[:].unsqueeze(1).to_broadcast([P, n_exp, steps]),
                                               cnt[:].unsqueeze(2).to_broadcast([P, n_exp, steps]), ALU.is_lt))
                c.link(nc.vector.tensor_reduce(ng[:], more[:], AX, ALU.add))
                c.link(nc.vector.tensor_tensor_scan(upto[:], k.ones_f[:, 0:n_exp], ng[:], 0.0, ALU.mult, ALU.add))
                c.link(nc.vector.tensor_tensor(before[:], upto[:], ng[:], ALU.subtract))
                c.link(nc.vector.scalar_tensor_tensor(row0[:, 1], before[:], -float(GRP), row0[:, 0], ALU.mult, ALU.add))
                nc.vector.tensor_copy(k.step[:, 0:1], row0[:, 1, 0:1])
                nc.vector.tensor_tensor(k.step[:, 1:n_exp], row0[:, 1, 1:n_exp], row0[:, 1, 0:n_exp - 1], ALU.subtract)
                wide = [P, n_grp, n_exp]
                c.link(nc.vector.tensor_tensor(begun[:], k.iota[:, 0:n_grp].unsqueeze(2).to_broadcast(wide),
                                               before[:].unsqueeze(1).to_broadcast(wide), ALU.is_ge))
                nc.vector.tensor_tensor(move[:], begun[:], k.step[:, 0:n_exp].unsqueeze(1).to_broadcast(wide), ALU.mult)
                nc.vector.tensor_scalar(live[:], k.iota[:, 0:n_grp], upto[:, n_exp - 1:n_exp], None, ALU.is_lt)
                c.link(nc.vector.tensor_reduce(experts[:], begun[:], AX, ALU.add))
                c.link(nc.vector.tensor_reduce(moved[:, 0], move[:], AX, ALU.add))
                nc.vector.tensor_scalar(k.table[:, 0:n_grp, 1], experts[:], float(P), -float(P), ALU.mult, ALU.add)
                c.link(nc.vector.scalar_tensor_tensor(moved[:, 1], k.iota[:, 0:n_grp], float(GRP), moved[:, 0], ALU.mult, ALU.add))
                if base_d is None:
                    c.link(nc.vector.scalar_tensor_tensor(moved[:, 2], moved[:, 1], -float(spare), live[:], ALU.add, ALU.mult))
                    nc.vector.tensor_scalar(k.table[:, 0:n_grp, 0], moved[:, 2], float(spare), None, ALU.add)
                else:
                    nc.vector.tensor_scalar(ahead[:, 0], k.iota[:, 0:n_grp], upto[:, n_exp - 1:n_exp], None, ALU.subtract)
                    c.link(nc.vector.tensor_scalar(ahead[:, 2], moved[:, 1], -float(spare), None, ALU.add))
                    c.link(nc.vector.scalar_tensor_tensor(ahead[:, 1], ahead[:, 0], float(GRP), ahead[:, 2],
                                                          ALU.mult, ALU.subtract))
                    c.link(nc.vector.tensor_tensor(moved[:, 2], ahead[:, 1], live[:], ALU.mult))
                    c.link(nc.vector.scalar_tensor_tensor(ahead[:, 1], ahead[:, 0], float(GRP), moved[:, 2],
                                                          ALU.mult, ALU.subtract))
                    nc.vector.tensor_scalar(k.table[:, 0:n_grp, 0], ahead[:, 1], float(spare), None, ALU.add)


def expert_ffn(nc, k, layer, xs_d, ys_d, w_d, name, meta_d=None, base_d=None):
    gated = layer == 1
    n_exp, n_grp, chunks = (E1, NG1, FC1) if gated else (E0, NG0, F0 // P)
    wup = (2 if gated else 1) * chunks * P
    wcols = w_d.shape[1]
    GT = GRP // P
    n_slots = 2 * NT
    last_row = n_exp * REG + ((n_exp - 1) * GRP if gated else 0)
    with ExitStack() as ctx:
        sb, ps, sem = allocators(nc, ctx)
        x = sb(name + "_x", [P, NBUF, GT, D])
        w = sb(name + "_w", [P, NBUF, wcols])
        xT = sb(name + "_xT", [P, 2, GRP])
        g = sb(name + "_g", [P, 2, GRP])
        h = sb(name + "_h", [P, 2, chunks, GRP])
        y = sb(name + "_y", [P, NBUF, GT, D])
        ps_x = [ps(f"{name}_ps_x{n}", [P, 512]) for n in range(2)]
        ps_h = [ps(f"{name}_ps_h{n}", [P, 2, GRP]) for n in range(4)]
        ps_y = [ps(f"{name}_ps_y{n}", [P, 512]) for n in range(2)]
        if gated:
            base = sb(name + "_base", [P, NBUF, GT, D + 1])
            base_in = [sem(f"{name}_base_in{n}") for n in range(NBUF)]
        else:
            meta = sb(name + "_meta", [P, NB, 4 * NT], U32)
            slot = sb(name + "_slot", [P, NB, n_slots])
            down_by = sb(name + "_down_by", [P, 2, NB, n_slots])
            total = sb(name + "_total", [P, 2, NB, n_slots])
        meta_in, meta_new, meta_out, pool_chain = (sem(f"{name}_{n}") for n in ("meta_in", "meta_new", "meta_out", "pool_chain"))
        x_in = [sem(f"{name}_x_in{n}") for n in range(NBUF)]
        w_in = [sem(f"{name}_w_in{n}") for n in range(NBUF)]
        y_out = k.put if gated else [sem(f"{name}_y_out{n}") for n in range(NBUF)]
        y_dmas = 16 * GT if gated else 16
        xT_ps, xT_sb, h_ps, g_sb, h_sb, y_ps, y_sb = (sem(f"{name}_{n}") for n in ("xT_ps", "xT_sb", "h_ps", "g_sb", "h_sb", "y_ps", "y_sb"))
        with nc.Block() as block:

            @block.sync
            def _(sp):
                def load(j, i, q):
                    row = sp.value_load(k.table[0:1, bass.ds(j, 1), 0], min_val=0, max_val=last_row)
                    if not (isinstance(i, int) and i == 0):
                        sp.wait_ge(y_sb, j - NBUF + 1)
                    sp.dma_start(x[:, q], xs_d[bass.ds(row, GRP), :].rearrange("(t p) d -> p t d", p=P)).then_inc(x_in[q], 16)
                    if gated:
                        if not (isinstance(i, int) and i == 0):
                            sp.wait_ge(y_out[q], y_dmas * i)
                        sp.dma_start(base[:, q], base_d[bass.ds(row, GRP), :].rearrange("(t p) d -> p t d", p=P)).then_inc(base_in[q], 16)

                for q in range(NBUF):
                    load(q, 0, q)
                if not gated:
                    sp.dma_start(meta[:], meta_d.rearrange("(b p) c -> p b c", p=P)).then_inc(meta_in, 16)
                with sp.Fori(1, n_grp // NBUF) as i:
                    for q in range(NBUF):
                        load(NBUF * i + q, i, q)
                if not gated:
                    sp.wait_ge(meta_new, 1)
                    sp.dma_start(meta_d.rearrange("(b p) c -> p b c", p=P), meta[:]).then_inc(meta_out, 16)
                    sp.wait_ge(meta_out, 16)

            def pipeline(eng, rows_of, up, down):
                last = n_grp // NBUF - 1

                def turn(i, q, final=False):
                    j = NBUF * i + q
                    if not (final and q >= NBUF - 2):
                        rows_of(j + 2, i + (q + 2) // NBUF, (q + 2) % NBUF)
                    if not (final and q >= NBUF - 1):
                        up(j + 1, i + (q + 1) // NBUF, (q + 1) % NBUF)
                    down(j, i, q)

                rows_of(0, 0, 0)
                rows_of(1, 0, 1)
                up(0, 0, 0)
                for q in range(NBUF):
                    turn(0, q)
                with eng.Fori(1, last) as i:
                    for q in range(NBUF):
                        turn(i, q)
                for q in range(NBUF):
                    turn(last, q, True)

            def nothing(j, i, q):
                pass

            @block.gpsimd
            def _(pool):
                def put_rows(j, i, q):
                    pool.wait_ge(y_sb, j + 1)
                    passed(pool, k.passed_pool)
                    for t in range(GT):
                        nc.gpsimd.indirect_dma_start(
                            ys_d, bass.IndirectOffsetOnAxis(ap=base[:, q, t, D:D + 1].bitcast(U32), axis=0),
                            y[:, q, t, :], None).then_inc(y_out[q], 16)

                def move_slots():
                    c = Chain(pool, pool_chain, 0)
                    c.at(0)
                    pool.wait_ge(meta_in, 16)
                    nc.gpsimd.memset(total[:, 1], 0.0)
                    c.link(nc.gpsimd.tensor_copy(slot[:], meta[:, :, 0:n_slots]))
                    for e in range(n_exp):
                        c.link(nc.gpsimd.tensor_scalar(down_by[:, e % 2], slot[:], float(e * REG), k.step[:, e:e + 1],
                                                       ALU.is_ge, ALU.mult))
                        c.link(nc.gpsimd.tensor_tensor(total[:, e % 2], total[:, 1 - e % 2], down_by[:, e % 2], ALU.add))
                    c.link(nc.gpsimd.tensor_tensor(down_by[:, 0], slot[:], total[:, (n_exp - 1) % 2], ALU.subtract))
                    nc.gpsimd.tensor_copy(meta[:, :, 0:n_slots], down_by[:, 0]).then_inc(meta_new, 1)

                if gated:
                    pipeline(pool, nothing, nothing, put_rows)
                    for q in range(NBUF):
                        pool.wait_ge(y_out[q], y_dmas * (n_grp // NBUF))
                else:
                    move_slots()

            @block.tensor
            def _(pe):
                def rows_of(j, i, q):
                    pe.wait_ge(x_in[q], 16 * (i + 1))
                    if not isinstance(j, int) or j >= 2:
                        pe.wait_ge(xT_sb, j - 1)
                    for t in range(GT):
                        last = nc.tensor.transpose(ps_x[q % 2][:, t * P:(t + 1) * P], x[:, q, t, :], k.ident[:])
                    last.then_inc(xT_ps, 1)

                def up(j, i, q):
                    pe.wait_ge(w_in[q], 16 * (i + 1))
                    pe.wait_ge(xT_sb, j + 1)
                    for c in range(chunks):
                        u = (q * chunks + c) % 4
                        if not isinstance(j, int) or chunks * j + c >= 4:
                            pe.wait_ge(h_sb, chunks * j + c - 3)
                        for n in range(2 if gated else 1):
                            col = (n * chunks + c) * P
                            last = nc.tensor.matmul(ps_h[u][:, n, :], w[:, q, col:col + P], xT[:, q % 2, :], start=True, stop=True)
                        last.then_inc(h_ps, 1)

                def down(j, i, q):
                    pe.wait_ge(h_sb, chunks * (j + 1))
                    if not isinstance(j, int) or j >= 2:
                        pe.wait_ge(y_sb, j - 1)
                    for t in range(GT):
                        for c in range(chunks):
                            col = wup + c * D
                            last = nc.tensor.matmul(ps_y[q % 2][:, t * D:(t + 1) * D], h[:, q % 2, c, t * P:(t + 1) * P],
                                                    w[:, q, col:col + D], start=c == 0, stop=c == chunks - 1)
                    last.then_inc(y_ps, 1)

                pipeline(pe, rows_of, up, down)

            @block.scalar
            def _(act):
                def up(j, i, q):
                    if not isinstance(j, int) or j >= 2:
                        act.wait_ge(y_ps, j - 1)
                    for c in range(chunks):
                        u = (q * chunks + c) % 4
                        act.wait_ge(h_ps, chunks * j + c + 1)
                        if gated:
                            if not isinstance(j, int) or chunks * j + c >= 2:
                                act.wait_ge(h_sb, chunks * j + c - 1)
                            nc.scalar.activation(g[:, u % 2, :], ps_h[u][:, 0, :], ACT.Silu).then_inc(g_sb, 1)
                        else:
                            bias = w[:, q, wup + chunks * D + c:wup + chunks * D + c + 1]
                            act.wait_ge(w_in[q], 16 * (i + 1))
                            nc.scalar.activation(h[:, q % 2, c, :], ps_h[u][:, 0, :], ACT.Gelu, bias=bias).then_inc(h_sb, 1)

                def load_weights(j, q):
                    row = act.value_load(k.table[0:1, bass.ds(j, 1), 1], min_val=0, max_val=(n_exp - 1) * P)
                    act.dma_start(w[:, q], w_d[bass.ds(row, P), :]).then_inc(w_in[q], 16)

                def store(j, q, more):
                    act.wait_ge(y_sb, j + 1)
                    if not gated:
                        act.dma_start(ys_d[bass.ds(j * GRP, GRP), :].rearrange("(t p) d -> p t d", p=P), y[:, q]).then_inc(y_out[q], 16)
                    if more:
                        load_weights(j + NBUF, q)

                def down(j, i, q):
                    static = isinstance(i, int)
                    if static and i == 0 and q == 0:
                        return
                    store(j - 1, (q - 1) % NBUF, not (static and i == n_grp // NBUF - 1 and q > 0))

                for q in range(NBUF):
                    load_weights(q, q)
                pipeline(act, nothing, up, down)
                store(n_grp - 1, NBUF - 1, False)
                if not gated:
                    for q in range(NBUF):
                        act.wait_ge(y_out[q], y_dmas * (n_grp // NBUF))

            @block.vector
            def _(dve):
                def rows_of(j, i, q):
                    dve.wait_ge(xT_ps, j + 1)
                    if not isinstance(j, int) or j >= 2:
                        dve.wait_ge(h_ps, chunks * (j - 1))
                    nc.vector.tensor_copy(xT[:, q % 2, :], ps_x[q % 2][:, 0:GRP]).then_inc(xT_sb, 1)

                def up(j, i, q):
                    if not gated:
                        return
                    if not isinstance(j, int) or j >= 2:
                        dve.wait_ge(y_ps, j - 1)
                    for c in range(chunks):
                        u = (q * chunks + c) % 4
                        dve.wait_ge(g_sb, chunks * j + c + 1)
                        nc.vector.tensor_tensor(h[:, q % 2, c, :], ps_h[u][:, 1, :], g[:, u % 2, :], ALU.mult).then_inc(h_sb, 1)

                def down(j, i, q):
                    dve.wait_ge(y_ps, j + 1)
                    dve.wait_ge(y_out[q], y_dmas * i)
                    src = ps_y[q % 2][:, 0:GRP].rearrange("p (t d) -> p t d", t=GT)
                    if gated:
                        dve.wait_ge(base_in[q], 16 * (i + 1))
                        nc.vector.tensor_tensor(y[:, q], src, base[:, q, :, 0:D], ALU.add).then_inc(y_sb, 1)
                    else:
                        b2 = w[:, q, wcols - D:wcols].unsqueeze(1).to_broadcast([P, GT, D])
                        dve.wait_ge(w_in[q], 16 * (i + 1))
                        nc.vector.tensor_tensor(y[:, q], src, b2, ALU.add).then_inc(y_sb, 1)

                pipeline(dve, rows_of, up, down)


TERMS = 9
SROW = TERMS * DH1
KROWS = 96
QSCALE = float(D) ** -0.5


def layer1_attention(nc, k, ys_d, base_d, meta_d, rf_d, base2_d, xs2_d):
    HL = KV1
    with ExitStack() as ctx:
        sb, ps, sem = allocators(nc, ctx)
        xb = sb("c_xb", [P, 2, NT, D])
        mt = sb("c_mt", [P, 2, 4 * NT], U32)
        gy = sb("c_gy", [P, 2, 2 * NT, D])
        gsum = sb("c_gsum", [P, NT, D])
        x1 = sb("c_x1", [P, 2, NT, D])
        xr = sb("c_xr", [P, 2, NT, D])
        xn = sb("c_xn", [P, 2, NT, D])
        stats = sb("c_stats", [P, NT, 6])
        mv = sb("c_mv", [P, NT, 2])
        tmp4 = sb("c_tmp4", [P, 3, NT])
        rstd = sb("c_rstd", [P, NT])
        r2 = sb("c_r2", [P, 2, NT])
        xnT = sb("c_xnT", [P, L])
        prj = sb("c_prj", [P, NT, PRJ1])
        rf = sb("c_rf", [P, NT, DH1])
        qk = sb("c_qk", [P, NT, 2 * P])
        vp = sb("c_vp", [P, 2, NT, KV1, 32])
        q32 = sb("c_q32", [P, L])
        qr = sb("c_qr", [P, L])
        qp = sb("c_qp", [P, 3, L], BF16)
        k32 = sb("c_k32", [96, L])
        kr = sb("c_kr", [96, L])
        kh = sb("c_kh", [96, L], BF16)
        km = sb("c_km", [96, L], BF16)
        kl = sb("c_kl", [96, L], BF16)
        kb = sb("c_kb", [96, L], BF16)
        qst = sb("c_qst", [KROWS, 2, H1, L], BF16)
        kmx = sb("c_kmx", [KROWS, 2, KV1, L], BF16)
        kex = sb("c_kex", [KROWS, 2, KV1, L], BF16)
        ones2 = sb("c_ones2", [2, 2 * KV1 * L], BF16)
        mx = sb("c_mx", [P, 2, P])
        shb = sb("c_shb", [NT * HL, 2, 2, P], BF16)
        pt = sb("c_pt", [P, 2, HL, L])
        ov = sb("c_ov", [P, L])
        rcp = sb("c_rcp", [P, NT, HL])
        sall = sb("c_sall", [P, NT, D])
        sT = sb("c_sT", [P, L])
        sx = sb("c_sx", [P, NT, D])
        bs = sb("c_bs", [P, 2, NT, D + 1])
        mx8 = sb("c_mx8", [P, NT, 8])
        ix8 = sb("c_ix8", [P, NT, 8], U32)
        ixf = sb("c_ixf", [P, NT])
        oh = sb("c_oh", [P, NT, E1])
        ohb = sb("c_ohb", [P, NT, E1], BF16)
        pos = sb("c_pos", [P, NT, E1])
        ohp = sb("c_ohp", [P, NT, E1])
        slotf = sb("c_slotf", [P, NT])
        sl = sb("c_sl", [P, 2, NT], U32)

        ps_mx = [ps(f"c_ps_mx{n}", [P, L]) for n in range(2)]
        ps_e = ps("c_ps_e", [P, 2, 2, L])
        ps_v = ps("c_ps_v", [P, L])
        ps_j = ps("c_ps_j", [P, L])

        def sems(*names):
            return [sem("c_" + n) for n in names]

        gathered, scattered, based = k.gathered1, k.scattered1, k.based
        base_in, meta_in, k_in, q_in, sh_in = (
            [sem(f"c_{n}{p}") for p in range(2)]
            for n in ("base_in", "meta_in", "k_in", "q_in", "sh_in"))
        (comb_done, stats_ready, rstd_ready, xn_ready, xr_ready, xT_ps, xT_sb, proj_ps, prj_sb, qk_ready, v_ready,
         kT_ps, kT_sb, kr_ready, km_ready, kl_ready, kb_ready, qT_ps, qT_sb, qr_ready, qm_ready, ql_ready) = sems(
            "comb", "stats_r", "rstd_r", "xn_r", "xr_r", "xT_ps", "xT_sb", "proj", "prj_sb", "qk_r", "v_r",
            "kT_ps", "kT_sb", "kr_r", "km_r", "kl_r", "kb_r", "qT_ps", "qT_sb", "qr_r", "qm_r", "ql_r")
        (mx_ps, mx_done, mt_ps, sh_ready, s_ps, exp_done, pv, ov_sb, ot_ps, ot_sb, sT_ps, sT_sb, wo_ps, wo_sb,
         sx_ready, oh_ready, rank_ps, rank_used, slot_ready, const_in) = sems(
            "mx_ps", "mx_done", "mt_ps", "sh_r", "s_ps", "exp", "pv", "ov_sb", "ot_ps", "ot_sb", "sT_ps", "sT_sb",
            "wo_ps", "wo_sb", "sx_r", "oh_r", "rank_ps", "rank_u", "slot_r", "const")
        dve_pro, dve_ln, dve_sh, dve_ot, pool_ln, made, vp_made, next_tokens = sems(
            "dve_pro", "dve_ln", "dve_sh", "dve_ot", "pool_ln", "made", "vp_made", "next_tokens")

        with nc.Block() as block:

            @block.sync
            def _(sp):
                def load(i, o):
                    b, h, p = batch(i, o)
                    if not (isinstance(b, int) and b < 2):
                        sp.wait_ge(comb_done, b - 1)
                        passed(sp, k.passed_sp)
                    sp.dma_start(xb[:, p], base_d[bass.ds(b * L, L), :].rearrange("(t p) d -> p t d", p=P)).then_inc(base_in[p], 16)
                    sp.dma_start(mt[:, p], meta_d[bass.ds(b * P, P), :]).then_inc(meta_in[p], 16)

                def k_stack(i, o):
                    b, h, p = batch(i, o)
                    sp.wait_ge(kl_ready, b + 1)
                    passed(sp, k.passed_sp)
                    sp.wait_ge(kb_ready, b + 1)
                    passed(sp, k.passed_sp)
                    if not (isinstance(b, int) and b < 2):
                        sp.wait_ge(s_ps, 32 * (b - 1))
                        passed(sp, k.passed_sp)
                        sp.wait_ge(mx_ps, 64 * (b - 1))
                        passed(sp, k.passed_sp)
                    for dst in (kmx, kex):
                        for a in range(3):
                            sp.dma_start(dst[3 * DH1 * a:3 * DH1 * (a + 1), p], kb[:]).then_inc(k_in[p], 16)

                def q_stack(i, o):
                    b, h, p = batch(i, o)
                    sp.wait_ge(ql_ready, b + 1)
                    passed(sp, k.passed_sp)
                    for t in range(TERMS):
                        sp.dma_start(qst[DH1 * t:DH1 * (t + 1), p], qp[:, t // 3, :]).then_inc(q_in[p], 16)

                def shift(i, o, g):
                    b, h, p = batch(i, o)
                    sp.wait_ge(sh_ready, 4 * b + g + 1)
                    passed(sp, k.passed_sp)
                    for n in range(2):
                        sp.dma_start(qst[SROW + n:SROW + n + 1, p, HL * g:HL * (g + 1), :],
                                     shb[:, g % 2, n, :]).then_inc(sh_in[g % 2], 16)

                def body(i, o):
                    prev, nxt, nxt2, nxt3 = flags(i, o)
                    shift(i, o, 1)
                    if nxt:
                        k_stack(i, o + 1)
                        q_stack(i, o + 1)
                    if nxt3:
                        load(i, o + 3)
                    shift(i, o, 2)
                    shift(i, o, 3)
                    if nxt:
                        shift(i, o + 1, 0)

                load(0, 0)
                load(0, 1)
                sp.dma_start(rf[:], rf_d.rearrange("(t p) d -> p t d", p=P)).then_inc(const_in, 16)
                sp.wait_ge(made, 3)
                sp.dma_start(kex[SROW:SROW + 2], ones2[:]).then_inc(const_in, 16)
                load(0, 2)
                k_stack(0, 0)
                q_stack(0, 0)
                shift(0, 0, 0)
                bodies(sp, body)

            @block.gpsimd
            def _(pool):
                def gather(i, o):
                    b, h, p = batch(i, o)
                    pool.wait_ge(meta_in[p], 16 * (h + 1))
                    if not (isinstance(b, int) and b < 2):
                        pool.wait_ge(comb_done, b - 1)
                    passed(pool, k.passed_pool)
                    for n in range(2 * NT):
                        nc.gpsimd.indirect_dma_start(
                            gy[:, p, n, :], None, ys_d,
                            bass.IndirectOffsetOnAxis(ap=mt[:, p, n:n + 1], axis=0)).then_inc(gathered[p], 16)

                def combine(ln, i, o):
                    b, h, p = batch(i, o)
                    ln.at(b)
                    pool.wait_ge(gathered[p], 16 * 2 * NT * (h + 1))
                    pool.wait_ge(base_in[p], 16 * (h + 1))
                    w = mt[:, p, 2 * NT:4 * NT].bitcast(F32).unsqueeze(2).to_broadcast([P, 2 * NT, D])
                    ln.link(nc.gpsimd.tensor_tensor(gy[:, p], gy[:, p], w, ALU.mult))
                    ln.link(nc.gpsimd.tensor_tensor(gsum[:], gy[:, p, 0:NT, :], gy[:, p, NT:2 * NT, :], ALU.add))
                    if not (isinstance(b, int) and b < 2):
                        pool.wait_ge(xr_ready, b - 1)
                    nc.gpsimd.tensor_tensor(x1[:, p], gsum[:], xb[:, p], ALU.add).then_inc(comb_done, 1)

                def norms(ln, i, o):
                    b, h, p = batch(i, o)
                    pool.wait_ge(stats_ready, b + 1)
                    pool.wait_ge(xn_ready, b)
                    if not (isinstance(b, int) and b < 2):
                        pool.wait_ge(prj_sb, NT * (b - 1))
                    passed(pool, k.passed_pool)
                    ln.link(nc.gpsimd.tensor_scalar(tmp4[:, 0], mv[:, :, 1], EPS_LN, None, ALU.add))
                    ln.link(nc.gpsimd.tensor_tensor(rstd[:], tmp4[:, 0], k.mhalf[:, 0:NT], ALU.pow))
                    ln.link(nc.gpsimd.tensor_tensor(tmp4[:, 1], rstd[:], rstd[:], ALU.mult))
                    ln.link_apart(nc.gpsimd.tensor_tensor(tmp4[:, 2], tmp4[:, 1], mv[:, :, 1], ALU.mult))
                    ln.link(nc.gpsimd.tensor_scalar(tmp4[:, 0], tmp4[:, 2], float(np.finfo(np.float32).eps), None, ALU.add))
                    ln.link(nc.gpsimd.tensor_tensor(r2[:, p], tmp4[:, 0], k.mhalf[:, 0:NT], ALU.pow))
                    nc.gpsimd.tensor_tensor(tmp4[:, 1], r2[:, p], r2[:, p], ALU.mult).then_inc(rstd_ready, 1)

                    ln.end()

                def rotate(i, o):
                    b, h, p = batch(i, o)
                    pool.wait_ge(prj_sb, NT * (b + 1))
                    pool.wait_ge(qT_ps, b)
                    qd = prj[:, :, 0:D].rearrange("p t (d h) -> p t d h", d=DH1)
                    nc.gpsimd.tensor_tensor(qk[:, :, 0:D].rearrange("p t (d h) -> p t d h", d=DH1), qd,
                                            rf[:].unsqueeze(3).to_broadcast([P, NT, DH1, H1]), ALU.mult)
                    kd = prj[:, :, D:D + 32].rearrange("p t (d h) -> p t d h", d=DH1)
                    for r in range(3):
                        last = nc.gpsimd.tensor_tensor(
                            qk[:, :, D + 32 * r:D + 32 * (r + 1)].rearrange("p t (d h) -> p t d h", d=DH1), kd,
                            rf[:].unsqueeze(3).to_broadcast([P, NT, DH1, KV1]), ALU.mult)
                    last.then_inc(qk_ready, 1)

                def v_rows(i, o):
                    b, h, p = batch(i, o)
                    pool.wait_ge(prj_sb, NT * (b + 1))
                    pool.wait_ge(pv, 16 * (b - 1) + 2 if not (isinstance(b, int) and b < 1) else 2)
                    passed(pool, k.passed_pool)
                    nc.gpsimd.tensor_copy(vp[:, p, :, :, 0:DH1],
                                          prj[:, :, D + 32:QKV1].rearrange("p t (h d) -> p t h d", h=KV1)).then_inc(v_ready, 1)

                def parts(i, o):
                    b, h, p = batch(i, o)
                    pool.wait_ge(kT_sb, b + 1)
                    pool.wait_ge(km_ready, b)
                    nc.gpsimd.tensor_tensor(kr[:], k32[:], kh[:], ALU.subtract).then_inc(kr_ready, 1)
                    pool.wait_ge(qT_sb, b + 1)
                    pool.wait_ge(qm_ready, b)
                    nc.gpsimd.tensor_tensor(qr[:], q32[:], qp[:, 0, :], ALU.subtract).then_inc(qr_ready, 1)
                    pool.wait_ge(km_ready, b + 1)
                    pool.wait_ge(kb_ready, b)
                    nc.gpsimd.tensor_tensor(kl[:], kr[:], km[:], ALU.subtract).then_inc(kl_ready, 1)
                    pool.wait_ge(qm_ready, b + 1)
                    nc.gpsimd.tensor_tensor(qp[:, 2, :], qr[:], qp[:, 1, :], ALU.subtract).then_inc(ql_ready, 1)

                def residual(i, o):
                    b, h, p = batch(i, o)
                    pool.wait_ge(ot_sb, 4 * (b + 1))
                    pool.wait_ge(xr_ready, b + 1)
                    pool.wait_ge(wo_sb, b)
                    nc.gpsimd.tensor_tensor(sx[:], sall[:], xr[:, p], ALU.add).then_inc(sx_ready, 1)

                def scatter(i, o):
                    b, h, p = batch(i, o)
                    pool.wait_ge(slot_ready, b + 1)
                    passed(pool, k.passed_pool)
                    for t in range(NT):
                        nc.gpsimd.indirect_dma_start(
                            xs2_d, bass.IndirectOffsetOnAxis(ap=sl[:, p, t:t + 1], axis=0),
                            xn[:, p, t, :], None).then_inc(scattered[p], 16)

                def scatter_base(i, o):
                    b, h, p = batch(i, o)
                    pool.wait_ge(wo_sb, b + 1)
                    passed(pool, k.passed_pool)
                    for t in range(NT):
                        nc.gpsimd.indirect_dma_start(
                            base2_d, bass.IndirectOffsetOnAxis(ap=sl[:, p, t:t + 1], axis=0),
                            bs[:, p, t, :], None).then_inc(based[p], 16)

                ln = Chain(pool, pool_ln, NORM_LINKS1, k.passed_pool)

                def body(i, o):
                    prev, nxt, nxt2, nxt3 = flags(i, o)
                    if nxt:
                        parts(i, o + 1)
                        v_rows(i, o + 1)
                    if prev:
                        residual(i, o - 1)
                    if nxt2:
                        combine(ln, i, o + 2)
                    if prev:
                        scatter_base(i, o - 1)
                    if nxt2:
                        norms(ln, i, o + 2)
                    if nxt:
                        scatter(i, o + 1)
                    if nxt3:
                        gather(i, o + 3)
                    if nxt2:
                        rotate(i, o + 2)

                gather(0, 0)
                nc.gpsimd.memset(kex[:], 0.0).then_inc(made, 1)
                nc.gpsimd.memset(qk[:], 0.0).then_inc(pv, 2)
                nc.gpsimd.memset(vp[:], 0.0).then_inc(vp_made, 1)
                combine(ln, 0, 0)
                norms(ln, 0, 0)
                pool.wait_ge(vp_made, 1)
                nc.gpsimd.memset(vp[:, :, :, :, DH1:DH1 + 1], 1.0).then_inc(vp_made, 1)
                pool.wait_ge(const_in, 32)
                pool.wait_ge(vp_made, 2)
                rotate(0, 0)
                parts(0, 0)
                v_rows(0, 0)
                gather(0, 1)
                combine(ln, 0, 1)
                norms(ln, 0, 1)
                scatter(0, 0)
                gather(0, 2)
                rotate(0, 1)
                bodies(pool, body)
                residual(0, NB - 1)
                scatter_base(0, NB - 1)
                for p in range(2):
                    pool.wait_ge(scattered[p], 16 * NT * (NB // 2))
                    pool.wait_ge(based[p], 16 * NT * (NB // 2))

            @block.scalar
            def _(act):
                def exps(i, o, s, half):
                    b, h, p = batch(i, o)
                    gs = 16 * b + s
                    act.wait_ge(s_ps, 2 * gs + half + 1)
                    if half == 0:
                        act.wait_ge(pv, gs + 1)
                    nc.scalar.activation(pt[:, s % 2, 2 * half:2 * half + 2, :], ps_e[:, half], ACT.Exp,
                                         scale=QSCALE).then_inc(exp_done, 1)

                def ov_copy(i, o, g):
                    b, h, p = batch(i, o)
                    act.wait_ge(pv, 4 * (4 * b + g + 1) + 2)
                    act.wait_ge(ot_ps, 4 * b + g)
                    nc.scalar.activation(ov[:], ps_v[:], ACT.Copy).then_inc(ov_sb, 1)

                def xT_copy(i, o):
                    b, h, p = batch(i, o)
                    act.wait_ge(xT_ps, b + 1)
                    act.wait_ge(proj_ps, 2 * b)
                    nc.scalar.activation(xnT[:], ps_j[:], ACT.Copy).then_inc(xT_sb, 1)

                def prj_copy(i, o, pair):
                    b, h, p = batch(i, o)
                    act.wait_ge(proj_ps, 2 * b + pair + 1)
                    if pair == 0:
                        act.wait_ge(rstd_ready, b + 1)
                        act.wait_ge(v_ready, b)
                        act.wait_ge(oh_ready, b)
                    for t in (2 * pair, 2 * pair + 1):
                        nc.scalar.activation(prj[:, t, :], ps_j[:, t % 2 * PRJ1:(t % 2 + 1) * PRJ1], ACT.Copy,
                                             scale=r2[:, p, t:t + 1]).then_inc(prj_sb, 1)

                def kT_copy(i, o):
                    b, h, p = batch(i, o)
                    act.wait_ge(kT_ps, b + 1)
                    act.wait_ge(kb_ready, b)
                    act.wait_ge(kr_ready, b)
                    nc.scalar.activation(kh[:], ps_j[0:96, :], ACT.Copy)
                    nc.scalar.activation(k32[:], ps_j[0:96, :], ACT.Copy).then_inc(kT_sb, 1)

                def qT_copy(i, o):
                    b, h, p = batch(i, o)
                    _, hq, pq = batch(i, o + 1)
                    act.wait_ge(qT_ps, b + 1)
                    act.wait_ge(qr_ready, b)
                    if not (isinstance(b, int) and b < 1):
                        act.wait_ge(q_in[pq], 16 * TERMS * hq)
                    nc.scalar.activation(qp[:, 0, :], ps_j[:], ACT.Copy)
                    nc.scalar.activation(q32[:], ps_j[:], ACT.Copy).then_inc(qT_sb, 1)

                def sT_copy(i, o):
                    b, h, p = batch(i, o)
                    act.wait_ge(sT_ps, b + 1)
                    act.wait_ge(wo_ps, b)
                    nc.scalar.activation(sT[:], ps_j[:], ACT.Copy).then_inc(sT_sb, 1)

                def body(i, o):
                    prev, nxt, nxt2, nxt3 = flags(i, o)
                    for s in range(16):
                        exps(i, o, s, 0)
                        if s == 11 and nxt2:
                            xT_copy(i, o + 2)
                        if s == 12 and nxt2:
                            prj_copy(i, o + 2, 1)
                        if s == 15 and nxt2:
                            kT_copy(i, o + 2)
                        if s == 3 and prev:
                            sT_copy(i, o - 1)
                        if s == 0 and prev:
                            ov_copy(i, o - 1, 3)
                        if s > 0 and s % 4 == 0:
                            ov_copy(i, o, s // 4 - 1)
                        exps(i, o, s, 1)
                        if s == 11 and nxt2:
                            prj_copy(i, o + 2, 0)
                        if s == 15 and nxt2:
                            qT_copy(i, o + 2)

                for o in range(2):
                    xT_copy(0, o)
                    prj_copy(0, o, 0)
                    prj_copy(0, o, 1)
                    kT_copy(0, o)
                    qT_copy(0, o)
                bodies(act, body)
                ov_copy(0, NB - 1, 3)
                sT_copy(0, NB - 1)

            @block.vector
            def _(dve):
                def row_max(i, o, n):
                    b, h, p = batch(i, o)
                    g = n // 16
                    if n % 16 == 0 and not (isinstance(b, int) and 4 * b + g < 2):
                        dve.wait_ge(mt_ps, 4 * b + g - 1)
                    dve.wait_ge(mx_ps, 64 * b + n + 1)
                    nc.vector.tensor_reduce(mx[:, g % 2, n % 16:n % 16 + 1], ps_mx[n % 2][:], AX, ALU.max).then_inc(mx_done, 1)

                def shifts(i, o, g):
                    b, h, p = batch(i, o)
                    dve.wait_ge(mt_ps, 4 * b + g + 1)
                    if not (isinstance(b, int) and 4 * b + g < 2):
                        dve.wait_ge(sh_in[g % 2], 32 * (2 * b + g // 2))
                    src = ps_j[0:NT * HL, 0:P]
                    nc.vector.tensor_scalar(shb[:, g % 2, 0, :], src, -1.0, None, ALU.mult).then_inc(dve_sh, 1)
                    dve.wait_ge(dve_sh, 4 * b + g + 1)
                    nc.vector.scalar_tensor_tensor(shb[:, g % 2, 1, :], src, -1.0, shb[:, g % 2, 0, :],
                                                   ALU.mult, ALU.subtract).then_inc(sh_ready, 1)

                def normalise(i, o, g):
                    b, h, p = batch(i, o)
                    dve.wait_ge(ot_ps, 4 * b + g + 1)
                    src = ps_j[:].rearrange("p (t h c) -> p t h c", t=NT, h=HL)
                    if g == 0:
                        dve.wait_ge(sx_ready, b)
                        dve.wait_ge(sT_ps, b)
                    nc.vector.reciprocal(rcp[:], src[:, :, :, DH1]).then_inc(dve_ot, 1)
                    dve.wait_ge(dve_ot, 4 * b + g + 1)
                    nc.vector.tensor_tensor(sall[:, :, 32 * g:32 * (g + 1)].rearrange("p t (h d) -> p t h d", h=HL),
                                            src[:, :, :, 0:DH1], rcp[:].unsqueeze(3).to_broadcast([P, NT, HL, DH1]),
                                            ALU.mult).then_inc(ot_sb, 1)

                def output(i, o):
                    b, h, p = batch(i, o)
                    dve.wait_ge(wo_ps, b + 1)
                    dve.wait_ge(sx_ready, b + 1)
                    dve.wait_ge(based[p], 16 * NT * h)
                    dve.wait_ge(next_tokens, b)
                    nc.vector.tensor_copy(bs[:, p, :, D].bitcast(U32), k.token[:])
                    nc.vector.tensor_scalar(k.token[:], k.token[:], float(L), None, ALU.add).then_inc(next_tokens, 1)
                    nc.vector.tensor_tensor(bs[:, p, :, 0:D], ps_j[:].rearrange("p (t d) -> p t d", t=NT), sx[:],
                                            ALU.add).then_inc(wo_sb, 1)

                def keep_x1(i, o):
                    b, h, p = batch(i, o)
                    if not (isinstance(b, int) and b < 2):
                        dve.wait_ge(sx_ready, b - 1)
                    dve.wait_ge(comb_done, b + 1)
                    nc.vector.tensor_copy(xr[:, p], x1[:, p]).then_inc(xr_ready, 1)

                def k_mid(i, o):
                    b, h, p = batch(i, o)
                    dve.wait_ge(kr_ready, b + 1)
                    dve.wait_ge(kl_ready, b)
                    nc.vector.tensor_copy(km[:], kr[:]).then_inc(km_ready, 1)

                def k_join(i, o):
                    b, h, p = batch(i, o)
                    _, hq, pq = batch(i, o + 1)
                    if not (isinstance(b, int) and b < 1):
                        dve.wait_ge(k_in[pq], 16 * 6 * hq)
                    dve.wait_ge(km_ready, b + 1)
                    dve.wait_ge(kT_sb, b + 1)
                    dve.wait_ge(kl_ready, b + 1)
                    for n, part in enumerate((kh, km, kl)):
                        rows = slice(32 * n, 32 * (n + 1))
                        last = nc.vector.tensor_copy(kb[rows], part[rows])
                    last.then_inc(kb_ready, 1)

                def q_mid(i, o):
                    b, h, p = batch(i, o)
                    dve.wait_ge(qr_ready, b + 1)
                    nc.vector.tensor_copy(qp[:, 1, :], qr[:]).then_inc(qm_ready, 1)

                pro = Chain(dve, dve_pro, ROUTE_LINKS1, k.passed_dve)

                def choose(i, o):
                    b, h, p = batch(i, o)
                    pro.at(b)
                    dve.wait_ge(prj_sb, NT * (b + 1))
                    passed(dve, k.passed_dve)
                    lg = prj[:, :, QKV1:PRJ1]
                    for t in range(NT):
                        last = nc.vector.max(mx8[:, t, :], lg[:, t, :])
                    pro.link_apart(last)
                    for t in range(NT):
                        last = nc.vector.max_index(ix8[:, t, :], mx8[:, t, :], lg[:, t, :])
                    pro.link(last)
                    pro.link(nc.vector.tensor_copy(ixf[:], ix8[:, :, 0]))
                    pro.link(nc.vector.tensor_tensor(oh[:], k.iota[:, 0:E1].unsqueeze(1).to_broadcast([P, NT, E1]),
                                                     ixf[:].unsqueeze(2).to_broadcast([P, NT, E1]), ALU.is_equal))
                    dve.wait_ge(rank_ps, b)
                    nc.vector.tensor_copy(ohb[:], oh[:]).then_inc(oh_ready, 1)

                def slots(i, o):
                    b, h, p = batch(i, o)
                    dve.wait_ge(rank_ps, b + 1)
                    for t in range(NT):
                        nc.vector.tensor_tensor(pos[:, t], ps_j[:, t * E1:(t + 1) * E1], k.run1[:], ALU.add)
                        last = nc.vector.tensor_tensor(k.run1[:], ps_j[:, (NT + t) * E1:(NT + t + 1) * E1], k.run1[:], ALU.add)
                        if t < NT - 1:
                            pro.link(last)
                    last.then_inc(rank_used, 1)
                    dve.wait_ge(rank_used, b + 1)
                    pro.link(nc.vector.tensor_tensor(ohp[:], oh[:], pos[:], ALU.mult))
                    pro.link(nc.vector.tensor_reduce(slotf[:], ohp[:], AX, ALU.add))
                    dve.wait_ge(scattered[p], 16 * NT * h)
                    dve.wait_ge(based[p], 16 * NT * h)
                    nc.vector.tensor_copy(sl[:, p], slotf[:]).then_inc(slot_ready, 1)
                    pro.end()

                ln = Chain(dve, dve_ln, 1, k.passed_dve)

                def statistics(i, o):
                    b, h, p = batch(i, o)
                    ln.at(b)
                    dve.wait_ge(comb_done, b + 1)
                    dve.wait_ge(rstd_ready, b)
                    for t in range(NT):
                        last = nc.vector.bn_stats(stats[:, t, :], x1[:, p, t, :])
                    ln.link_apart(last)
                    for t in range(NT):
                        last = nc.vector.bn_aggr(mv[:, t, :], stats[:, t, :])
                    last.then_inc(stats_ready, 1)
                    ln.end()

                def normal_rows(i, o):
                    b, h, p = batch(i, o)
                    dve.wait_ge(rstd_ready, b + 1)
                    dve.wait_ge(scattered[p], 16 * NT * h)
                    for t in range(NT):
                        last = nc.vector.tensor_scalar(xn[:, p, t, :], x1[:, p, t, :], mv[:, t, 0:1], rstd[:, t:t + 1],
                                                       ALU.subtract, ALU.mult)
                    last.then_inc(xn_ready, 1)

                def maxima(i, o, s, first):
                    m = s + 7
                    if m >= 16 and not flags(i, o)[1]:
                        return
                    for j in (0, 1) if first else (2, 3):
                        row_max(i, o + m // 16, 4 * (m % 16) + j)

                def body(i, o):
                    prev, nxt, nxt2, nxt3 = flags(i, o)
                    for s in range(16):
                        maxima(i, o, s, True)
                        if s in (1, 5, 9):
                            shifts(i, o, s // 4 + 1)
                        if s == 3 and nxt:
                            choose(i, o + 1)
                        if s == 4 and prev:
                            output(i, o - 1)
                        if s == 8 and nxt:
                            keep_x1(i, o + 1)
                        if s == 6 and nxt2:
                            statistics(i, o + 2)
                        if s == 13 and nxt:
                            shifts(i, o + 1, 0)
                        maxima(i, o, s, False)
                        if s == 0 and nxt:
                            k_mid(i, o + 1)
                            q_mid(i, o + 1)
                        if s == 1 and prev:
                            normalise(i, o - 1, 3)
                        if s == 2 and nxt:
                            k_join(i, o + 1)
                        if s == 6 and nxt:
                            slots(i, o + 1)
                        if s in (5, 9, 13):
                            normalise(i, o, s // 4 - 1)
                        if s == 9 and nxt2:
                            normal_rows(i, o + 2)

                nc.vector.memset(qst[:], 0.0).then_inc(made, 1)
                nc.vector.memset(kmx[:], 0.0).then_inc(exp_done, 2)
                nc.vector.memset(ones2[:], 1.0).then_inc(made, 1)
                nc.vector.memset(mx[:], 0.0).then_inc(mx_done, 2)
                dve.wait_ge(mx_done, 2)
                statistics(0, 0)
                normal_rows(0, 0)
                choose(0, 0)
                k_mid(0, 0)
                q_mid(0, 0)
                k_join(0, 0)
                keep_x1(0, 0)
                slots(0, 0)
                statistics(0, 1)
                for m in range(7):
                    for j in range(4):
                        row_max(0, 0, 4 * m + j)
                    if m == 1:
                        normal_rows(0, 1)
                    if m == 3:
                        shifts(0, 0, 0)
                bodies(dve, body)
                normalise(0, NB - 1, 3)
                output(0, NB - 1)

            @block.tensor
            def _(pe):
                def scores(i, o, s, half):
                    b, h, p = batch(i, o)
                    g, kt = s // 4, s % 4
                    if kt == 0 and half == 0:
                        pe.wait_ge(sh_in[g % 2], 32 * (2 * b + g // 2 + 1))
                    pe.wait_ge(exp_done, 2 * (16 * b + s) + half + 1)
                    for j in range(2):
                        hl = 2 * half + j
                        last = nc.tensor.matmul(ps_e[:, half, j, :], kex[:, p, hl, kt * P:(kt + 1) * P],
                                                qst[:, p, HL * g + hl, :], start=True, stop=True)
                    last.then_inc(s_ps, 1)

                def values(i, o, s):
                    b, h, p = batch(i, o)
                    gs = 16 * b + s
                    kt = s % 4
                    pe.wait_ge(exp_done, 2 * gs + 4)
                    if kt == 0:
                        pe.wait_ge(ov_sb, 4 * b + s // 4)
                    if s == 0:
                        pe.wait_ge(v_ready, b + 1)
                    for hl in range(HL):
                        last = nc.tensor.matmul(ps_v[32 * hl:32 * (hl + 1), :], vp[:, p, kt, hl, :], pt[:, s % 2, hl, :],
                                                start=kt == 0, stop=kt == NT - 1)
                    last.then_inc(pv, 1)

                def score_max(i, o, n):
                    b, h, p = batch(i, o)
                    g, hl, qt = n // 16, n // 4 % 4, n % 4
                    if n == 0:
                        if isinstance(b, int) and b == 0:
                            pe.wait_ge(exp_done, 2)
                            pe.wait_ge(const_in, 32)
                        pe.wait_ge(k_in[p], 16 * 6 * (h + 1))
                        pe.wait_ge(q_in[p], 16 * TERMS * (h + 1))
                    pe.wait_ge(mx_done, 64 * b + n + 1)
                    nc.tensor.matmul(ps_mx[n % 2][:], qst[:, p, HL * g + hl, qt * P:(qt + 1) * P], kmx[:, p, hl, :],
                                     start=True, stop=True).then_inc(mx_ps, 1)

                def maximum(i, o, s, j):
                    m = s + 7
                    if m < 16 or flags(i, o)[1]:
                        score_max(i, o + m // 16, 4 * (m % 16) + j)

                def transposes(src, done):
                    for t in range(NT):
                        last = nc.tensor.transpose(ps_j[:, t * P:(t + 1) * P], src(t), k.ident[:])
                    last.then_inc(done, 1)

                def x_rows(free, i, o):
                    b, h, p = batch(i, o)
                    pe.wait_ge(*free)
                    pe.wait_ge(xn_ready, b + 1)
                    transposes(lambda t: xn[:, p, t, :], xT_ps)
                    return xT_sb, b + 1

                def project(free, i, o, pair):
                    b, h, p = batch(i, o)
                    pe.wait_ge(*free)
                    pe.wait_ge(xT_sb, b + 1)
                    for t in (2 * pair, 2 * pair + 1):
                        last = nc.tensor.matmul(ps_j[:, t % 2 * PRJ1:(t % 2 + 1) * PRJ1], xnT[:, t * P:(t + 1) * P], k.w1[:],
                                                start=True, stop=True)
                    last.then_inc(proj_ps, 1)
                    return prj_sb, NT * b + 2 * (pair + 1)

                def k_columns(free, i, o):
                    b, h, p = batch(i, o)
                    pe.wait_ge(*free)
                    pe.wait_ge(qk_ready, b + 1)
                    transposes(lambda t: qk[:, t, P:2 * P], kT_ps)
                    return kT_sb, b + 1

                def q_columns(free, i, o):
                    b, h, p = batch(i, o)
                    pe.wait_ge(*free)
                    pe.wait_ge(qk_ready, b + 1)
                    transposes(lambda t: qk[:, t, 0:P], qT_ps)
                    return qT_sb, b + 1

                def ranks(free, i, o):
                    b, h, p = batch(i, o)
                    pe.wait_ge(*free)
                    pe.wait_ge(oh_ready, b + 1)
                    flat = ohb[:].rearrange("p t e -> p (t e)")
                    nc.tensor.matmul(ps_j[:, 0:NT * E1], k.tri[:], flat, start=True, stop=True)
                    nc.tensor.matmul(ps_j[:, NT * E1:2 * NT * E1], k.ones_b[:], flat, start=True, stop=True).then_inc(rank_ps, 1)
                    return rank_used, b + 1

                def max_columns(free, i, o, g):
                    b, h, p = batch(i, o)
                    pe.wait_ge(*free)
                    pe.wait_ge(mx_done, 16 * (4 * b + g + 1) + 2)
                    nc.tensor.transpose(ps_j[:, 0:P], mx[:, g % 2, :], k.ident[:]).then_inc(mt_ps, 1)
                    return sh_ready, 4 * b + g + 1

                def token_rows(free, i, o, g):
                    b, h, p = batch(i, o)
                    pe.wait_ge(*free)
                    pe.wait_ge(ov_sb, 4 * b + g + 1)
                    transposes(lambda t: ov[:, t * P:(t + 1) * P], ot_ps)
                    return ot_sb, 4 * b + g + 1

                def s_rows(free, i, o):
                    b, h, p = batch(i, o)
                    pe.wait_ge(*free)
                    pe.wait_ge(ot_sb, 4 * (b + 1))
                    transposes(lambda t: sall[:, t, :], sT_ps)
                    return sT_sb, b + 1

                def s_project(free, i, o):
                    b, h, p = batch(i, o)
                    pe.wait_ge(*free)
                    pe.wait_ge(sT_sb, b + 1)
                    for t in range(NT):
                        last = nc.tensor.matmul(ps_j[:, t * P:(t + 1) * P], sT[:, t * P:(t + 1) * P], k.wo1[:],
                                                start=True, stop=True)
                    last.then_inc(wo_ps, 1)
                    return wo_sb, b + 1

                def body(i, o):
                    prev, nxt, nxt2, nxt3 = flags(i, o)
                    b = batch(i, o)[0]
                    free = (qT_sb, b + 2) if nxt else (ot_sb, 4 * b - 1)
                    for s in range(16):
                        maximum(i, o, s, 0)
                        scores(i, o, s, 0)
                        maximum(i, o, s, 1)
                        if s in (1, 5, 9):
                            free = max_columns(free, i, o, s // 4 + 1)
                        if s == 3 and prev:
                            free = s_rows(free, i, o - 1)
                        if s == 6 and nxt:
                            free = ranks(free, i, o + 1)
                        if s == 11 and nxt2:
                            free = x_rows(free, i, o + 2)
                        if s == 12 and nxt2:
                            free = project(free, i, o + 2, 1)
                        if s == 13 and nxt:
                            free = max_columns(free, i, o + 1, 0)
                        if s == 15 and nxt2:
                            free = k_columns(free, i, o + 2)
                        if s > 0:
                            values(i, o, s - 1)
                        elif prev:
                            values(i, o - 1, 15)
                        maximum(i, o, s, 2)
                        scores(i, o, s, 1)
                        maximum(i, o, s, 3)
                        if s == 1 and prev:
                            free = token_rows(free, i, o - 1, 3)
                        if s == 3 and prev:
                            free = s_project(free, i, o - 1)
                        if s in (5, 9, 13):
                            free = token_rows(free, i, o, s // 4 - 1)
                        if s == 11 and nxt2:
                            free = project(free, i, o + 2, 0)
                        if s == 15 and nxt2:
                            free = q_columns(free, i, o + 2)

                free = x_rows((xn_ready, 1), 0, 0)
                free = project(free, 0, 0, 0)
                free = project(free, 0, 0, 1)
                free = k_columns(free, 0, 0)
                free = q_columns(free, 0, 0)
                free = ranks(free, 0, 0)
                for m in range(7):
                    for j in range(4):
                        score_max(0, 0, 4 * m + j)
                    if m == 2:
                        free = x_rows(free, 0, 1)
                    if m == 3:
                        free = max_columns(free, 0, 0, 0)
                    if m == 4:
                        free = project(free, 0, 1, 0)
                    if m == 5:
                        free = project(free, 0, 1, 1)
                free = k_columns(free, 0, 1)
                q_columns(free, 0, 1)
                bodies(pe, body)
                values(0, NB - 1, 15)
                free = token_rows((ot_sb, 4 * NB - 1), 0, NB - 1, 3)
                free = s_rows(free, 0, NB - 1)
                s_project(free, 0, NB - 1)


def build(nc, i, out):
    def dram(name, shape, dt=F32):
        return nc.dram_tensor(name, shape, dt, kind="Internal").ap()

    base = dram("base", [T, D])
    meta = dram("meta", [NB * P, 4 * NT], U32)
    xs = dram("xs", [E0 * REG + GRP, D])
    ys = dram("ys", [NG0 * GRP, D])
    base2 = dram("base2", [E1 * (REG + GRP), D + 1])
    xs2 = dram("xs2", [E1 * (REG + GRP), D])
    with ExitStack() as ctx:
        k = Kept(nc, ctx)
        setup(nc, k, i, xs2, base2)
        layer0_attention(nc, k, i["x"], base, meta, xs)
        group_table(nc, k, k.run0, E0, NG0, xs, "gt0")
        expert_ffn(nc, k, 0, xs, ys, i["we0"], "f0", meta_d=meta)
        layer1_attention(nc, k, ys, base, meta, i["rf"], base2, xs2)
        group_table(nc, k, k.run1, E1, NG1, xs2, "gt1", base2)
        expert_ffn(nc, k, 1, xs2, out, i["we1"], "f1", base_d=base2)


def rotary_factors():
    d = np.arange(DH1)
    theta = np.power(np.float32(10000.0), (-2.0 * (d // 2) / DH1).astype(np.float32)).astype(np.float32)
    ang = (np.arange(L, dtype=np.float32)[:, None] * theta[None, :]).astype(np.float32)
    sign = np.where(np.arange(L) % 2 == 1, -1.0, 1.0).astype(np.float32)
    return (np.cos(ang) + sign[:, None] * np.sin(ang)).astype(np.float32)


def laid_out(a):
    def heads_last(w, heads):
        return w.reshape(D, heads, DH1).transpose(0, 2, 1).reshape(D, heads * DH1)

    def chunked(w):
        out = np.zeros((E1, D, FC1 * P), w.dtype)
        out[:, :, :F1] = w.transpose(0, 2, 1)
        return out

    down = np.zeros((E1, FC1 * P, D), a["L1_ffn_down_w"].dtype)
    down[:, :F1] = a["L1_ffn_down_w"].transpose(0, 2, 1)
    arrays = {
        "x": a["L0_attn_x"].reshape(T, D),
        "w0cat": np.concatenate([a["L0_attn_Wq"], a["L0_attn_Wk"], a["L0_attn_Wv"], a["L0_ffn_Wr"]], 1),
        "w1cat": np.concatenate([heads_last(a["L1_attn_w_q"], H1), heads_last(a["L1_attn_w_k"], KV1), a["L1_attn_w_v"],
                                 a["L1_ffn_router_w"].T], 1),
        "L0_attn_Wo": a["L0_attn_Wo"],
        "L1_attn_w_o": a["L1_attn_w_o"],
        "norms": np.stack([a["L0_attn_norm_w"], a["L1_attn_g"]], 1),
        "gate": np.broadcast_to(a["L0_attn_gate"], (P, 1)),
        "logt": np.broadcast_to(a["L0_attn_log_temperature"], (P, 4)),
        "br0": np.broadcast_to(a["L0_ffn_br"], (P, E0)),
        "we0": np.concatenate([
            a["L0_ffn_W1"], a["L0_ffn_W2"].reshape(E0, F0 // P, P, D).transpose(0, 2, 1, 3).reshape(E0, P, F0 // P * D),
            a["L0_ffn_b1"].reshape(E0, F0 // P, P).transpose(0, 2, 1),
            np.broadcast_to(a["L0_ffn_b2"][:, None, :], (E0, P, D))], 2).reshape(E0 * P, -1),
        "we1": np.concatenate([
            chunked(a["L1_ffn_gate_w"]), chunked(a["L1_ffn_up_w"]),
            down.reshape(E1, FC1, P, D).transpose(0, 2, 1, 3).reshape(E1, P, FC1 * D)], 2).reshape(E1 * P, -1),
        "rf": rotary_factors(),
    }
    return {n: np.ascontiguousarray(v) for n, v in arrays.items()}


def kernel(**inputs):
    import concourse.bacc as bacc
    from concourse.bass_utils import run_bass_kernel_spmd

    nc = bacc.Bacc("TRN2", target_bir_lowering=False, num_devices=1)
    arrays = {f"in_{n}": v for n, v in laid_out({n: np.asarray(v) for n, v in inputs.items()}).items()}
    aps = {n[3:]: nc.dram_tensor(n, v.shape, mybir.dt.from_np(v.dtype), kind="ExternalInput").ap() for n, v in arrays.items()}
    out = nc.dram_tensor("out", (T + PAD, D), F32, kind="ExternalOutput").ap()
    build(nc, aps, out)
    r = run_bass_kernel_spmd(nc, [arrays], core_ids=[0])
    return r.results[0]["out"][:T].reshape(NB, L, D)
```
